# Optimizing a Trainium2 kernel written in Bass

```python
import numpy as np
import jax
import jax.numpy as jnp

def _softmax(x, axis=-1):
    return jax.nn.softmax(x, axis=axis)

def _gelu(x):
    return jax.nn.gelu(x, approximate=True)

def _silu(x):
    return jax.nn.silu(x)

def _sigmoid(x):
    return jax.nn.sigmoid(x)

def _layernorm(x, axis=-1, eps=1e-05):
    m = jnp.mean(x, axis=axis, keepdims=True)
    v = jnp.var(x, axis=axis, keepdims=True)
    return (x - m) / jnp.sqrt(v + eps)

def _scatter_add(tgt, idx, src, axis=0):
    return tgt.at[idx].add(src)

def _segment_sum(src, seg, n):
    return jax.ops.segment_sum(src, seg, n)
kernel_name = 'mk_adaln_attn_ffn_d1_seqx_r4_7770c5'

def setup_inputs(seed: int=0):
    np.random.seed(seed)
    _w = jnp.asarray

    def _rec_inputs():
        import jax
        import jax.numpy as jnp
        _rk = jax.random.key(seed)
        x = -0.000125 + 0.9999 * jax.random.normal(jax.random.fold_in(_rk, 1), (2, 1024, 256), jnp.float32)
        _lenS = 1024 - jax.random.randint(jax.random.fold_in(_rk, 7), (2,), 0, max(1, 1024 // 4) + 1, jnp.int32)
        _lenS2 = 1024 - jax.random.randint(jax.random.fold_in(_rk, 8), (2,), 0, max(1, 1024 // 4) + 1, jnp.int32)
        fside_Bx2_0 = -2.90419 + 8.51931 * jax.random.normal(jax.random.fold_in(_rk, 11), (2, 2), jnp.float32)
        condB_angle = 0.0111926 + 0.196324 * jax.random.normal(jax.random.fold_in(_rk, 12), (2,), jnp.float32)
        condB_zX = jax.random.uniform(jax.random.fold_in(_rk, 13), (2,), jnp.float32, 0.0, 0.983423)
        condB_zY = jax.random.uniform(jax.random.fold_in(_rk, 14), (2,), jnp.float32, 0.0, 0.979075)
        condB_zR = jax.random.uniform(jax.random.fold_in(_rk, 15), (2,), jnp.float32, 0.0, 0.9968)
        return (x, fside_Bx2_0, condB_angle, condB_zX, condB_zY, condB_zR)
    x, fside_Bx2_0, condB_angle, condB_zX, condB_zY, condB_zR = _rec_inputs()

    def _L0_cond_setup():
        import jax, jax.numpy as jnp
        import numpy as np
        B, H, W = (32, 256, 256)
        SCALE_DX = 1.0
        SCALE_ANGLE = 1.0

        def _rigid_transform(X, dx, angle):
            b, h, w = X.shape
            gx = jnp.arange(w, dtype=jnp.float32)[None, :] - w / 2.0
            gy = jnp.arange(h, dtype=jnp.float32)[:, None] - h / 2.0
            theta = angle * SCALE_ANGLE
            c = jnp.cos(theta)[:, None, None]
            s = jnp.sin(theta)[:, None, None]
            xp = c * gx - s * gy + dx[:, 0, None, None] * SCALE_DX
            yp = s * gx + c * gy + dx[:, 1, None, None] * SCALE_DX
            gx_n = yp / h * 2.0
            gy_n = xp / w * 2.0
            ix = (gx_n + 1.0) * 0.5 * (w - 1)
            iy = (gy_n + 1.0) * 0.5 * (h - 1)
            ix0 = jnp.floor(ix)
            iy0 = jnp.floor(iy)
            wx1 = ix - ix0
            wy1 = iy - iy0
            wx0 = 1.0 - wx1
            wy0 = 1.0 - wy1
            ix0i = ix0.astype(jnp.int32)
            iy0i = iy0.astype(jnp.int32)
            ix1i = ix0i + 1
            iy1i = iy0i + 1
            bidx = jnp.arange(b, dtype=jnp.int32)[:, None, None]

            def gather(yi, xi):
                valid = (xi >= 0) & (xi <= w - 1) & (yi >= 0) & (yi <= h - 1)
                xc = jnp.clip(xi, 0, w - 1)
                yc = jnp.clip(yi, 0, h - 1)
                return X[bidx, yc, xc] * valid.astype(X.dtype)
            out = gather(iy0i, ix0i) * (wy0 * wx0) + gather(iy0i, ix1i) * (wy0 * wx1) + gather(iy1i, ix0i) * (wy1 * wx0) + gather(iy1i, ix1i) * (wy1 * wx1)
            return out
        key = jax.random.key(seed)
        k1, k2, k3 = jax.random.split(key, 3)
        X = jax.random.normal(k1, (B, H, W), dtype=jnp.float32)
        dx = jax.random.normal(k2, (B, 2), dtype=jnp.float32) * 8.0
        angle = jax.random.normal(k3, (B,), dtype=jnp.float32) * 0.2
        return {'X': X, 'dx': dx, 'angle': angle}
    _L0_cond_all = _L0_cond_setup()
    _L0_cond_in = {k: v for k, v in _L0_cond_all.items() if k in ()}
    del _L0_cond_all

    def _L0_attn_setup():
        import jax, jax.numpy as jnp
        import numpy as np
        B, S, D, H = (4, 512, 256, 16)
        DH = D // H
        key = jax.random.key(seed)
        ks = jax.random.split(key, 9)
        sc = 0.02
        return {'x': jax.random.normal(ks[0], (B, S, D), jnp.float32), 'WQ': jax.random.normal(ks[1], (D, D), jnp.float32) * sc, 'bQ': jax.random.normal(ks[2], (D,), jnp.float32) * sc, 'WK': jax.random.normal(ks[3], (D, D), jnp.float32) * sc, 'bK': jax.random.normal(ks[4], (D,), jnp.float32) * sc, 'WV': jax.random.normal(ks[5], (D, D), jnp.float32) * sc, 'bV': jax.random.normal(ks[6], (D,), jnp.float32) * sc, 'WO': jax.random.normal(ks[7], (DH, D), jnp.float32) * sc, 'bO': jax.random.normal(ks[8], (D,), jnp.float32) * sc}
    _L0_attn_all = _L0_attn_setup()
    _L0_attn_in = {k: v for k, v in _L0_attn_all.items() if k in ('WQ', 'bQ', 'WK', 'bK', 'WV', 'bV', 'WO', 'bO')}
    del _L0_attn_all

    def _L0_cond2_setup():
        import jax, jax.numpy as jnp
        import numpy as np
        key = jax.random.key(seed)
        k1, k2, k3, k4 = jax.random.split(key, 4)
        B, H, W = (64, 256, 256)
        return {'y': jax.random.uniform(k1, (B, H, W), dtype=jnp.float32), 'zX': jax.random.uniform(k2, (B, 1), dtype=jnp.float32), 'zY': jax.random.uniform(k3, (B, 1), dtype=jnp.float32), 'zR': jax.random.uniform(k4, (B, 1), dtype=jnp.float32), 'dx': 1, 'dy': 1}
    _L0_cond2_all = _L0_cond2_setup()
    _L0_cond2_in = {k: v for k, v in _L0_cond2_all.items() if k in ()}
    del _L0_cond2_all

    def _L0_ffn_setup():
        import jax, jax.numpy as jnp
        import numpy as np
        N_EMBD = 256
        NUM_EXPERTS = 8
        TOP_K = 2
        D_FF = 4 * N_EMBD
        B, S = (4, 512)
        key = jax.random.key(seed)
        ks = jax.random.split(key, 7)
        scale = lambda fan_in: 1.0 / np.sqrt(fan_in)
        x = jax.random.normal(ks[0], (B, S, N_EMBD), dtype=jnp.float32)
        W_router = jax.random.normal(ks[1], (N_EMBD, NUM_EXPERTS), dtype=jnp.float32) * scale(N_EMBD)
        b_router = jnp.zeros((NUM_EXPERTS,), dtype=jnp.float32)
        W1 = jax.random.normal(ks[2], (NUM_EXPERTS, N_EMBD, D_FF), dtype=jnp.float32) * scale(N_EMBD)
        b1 = jnp.zeros((NUM_EXPERTS, D_FF), dtype=jnp.float32)
        W2 = jax.random.normal(ks[3], (NUM_EXPERTS, D_FF, N_EMBD), dtype=jnp.float32) * scale(D_FF)
        b2 = jnpp = jnp.zeros((NUM_EXPERTS, N_EMBD), dtype=jnp.float32)
        return {'x': x, 'W_router': W_router, 'b_router': b_router, 'W1': W1, 'b1': b1, 'W2': W2, 'b2': b2}
    _L0_ffn_all = _L0_ffn_setup()
    _L0_ffn_in = {k: v for k, v in _L0_ffn_all.items() if k in ('W_router', 'b_router', 'W1', 'b1', 'W2', 'b2')}
    del _L0_ffn_all
    return {'x': x, 'fside_Bx2_0': fside_Bx2_0, 'condB_angle': condB_angle, 'condB_zX': condB_zX, 'condB_zY': condB_zY, 'condB_zR': condB_zR, 'L0_attn_WQ': _L0_attn_in['WQ'], 'L0_attn_bQ': _L0_attn_in['bQ'], 'L0_attn_WK': _L0_attn_in['WK'], 'L0_attn_bK': _L0_attn_in['bK'], 'L0_attn_WV': _L0_attn_in['WV'], 'L0_attn_bV': _L0_attn_in['bV'], 'L0_attn_WO': _L0_attn_in['WO'], 'L0_attn_bO': _L0_attn_in['bO'], 'L0_ffn_W_router': _L0_ffn_in['W_router'], 'L0_ffn_b_router': _L0_ffn_in['b_router'], 'L0_ffn_W1': _L0_ffn_in['W1'], 'L0_ffn_b1': _L0_ffn_in['b1'], 'L0_ffn_W2': _L0_ffn_in['W2'], 'L0_ffn_b2': _L0_ffn_in['b2']}

def reference(x, fside_Bx2_0, condB_angle, condB_zX, condB_zY, condB_zR, L0_attn_WQ, L0_attn_bQ, L0_attn_WK, L0_attn_bK, L0_attn_WV, L0_attn_bV, L0_attn_WO, L0_attn_bO, L0_ffn_W_router, L0_ffn_b_router, L0_ffn_W1, L0_ffn_b1, L0_ffn_W2, L0_ffn_b2):
    import jax
    import jax.numpy as jnp

    def _L0_cond_ref(X, dx, angle):
        import jax, jax.numpy as jnp
        import numpy as np
        B, H, W = (32, 256, 256)
        SCALE_DX = 1.0
        SCALE_ANGLE = 1.0

        def _rigid_transform(X, dx, angle):
            b, h, w = X.shape
            gx = jnp.arange(w, dtype=jnp.float32)[None, :] - w / 2.0
            gy = jnp.arange(h, dtype=jnp.float32)[:, None] - h / 2.0
            theta = angle * SCALE_ANGLE
            c = jnp.cos(theta)[:, None, None]
            s = jnp.sin(theta)[:, None, None]
            xp = c * gx - s * gy + dx[:, 0, None, None] * SCALE_DX
            yp = s * gx + c * gy + dx[:, 1, None, None] * SCALE_DX
            gx_n = yp / h * 2.0
            gy_n = xp / w * 2.0
            ix = (gx_n + 1.0) * 0.5 * (w - 1)
            iy = (gy_n + 1.0) * 0.5 * (h - 1)
            ix0 = jnp.floor(ix)
            iy0 = jnp.floor(iy)
            wx1 = ix - ix0
            wy1 = iy - iy0
            wx0 = 1.0 - wx1
            wy0 = 1.0 - wy1
            ix0i = ix0.astype(jnp.int32)
            iy0i = iy0.astype(jnp.int32)
            ix1i = ix0i + 1
            iy1i = iy0i + 1
            bidx = jnp.arange(b, dtype=jnp.int32)[:, None, None]

            def gather(yi, xi):
                valid = (xi >= 0) & (xi <= w - 1) & (yi >= 0) & (yi <= h - 1)
                xc = jnp.clip(xi, 0, w - 1)
                yc = jnp.clip(yi, 0, h - 1)
                return X[bidx, yc, xc] * valid.astype(X.dtype)
            out = gather(iy0i, ix0i) * (wy0 * wx0) + gather(iy0i, ix1i) * (wy0 * wx1) + gather(iy1i, ix0i) * (wy1 * wx0) + gather(iy1i, ix1i) * (wy1 * wx1)
            return out
        return _rigid_transform(X, dx, angle)

    def _L0_attn_ref(x, WQ, bQ, WK, bK, WV, bV, WO, bO):
        import jax, jax.numpy as jnp
        import numpy as np
        B, S, D, H = (4, 512, 256, 16)
        DH = D // H
        b, s, d = x.shape
        h, dh = (H, DH)
        Q = (x @ WQ + bQ).reshape(b, s, h, dh).transpose(0, 2, 1, 3)
        K = (x @ WK + bK).reshape(b, s, h, dh).transpose(0, 2, 1, 3)
        V = (x @ WV + bV).reshape(b, s, h, dh).transpose(0, 2, 1, 3)
        scale = jnp.sqrt(jnp.float32(dh))
        scores = jnp.einsum('bhqd,bhkd->bhqk', Q, K) / scale
        causal = jnp.tril(jnp.ones((s, s), dtype=bool))
        scores = jnp.where(causal, scores, jnp.float32(-100000.0))
        A = jax.nn.softmax(scores, axis=-1)
        Z = jnp.einsum('bhqk,bhkd->bhqd', A, V)
        out = jnp.einsum('bhsd,de->bse', Z, WO) + jnp.float32(h) * bO
        return out

    def _L0_cond2_ref(y, zX, zY, zR, dx, dy):
        import jax, jax.numpy as jnp
        import numpy as np
        yp_x = jnp.pad(y, ((0, 0), (0, 0), (1, 1)), mode='reflect')
        lap_x = (yp_x[:, :, :-2] - 2.0 * y + yp_x[:, :, 2:]) / (dx * dx)
        yp_y = jnp.pad(y, ((0, 0), (1, 1), (0, 0)), mode='reflect')
        lap_y = (yp_y[:, :-2, :] - 2.0 * y + yp_y[:, 2:, :]) / (dy * dy)
        du_dt = zX[:, :, None] * lap_x + zY[:, :, None] * lap_y + zR[:, :, None] * y * (1.0 - y)
        return du_dt

    def _L0_ffn_ref(x, W_router, b_router, W1, b1, W2, b2):
        import jax, jax.numpy as jnp
        import numpy as np
        N_EMBD = 256
        NUM_EXPERTS = 8
        TOP_K = 2
        D_FF = 4 * N_EMBD
        B, S = (4, 512)
        Bv, Sv, D = x.shape
        flat_x = x.reshape(-1, D)
        T = flat_x.shape[0]
        logits = flat_x @ W_router + b_router
        top_vals, top_idx = jax.lax.top_k(logits, TOP_K)
        neg_inf = jnp.full_like(logits, -jnp.inf)
        sparse_logits = neg_inf.at[jnp.arange(T)[:, None], top_idx].set(top_vals)
        router_weights = jax.nn.softmax(sparse_logits, axis=-1)
        final_output = jnp.zeros_like(flat_x)
        for e in range(NUM_EXPERTS):
            expert_mask = jnp.any(top_idx == e, axis=-1)
            h = jax.nn.relu(flat_x @ W1[e] + b1[e])
            y = h @ W2[e] + b2[e]
            w = router_weights[:, e] * expert_mask.astype(x.dtype)
            final_output = final_output + y * w[:, None]
        return final_output.reshape(Bv, Sv, D)
    x = x + _L0_attn_ref(_L0_cond_ref(x, fside_Bx2_0, condB_angle), L0_attn_WQ, L0_attn_bQ, L0_attn_WK, L0_attn_bK, L0_attn_WV, L0_attn_bV, L0_attn_WO, L0_attn_bO)
    x = x + _L0_ffn_ref(_L0_cond2_ref(x, condB_zX[:, None], condB_zY[:, None], condB_zR[:, None], 1, 1), L0_ffn_W_router, L0_ffn_b_router, L0_ffn_W1, L0_ffn_b1, L0_ffn_W2, L0_ffn_b2)
    return x

_drawn_inputs = setup_inputs


def setup_inputs(seed=0):
    import zlib

    import numpy as np

    out = dict(_drawn_inputs(seed))
    spreads = {'L0_ffn_b_router': (0.0, 0.1), 'L0_ffn_b1': (0.0, 0.1), 'L0_ffn_b2': (0.0, 0.1)}
    factors = {'L0_attn_WQ': 8.0, 'L0_attn_bQ': 33.236, 'L0_attn_WK': 5.208, 'L0_attn_bK': 64.0}
    for name, (base, spread) in spreads.items():
        noise = np.random.default_rng([zlib.crc32(name.encode()), seed]).standard_normal(out[name].shape)
        drawn = base * np.exp(spread * noise) if base else spread * noise
        out[name] = jnp.asarray(drawn.astype(out[name].dtype))
    for name, factor in factors.items():
        out[name] = (out[name] * factor).astype(out[name].dtype)
    return out
```

```python
from contextlib import ExitStack

import concourse.bass as bass
import numpy as np
from concourse import mybir

ALU = mybir.AluOpType
ACT = mybir.ActivationFunctionType
AX_X = mybir.AxisListType.X
F32 = mybir.dt.float32
BF16 = mybir.dt.bfloat16
I32 = mybir.dt.int32
U32 = mybir.dt.uint32

P = 128
NB, S, D = 2, 1024, 256
H, DH = 16, 16
E, FF = 8, 1024
SB = S // P
NBLK = NB * SB
DC = D // P
FC = FF // P

SHEAR = 192
J = D + 2 * SHEAR
JB = J // P
R = 8
R_LOW = 3
X_LOW = 36
XW = 336
MSHIFT = 32
PAD_Y = R
PAD_X = X_LOW + MSHIFT
PADW = 400
PADH = S + 2 * PAD_Y
BAND = (R - 1) * PADW + XW
XBLOCKS = [(0, P), (P, P), (2 * P, XW - 2 * P)]
KX = (D - 1) / S
KY = (S - 1) / D
NTAP = 9

SLOT_TILES = 2 * NB * S // P + E - 1
NSLOT = SLOT_TILES * P

HG = 4
NG = H // HG
PRODUCTS = [(0, 0), (0, 1), (0, 2), (1, 0), (1, 1), (2, 0)]
KROWS = DH * len(PRODUCTS)
SIDE_FIRST, SIDE_GROUP, SIDE_OUT = 49, 51, 2
SIDE_BATCH = SIDE_FIRST + SIDE_GROUP * (NG - 1) + SIDE_OUT
N_WEIGHTS = 3 + 2 + 1 + 2 * HG + 1 + 6
PROJ_BATCH = 8 + SB
ARENA = 37632

NEG = -1.0e30

CONST_PARTS = [("sheared", JB), ("row", SB), ("identity", P), ("mask_qk", P), ("mask_kq", P), ("before", P),
               ("lap_mid", P), ("lap_first", P), ("lap_last", P), ("lap_prev", P), ("lap_next", P),
               ("head_sum", P), ("experts", E), ("tiles", SLOT_TILES), ("column", D), ("ones", P)]
CONST_AT, CONST_W = {}, 0
for _name, _width in CONST_PARTS:
    CONST_AT[_name] = (CONST_W, _width)
    CONST_W += _width


def constants():
    p = np.arange(P)
    eye = np.eye(P)
    second = np.eye(P, k=1) + np.eye(P, k=-1) - 2 * eye
    first, last = second.copy(), second.copy()
    first[1, 0] = 2
    last[P - 2, P - 1] = 2
    prev, nxt = np.zeros((P, P)), np.zeros((P, P))
    prev[P - 1, 0] = nxt[0, P - 1] = 1
    sums = np.zeros((P, P))
    sums[(p // 32) * 32 + DH, p] = 1
    part = {
        "sheared": p[:, None] + P * np.arange(JB)[None, :] - D // 2 - SHEAR,
        "row": p[:, None] + P * np.arange(SB)[None, :] - S // 2,
        "identity": eye,
        "mask_qk": np.where(p[None, :] > p[:, None], NEG, 0),
        "mask_kq": np.where(p[None, :] < p[:, None], NEG, 0),
        "before": p[:, None] < p[None, :],
        "lap_mid": second, "lap_first": first, "lap_last": last, "lap_prev": prev, "lap_next": nxt,
        "head_sum": sums,
        "experts": np.broadcast_to(np.arange(E), (P, E)),
        "tiles": np.broadcast_to(np.arange(SLOT_TILES), (P, SLOT_TILES)),
        "column": np.broadcast_to(np.arange(D) - D // 2, (P, D)),
        "ones": np.ones((P, P)),
    }
    return np.concatenate([np.asarray(part[n], np.float32) for n, _ in CONST_PARTS], axis=1)


class Steps:

    def __init__(self, eng, sem, base=0, hold=None):
        self.eng, self.sem, self.base, self.n = eng, sem, base, 0
        self.hold = hold or eng.wait_ge

    def mark(self, ins):
        ins.then_inc(self.sem, 1)
        self.n += 1

    def wait(self):
        self.hold(self.sem, self.base + self.n)

    def do(self, ins):
        self.mark(ins)
        self.wait()


def build(nc, x, shift, angle, zx, zy, zr, wq, bq, wk, bk, wv, bv, wo, bo, wr, br, w1, b1, w2, b2, consts, out):
    ctx = ExitStack()
    with ctx:
        def sb(name, shape, dt=F32):
            return ctx.enter_context(nc.sbuf_tensor(name, shape, dt))

        def sem(name):
            return ctx.enter_context(nc.semaphore(name))

        def dram(name, shape, dt=F32):
            return nc.dram_tensor(name, shape, dt, kind="Internal").ap()

        padded = dram("padded", [NB * PADH * PADW])
        table = [dram(f"table{b}", [XW * R * J]) for b in range(NB)]
        fracs = dram("fracs", [NB * J * 2])
        qk_parts = [dram(f"qk_parts{b}", [2, 3, D, S], BF16) for b in range(NB)]
        pairs_x = dram("pairs_x", [NSLOT, D])
        pairs_y = dram("pairs_y", [NSLOT, D])
        padded_v = padded.rearrange("(b y x) -> b y x", b=NB, y=PADH)
        table_v = [t.rearrange("(x r j) -> x r j", x=XW, r=R) for t in table]

        cst = sb("cst", [P, CONST_W])

        def const(name):
            at, width = CONST_AT[name]
            return cst[:, at:at + width]

        ident = const("identity")
        zeros = sb("zeros", [P, SB * (PADW - D - PAD_X)])
        ang = sb("ang", [P, NB])
        shf = sb("shf", [P, NB, 2])
        prm = sb("prm", [P, 40, NB])
        col_f = sb("col_f", [P, NB, JB, 2])
        band_index = sb("band_index", [P, NB * JB], I32)
        tap_index = sb("tap_index", [P, NBLK], I32)
        frac_index = sb("frac_index", [P, NBLK], I32)
        row_bias = sb("row_bias", [P, NBLK, 4])
        row_par = sb("row_par", [P, NBLK, 4])
        steep = sb("steep", [P, NBLK], I32)
        tmp = sb("tmp", [P, 12, 16])
        tmp_i = sb("tmp_i", [P, 16], I32)
        band_col = sb("band_col", [P, 2], I32)
        tap_col = sb("tap_col", [P, 2], I32)
        frac_col = sb("frac_col", [P, 2], I32)
        xwT = sb("xwT", [P, DC, NB * S])
        x1 = sb("x1", [P, NBLK, D])
        wqkv = sb("wqkv", [P, 3, DC, D])
        bqk = sb("bqk", [P, 2, DC])
        bv_rows = sb("bv_rows", [P, D])
        wo_stack = sb("wo_stack", [P, D])
        ident_b = sb("ident_b", [P, P], BF16)
        mask_qk = sb("mask_qk", [P, P], BF16)
        mask_kq = sb("mask_kq", [P, P], BF16)
        z_cols = sb("z_cols", [P, 4, NB])
        wr_cols = sb("wr_cols", [P, DC, E])
        br_row = sb("br_row", [P, E])
        b1_rows = sb("b1_rows", [E * FC, P])
        b1_cols_t = sb("b1_cols", [P, E * FC])
        b1_cols = b1_cols_t[:].rearrange("p (e f) -> p e f", e=E)
        route = sb("route", [P, 8, NBLK])
        rt = sb("rt", [P, 6, NBLK, E])
        chosen = rt[:, 4].rearrange("p i e -> p (i e)")
        ex = sb("ex", [P, 5, E])
        ex_i = sb("ex_i", [P, E], I32)
        slot_index = sb("slot_index", [P, 2, NBLK], I32)
        te_f = sb("te_f", [P, SLOT_TILES, E])
        te_s = sb("te_s", [P, SLOT_TILES])
        tile_expert = sb("tile_expert", [P, SLOT_TILES], I32)
        du_t = [sb(f"du_t{u}", [P, DC, P])[:] for u in range(2)]
        arena = sb("arena", [P, ARENA])

        def region():
            at = [0]

            def tile(shape, dt=F32):
                n = int(np.prod(shape))
                words = n if dt != BF16 else (n + 1) // 2
                flat = arena[:, at[0]:at[0] + words]
                at[0] += words
                assert at[0] <= ARENA, at[0]
                if dt != F32:
                    flat = flat.bitcast(dt)
                names = [f"a{i}" for i in range(len(shape))]
                if len(shape) == 1:
                    return flat
                return flat.rearrange(f"p ({' '.join(names)}) -> p {' '.join(names)}",
                                      **{n_: k for n_, k in zip(names, shape)})
            return tile

        tile = region()
        band = [tile([BAND]) for u in range(2)]
        strip = [tile([3, R, P]) for u in range(2)]
        taps = [tile([3, 3, D]) for u in range(2)]
        frac = [tile([D, 2]) for u in range(2)]
        hats = [tile([2, 4, D]) for u in range(2)]
        warped = [tile([D]) for u in range(2)]
        slow = tile([5, D])
        slow_taps = tile([3, 3, D])
        slow_frac = tile([D, 2])
        slow_i = tile([D], I32)
        slow_par = tile([8])
        slow_col = tile([1], I32)
        slow_run = tile([PADW + 2])
        tile = region()
        q_stack = tile([H, S], BF16)
        k_stack = tile([H, S], BF16)
        probs = [[tile([S]) for h in range(HG)] for u in range(2)]
        v_all = tile([SB, H, 32])
        v_group = tile([SB, HG, 32])
        proj = tile([S])
        resid = tile([S])
        parts = [tile([3, S], BF16) for u in range(2)]
        max_parts = tile([2, HG * SB])
        neg_max = tile([HG * SB])
        neg_rows = tile([P])
        neg_parts = tile([3, P], BF16)
        o_group = tile([S])
        recip = proj
        o_sum = tile([S])

        tile = region()
        w1_all = tile([E, DC, FF])
        w2_all = tile([E, FC, D])
        b2_rows = tile([E, D])
        x_tile = tile([D])
        x_t = tile([DC, P])
        h_tile = tile([FF])
        hidden_t = tile([FC, P])
        y_tile = tile([D])
        y_back = region()([NBLK, 2, D])
        lap_x = arena[:, ARENA - SB * D:].rearrange("p (i d) -> p i d", d=D)
        du = xwT[:].rearrange("p c s -> p (c s)").rearrange("p (i d) -> p i d", d=D)

        psum = ctx.enter_context(nc.psum_tensor("psum", [P, 8, 512], F32))
        banks = [psum[:, i] for i in range(8)]

        consts_in = sem("consts_in")
        zeros_set = sem("zeros_set")
        padded_done = sem("padded_done")
        dve_steps = sem("dve_steps")
        fracs_done = sem("fracs_done")
        index_ready = sem("index_ready")
        pool_steps = sem("pool_steps")
        pool_held = sem("pool_held")
        band_landed = [sem(f"band_landed{u}") for u in range(2)]
        strips_turned = sem("strips_turned")
        strip_act = sem("strip_act")
        strip_dve = sem("strip_dve")
        strip_stored = [sem(f"strip_stored{u}") for u in range(2)]
        taps_landed = [sem(f"taps_landed{u}") for u in range(2)]
        hats_ready = sem("hats_ready")
        act_hats = sem("act_hats")
        warp_dve = sem("warp_dve")
        warp_mixed = sem("warp_mixed")
        fast_steps = [sem(f"fast_steps{b}") for b in range(NB)]
        slow_steps = [sem(f"slow_steps{b}") for b in range(NB)]
        slow_landed = [[sem(f"slow_landed{b}{u}") for u in range(2)] for b in range(NB)]
        warp_turned = sem("warp_turned")
        xwT_done = sem("xwT_done")
        wo_cleared = sem("wo_cleared")
        weights_in = sem("weights_in")
        masks_set = sem("masks_set")
        projected = sem("projected")
        proj_read = sem("proj_read")
        split_act = sem("split_act")
        split_dve = sem("split_dve")
        parts_ready = sem("parts_ready")
        parts_stored = [sem(f"parts_stored{u}") for u in range(2)]
        stack_in = sem("stack_in")
        v_ready = sem("v_ready")
        v_group_ready = sem("v_group_ready")
        scored = sem("scored")
        exp_done = sem("exp_done")
        pv_done = sem("pv_done")
        max_scored = sem("max_scored")
        max_read = sem("max_read")
        max_steps = sem("max_steps")
        neg_ready = sem("neg_ready")
        neg_parted = sem("neg_parted")
        neg_in = sem("neg_in")
        o_read = sem("o_read")
        o_normed = sem("o_normed")
        attended = sem("attended")
        x1_ready = sem("x1_ready")
        norm_steps = sem("norm_steps")
        v_cleared = sem("v_cleared")
        pairs_cleared = sem("pairs_cleared")
        experts_in = sem("experts_in")
        lap_made = sem("lap_made")
        du_ready = sem("du_ready")
        b1_turned = sem("b1_turned")
        du_turned = sem("du_turned")
        du_t_ready = sem("du_t_ready")
        routed = sem("routed")
        gap_ready = sem("gap_ready")
        gap_exp = sem("gap_exp")
        chosen_ready = sem("chosen_ready")
        ranked = sem("ranked")
        slots_ready = sem("slots_ready")
        scattered = sem("scattered")
        x_in = sem("x_in")
        x_turned = sem("x_turned")
        x_t_ready = sem("x_t_ready")
        h_made = sem("h_made")
        h_ready = sem("h_ready")
        h_turned = sem("h_turned")
        hidden_ready = sem("hidden_ready")
        y_made = sem("y_made")
        y_ready = sem("y_ready")
        y_stored = sem("y_stored")
        gathered = [sem(f"gathered{i}") for i in range(NBLK)]
        summed = sem("summed")
        all_out = sem("all_out")

        block = ctx.enter_context(nc.Block())

        def column_blocks(eng):
            for b in range(NB):
                with eng.Fori(0, JB // 2) as it:
                    for i in range(2):
                        at = b * JB + i
                        yield b, it * 2 + i, it * 2 + at, at % 2, it + at // 2
                for q in range(JB // 2 * 2, JB):
                    at = b * JB + q
                    yield b, q, at, at % 2, at // 2

        @block.sync
        def _(sp):
            sp.dma_start(cst[:], consts).then_inc(consts_in, 16)
            sp.dma_start(ang[:], angle.unsqueeze(0).broadcast_to([P, NB])).then_inc(consts_in, 16)
            sp.dma_start(shf[:], shift.rearrange("b t -> (b t)").unsqueeze(0).broadcast_to([P, NB * 2])
                         .rearrange("p (b t) -> p b t", b=NB)).then_inc(consts_in, 16)
            for b in range(NB):
                sp.dma_start(padded_v[b, PAD_Y:PAD_Y + S, PAD_X:PAD_X + D], x[b]).then_inc(padded_done, 16)
            sp.wait_ge(zeros_set, 1)
            for b in range(NB):
                for y in (0, PAD_Y + S):
                    sp.dma_start(padded_v[b, y:y + PAD_Y].rearrange("y x -> (y x)").rearrange("(p n) -> p n", p=16),
                                 zeros[0:16, 0:PAD_Y * PADW // 16]).then_inc(padded_done, 16)
                for x0, w in ((0, PAD_X), (PAD_X + D, PADW - PAD_X - D)):
                    sp.dma_start(padded_v[b, PAD_Y:PAD_Y + S, x0:x0 + w].rearrange("(q p) x -> p q x", p=P),
                                 zeros[:, 0:SB * w].rearrange("p (q x) -> p q x", q=SB)).then_inc(padded_done, 16)
            sp.dma_start(pairs_x.rearrange("(p i) d -> p i d", p=P),
                         zeros[:, 0:D].unsqueeze(1).broadcast_to([P, SLOT_TILES, D])).then_inc(pairs_cleared, 16)
            sp.wait_ge(index_ready, 1)
            for b in range(NB):
                sp.dma_start(fracs[b * J * 2:(b + 1) * J * 2].rearrange("(n p t) -> p n t", p=P, t=2),
                             col_f[:, b]).then_inc(fracs_done, 16)
            for b, q, n, u, turn in column_blocks(sp):
                sp.wait_ge(strip_act, n * 3 + 6)
                sp.wait_ge(strip_dve, n * 3 + 6)
                for k, (x0, w) in enumerate(XBLOCKS):
                    sp.dma_start(table_v[b][x0:x0 + w, :, bass.ds(q * P, P)],
                                 strip[u][0:w, k]).then_inc(strip_stored[u], 16)
            for b in range(NB):
                for k in range(2 * DC):
                    kind, c = k // DC, k % DC
                    sp.wait_ge(parts_ready, b * 2 * DC + k + 1)
                    sp.dma_start(qk_parts[b][kind, :, c * P:(c + 1) * P].rearrange("t p s -> p t s"),
                                 parts[k % 2]).then_inc(parts_stored[k % 2], 16)
                for u in range(2):
                    sp.wait_ge(parts_stored[u], 16 * DC * (b + 1))
                if b:
                    sp.wait_ge(pv_done, 2 + b * NG * SB)
                for i, pair in enumerate(PRODUCTS):
                    for kind, stack in enumerate((q_stack, k_stack)):
                        sp.dma_start(stack[i * DH:(i + 1) * DH],
                                     qk_parts[b][kind, pair[kind]].rearrange("(h d) s -> d h s", h=H)
                                     ).then_inc(stack_in, 16)

                def store_neg(g):
                    sp.wait_ge(neg_parted, b * NG + g + 1)
                    for i in range(3):
                        sp.dma_start(q_stack.rearrange("p h s -> p (h s)")[KROWS + i:KROWS + i + 1,
                                                                          bass.ds(g * (HG * S), HG * S)],
                                     neg_parts[0:HG * SB, i]).then_inc(neg_in, 16)

                store_neg(0)
                with sp.Fori(0, NG - 1) as g:
                    store_neg(g + 1)
            sp.wait_ge(x1_ready, NBLK)
            for e in range(E):
                sp.dma_start(w1_all[:, e], w1[e].rearrange("(c p) f -> p c f", p=P)).then_inc(experts_in, 16)
                sp.dma_start(w2_all[:, e], w2[e].rearrange("(c p) d -> p c d", p=P)).then_inc(experts_in, 16)
            sp.dma_start(b2_rows, b2.rearrange("e d -> (e d)").unsqueeze(0).broadcast_to([P, E * D])
                         .rearrange("p (e d) -> p e d", e=E)).then_inc(experts_in, 16)

            def load_tile(t):
                sp.wait_ge(x_turned, t + 1)
                sp.dma_start(x_tile, pairs_x[bass.ds(t * P, P), :]).then_inc(x_in, 16)

            def store_tile(t):
                sp.wait_ge(y_ready, t + 2)
                sp.dma_start(pairs_y[bass.ds(t * P, P), :], y_tile).then_inc(y_stored, 16)

            sp.wait_ge(scattered, 16 * 2 * NBLK)
            load_tile(0)
            load_tile(1)
            with sp.Fori(1, SLOT_TILES - 1) as t:
                load_tile(t + 1)
                store_tile(t - 1)
            store_tile(SLOT_TILES - 2)
            store_tile(SLOT_TILES - 1)
            for i in range(NBLK):
                sp.wait_ge(summed, i + 1)
                b, r = i // SB, i % SB
                sp.dma_start(out[b, r * P:(r + 1) * P], x1[:, i]).then_inc(all_out, 16)
            sp.wait_ge(all_out, 16 * NBLK)

        def pool_hold(semaphore, value):
            nc.gpsimd.wait_ge(semaphore, value)
            nc.gpsimd.sem_inc(pool_held, 1)

        SLOW_HEAD, SLOW_POINT = 32, 3
        SLOW_BLOCK = SLOW_HEAD + SLOW_POINT * D

        def steep_block(pool, b, blk, u, it):
            g = nc.gpsimd
            block_base = it * (2 * SLOW_BLOCK) + u * SLOW_BLOCK
            steps = Steps(pool, slow_steps[b], block_base, pool_hold)
            par = [slow_par[:, i:i + 1] for i in range(8)]
            us, vs, fl, ab, ix = (slow[:, i] for i in range(5))
            pool_hold(warp_mixed, blk + 1)
            steps.do(g.memset(slow_taps[:], 0.0))
            steps.do(g.tensor_copy(slow_par[:, 0:4], row_par[:, bass.ds(blk, 1)].squeeze(1)))
            steps.do(g.tensor_copy(slow_par[:, 4:8], row_bias[:, bass.ds(blk, 1)].squeeze(1)))
            steps.do(g.tensor_scalar(us, const("column"), par[0], par[2], ALU.mult, ALU.add))
            steps.do(g.tensor_scalar(us, us, -2.0, float(D + 2), ALU.max, ALU.min))
            steps.do(g.tensor_scalar(vs, const("column"), par[1], par[3], ALU.mult, ALU.add))
            steps.do(g.tensor_scalar(vs, vs, -2.0, float(S + 2), ALU.max, ALU.min))
            steps.do(g.memset(ix, float(b * PADH * PADW)))
            for ax, w, pad, width in ((0, us, PAD_X, 1), (1, vs, PAD_Y, PADW)):
                steps.do(g.tensor_copy(slow_i[:], w))
                steps.do(g.tensor_copy(fl, slow_i[:]))
                steps.do(g.tensor_tensor(ab, fl, w, ALU.subtract))
                steps.do(g.tensor_scalar(ab, ab, 0.0, None, ALU.is_gt))
                steps.do(g.tensor_tensor(fl, fl, ab, ALU.subtract))
                steps.do(g.tensor_tensor(w, w, fl, ALU.subtract))
                steps.do(g.tensor_scalar(w, w, par[4 + 2 * ax + 1], None, ALU.subtract))
                steps.do(g.tensor_scalar(slow_frac[:, :, ax], w, -1.0, None, ALU.add))
                steps.do(g.tensor_scalar(fl, fl, float(pad), None, ALU.add))
                steps.do(g.tensor_scalar(fl, fl, float(width), None, ALU.mult))
                steps.do(g.tensor_tensor(ix, ix, fl, ALU.add))
            steps.do(g.tensor_copy(slow_i[:], ix))
            steps.do(g.memset(slow_run[:, 0:2], 0.0))
            assert steps.n == SLOW_HEAD, steps.n
            with pool.Fori(0, D) as j:
                inner = Steps(pool, slow_steps[b], block_base + SLOW_HEAD + j * SLOW_POINT, pool_hold)
                inner.do(g.tensor_copy(slow_col[:], slow_i[:, bass.ds(j, 1)]))
                g.indirect_dma_start(slow_run[:], None, padded.unsqueeze(0),
                                     bass.IndirectOffsetOnAxis(ap=slow_col[:], axis=1)).then_inc(slow_landed[b][u], 16)
                pool_hold(slow_landed[b][u], it * (16 * D) + j * 16 + 16)
                for r in range(2):
                    inner.do(g.tensor_copy(slow_taps[:, 0:2, r, bass.ds(j, 1)],
                                           slow_run[:, r * PADW:r * PADW + 2].unsqueeze(2)))
            pool.dma_start(frac[u][:], slow_frac[:]).then_inc(taps_landed[u], 16)
            for d in range(3):
                for r in range(3):
                    pool.dma_start(taps[u][:, d, r], slow_taps[:, d, r]).then_inc(taps_landed[u], 16)
            pool_hold(taps_landed[u], (it + b * SB // 2) * 160 + 160)

        @block.gpsimd
        def _(pool):
            nc.gpsimd.memset(zeros[:], 0.0).then_inc(zeros_set, 1)
            nc.gpsimd.memset(wo_stack[:], 0.0).then_inc(wo_cleared, 1)
            pool.wait_ge(index_ready, 1)
            pool.wait_ge(padded_done, 16 * 5 * NB)
            for b, q, n, u, turn in column_blocks(pool):
                steps = Steps(pool, pool_steps, n, pool_hold)
                pool_hold(strips_turned, n * 6 + 6)
                steps.do(nc.gpsimd.tensor_copy(band_col[:, u:u + 1], band_index[:, bass.ds(n, 1)]))
                nc.gpsimd.indirect_dma_start(
                    band[u][:], None, padded.unsqueeze(0),
                    bass.IndirectOffsetOnAxis(ap=band_col[:, u:u + 1], axis=1)).then_inc(band_landed[u], 16)
            pool.wait_ge(fracs_done, 16 * NB)
            for b in range(NB):
                for u in range(2):
                    strips = ((b + 1) * JB + 1 - u) // 2
                    pool.wait_ge(strip_stored[u], 48 * (strips + 1))
                beyond = pool.value_load(steep[0:1, b * SB:b * SB + 1], min_val=0, max_val=1)
                with pool.If(beyond < 1):
                    with pool.Fori(0, SB // 2) as it:
                        steps = Steps(pool, fast_steps[b], it * 4, pool_hold)
                        for u in range(2):
                            blk = it * 2 + u + b * SB
                            pool_hold(warp_mixed, blk + 1)
                            steps.mark(nc.gpsimd.tensor_copy(tap_col[:, u:u + 1], tap_index[:, bass.ds(blk, 1)]))
                            steps.do(nc.gpsimd.tensor_copy(frac_col[:, u:u + 1], frac_index[:, bass.ds(blk, 1)]))
                            nc.gpsimd.indirect_dma_start(
                                frac[u][:].rearrange("p d t -> p (d t)"), None, fracs.unsqueeze(0),
                                bass.IndirectOffsetOnAxis(ap=frac_col[:, u:u + 1], axis=1)
                            ).then_inc(taps_landed[u], 16)
                            for d in range(3):
                                for r in range(3):
                                    nc.gpsimd.indirect_dma_start(
                                        taps[u][:, d, r], None, table[b].unsqueeze(0),
                                        bass.IndirectOffsetOnAxis(ap=tap_col[:, u:u + 1], axis=1),
                                        element_offset=(d * R + r) * J).then_inc(taps_landed[u], 16)
                with pool.If(beyond > 0):
                    with pool.Fori(0, SB // 2) as it:
                        for u in range(2):
                            blk = it * 2 + u + b * SB
                            steep_block(pool, b, blk, u, it)
            pool.wait_ge(xwT_done, NBLK + 2)
            g_ = nc.gpsimd
            g_.memset(v_all, 0.0).then_inc(v_cleared, 1)
            pool.wait_ge(v_cleared, 1)
            g_.memset(v_all[:, :, :, DH:DH + 1], 1.0).then_inc(v_cleared, 1)
            pool.wait_ge(v_cleared, 2)
            g_.memset(k_stack[KROWS:KROWS + 3], 1.0).then_inc(v_cleared, 1)
            for b in range(NB):
                pool.wait_ge(v_ready, b + 1)
                with pool.Fori(0, NG) as g:
                    pool_hold(pv_done, (g + b * NG) * SB + 2)
                    g_.tensor_copy(v_group, v_all[:, :, bass.ds(g * HG, HG)]).then_inc(v_group_ready, 1)
            pool.wait_ge(slots_ready, 1)
            pool.wait_ge(pairs_cleared, 16)
            for i in range(NBLK):
                for k in range(2):
                    g_.indirect_dma_start(pairs_x, bass.IndirectOffsetOnAxis(ap=slot_index[:, k, i:i + 1], axis=0),
                                          du[:, i], None).then_inc(scattered, 16)
            pool.wait_ge(y_stored, 16 * SLOT_TILES + 16)
            for i in range(NBLK):
                for k in range(2):
                    g_.indirect_dma_start(y_back[:, i, k], None, pairs_y,
                                          bass.IndirectOffsetOnAxis(ap=slot_index[:, k, i:i + 1], axis=0)
                                          ).then_inc(gathered[i], 16)

        @block.scalar
        def _(act):
            for i, w in enumerate((wq, wk, wv)):
                act.dma_start(wqkv[:, i], w.rearrange("(c p) n -> p c n", p=P)).then_inc(weights_in, 16)
            for i, w in enumerate((bq, bk)):
                act.dma_start(bqk[:, i], w.rearrange("(c p) -> p c", p=P),
                              allow_slow_non_contiguous=True).then_inc(weights_in, 16)
            act.dma_start(bv_rows[:], bv.unsqueeze(0).broadcast_to([P, D])).then_inc(weights_in, 16)
            for i, z in enumerate((zx, zy, zr)):
                act.dma_start(z_cols[:, i], z.unsqueeze(0).broadcast_to([P, NB])).then_inc(weights_in, 16)
            act.dma_start(wr_cols[:], wr.rearrange("(c p) e -> p c e", p=P)).then_inc(weights_in, 16)
            act.dma_start(br_row[:], br.unsqueeze(0).broadcast_to([P, E])).then_inc(weights_in, 16)
            act.dma_start(b1_rows[:], b1.rearrange("e (f p) -> (e f) p", p=P)).then_inc(weights_in, 16)
            act.wait_ge(wo_cleared, 1)
            for h in range(HG):
                act.dma_start(wo_stack[32 * h:32 * h + DH], wo).then_inc(weights_in, 16)
                act.dma_start(wo_stack[32 * h + DH:32 * h + DH + 1], bo.unsqueeze(0)).then_inc(weights_in, 16)
            act.dma_start(x1[:].rearrange("p (b i) d -> p b i d", b=NB),
                          x.rearrange("b (i p) d -> p b i d", p=P)).then_inc(weights_in, 16)
            for b, q, n, u, turn in column_blocks(act):
                act.wait_ge(strip_stored[u], turn * 48 + 48)
                for g in range(3):
                    k, half = g // 2, g % 2
                    w = XBLOCKS[k][1]
                    act.wait_ge(strips_turned, n * 6 + g + 13)
                    nc.scalar.activation(strip[u][0:w, k, 4 * half:4 * half + 4],
                                         banks[g][0:w, :].rearrange("p (r q) -> p r q", r=4),
                                         ACT.Copy).then_inc(strip_act, 1)
            with act.Fori(0, NBLK // 2) as it:
                steps = Steps(act, act_hats, it * 4)
                for u in range(2):
                    blk = it * 2 + u
                    act.wait_ge(taps_landed[u], it * 160 + 160)
                    act.wait_ge(warp_mixed, blk + 1)
                    for ax in range(2):
                        f = frac[u][:, :, ax]
                        up = row_bias[:, bass.ds(blk, 1), 2 * ax]
                        down = row_bias[:, bass.ds(blk, 1), 2 * ax + 1]
                        h = hats[u][:, ax]
                        nc.scalar.activation(h[:, 0], f, ACT.Relu, bias=up, scale=-1.0)
                        nc.scalar.activation(h[:, 2], f, ACT.Relu, bias=down)
                        steps.mark(nc.scalar.activation(h[:, 3], f, ACT.Abs, bias=down))
                    steps.wait()
                    for ax in range(2):
                        h = hats[u][:, ax]
                        ins = nc.scalar.activation(h[:, 1], h[:, 3], ACT.Relu, bias=const("ones")[:, 0:1], scale=-1.0)
                    ins.then_inc(hats_ready, 1)
                for u in range(2):
                    blk = it * 2 + u
                    act.wait_ge(warp_turned, blk + 1)
                    nc.scalar.activation(xwT[:, :, bass.ds(blk * P, P)],
                                         banks[6 + u][:, 0:D].rearrange("p (c q) -> p c q", c=DC),
                                         ACT.Copy).then_inc(xwT_done, 1)
            for b in range(NB):
                for k in range(2 * DC):
                    kind, c = k // DC, k % DC
                    n = b * 2 * DC + k
                    act.wait_ge(projected, b * PROJ_BATCH + 2 * k + 2)
                    act.wait_ge(parts_ready, n) if n else None
                    nc.scalar.activation(proj.rearrange("p (a q) -> p a q", a=2), psum[:, 2 * k:2 * k + 2],
                                         ACT.Identity, bias=bqk[:, kind, c:c + 1]).then_inc(proj_read, 1)
                with act.Fori(0, NG) as g:
                    n0 = (g + b * NG) * (SB * HG)
                    for kt in range(SB):
                        act.wait_ge(pv_done, (g + b * NG) * SB + kt + 1)
                        for h in range(HG):
                            act.wait_ge(scored, n0 + (kt * HG + h + 1))
                            slot = (kt * HG + h) % 2
                            nc.scalar.activation(
                                probs[kt % 2][h][:, kt * P:S],
                                psum[:, 2 * slot:2 * slot + 2].rearrange("p a q -> p (a q)")[:, kt * P:S],
                                ACT.Exp, scale=DH ** -0.5).then_inc(exp_done, 1)
                    act.wait_ge(pv_done, (g + b * NG) * SB + SB + 2)
                    act.wait_ge(o_normed, g + (b * NG + 1))
                    nc.scalar.activation(o_group.rearrange("p (a q) -> p a q", a=2), psum[:, 4:6],
                                         ACT.Copy).then_inc(o_read, 1)
            for i in range(NBLK):
                act.wait_ge(du_turned, i + 1)
                if i >= 2:
                    act.wait_ge(routed, i - 1)
                nc.scalar.activation(du_t[i % 2], banks[i % 2][:, 0:D].rearrange("p (c q) -> p c q", c=DC),
                                     ACT.Copy).then_inc(du_t_ready, 1)
            act.wait_ge(gap_ready, 1)
            nc.scalar.activation(route[:, 1], route[:, 0], ACT.Exp).then_inc(gap_exp, 1)

            def hidden(t):
                act.wait_ge(h_turned, t + 1)
                e = act.value_load(tile_expert[0:1, bass.ds(t, 1)], min_val=0, max_val=E - 1)
                for f in range(FC):
                    ins = nc.scalar.activation(hidden_t[:, f], banks[3 + f // 4][:, (f % 4) * P:(f % 4 + 1) * P],
                                               ACT.Relu, bias=b1_cols[:, bass.ds(e, 1), f])
                ins.then_inc(hidden_ready, 1)

            act.wait_ge(slots_ready, 1)
            with act.Fori(0, SLOT_TILES) as t:
                hidden(t)

        @block.tensor
        def _(pe):
            pe.wait_ge(consts_in, 48)
            for b, q, n, u, turn in column_blocks(pe):
                pe.wait_ge(band_landed[u], turn * 16 + 16)
                for g in range(6):
                    k, half = g // 2, g % 2
                    x0, w = XBLOCKS[k]
                    if g < 3:
                        pe.wait_ge(strip_act, n * 3 + g + 1)
                    else:
                        pe.wait_ge(strip_dve, n * 3 + g - 2)
                    for r in range(4):
                        at = (4 * half + r) * PADW + x0
                        ins = nc.tensor.transpose(banks[g][0:w, r * P:(r + 1) * P], band[u][:, at:at + w], ident)
                    ins.then_inc(strips_turned, 1)
            with pe.Fori(0, NBLK // 2) as it:
                for u in range(2):
                    blk = it * 2 + u
                    pe.wait_ge(warp_mixed, blk + 3)
                    pe.wait_ge(xwT_done, blk + 1)
                    for c in range(DC):
                        ins = nc.tensor.transpose(banks[6 + u][:, c * P:(c + 1) * P], warped[u][:, c * P:(c + 1) * P],
                                                  ident)
                    ins.then_inc(warp_turned, 1)
            t_ = nc.tensor
            for b in range(NB):
                pe.wait_ge(xwT_done, NBLK + 2)
                pe.wait_ge(weights_in, 16 * N_WEIGHTS)
                if b:
                    pe.wait_ge(x1_ready, SB * b)
                for k in range(2 * DC):
                    kind, c = k // DC, k % DC
                    for half in range(2):
                        for dc in range(DC):
                            ins = t_.matmul(banks[2 * k + half], wqkv[:, kind, dc, c * P:(c + 1) * P],
                                            xwT[:, dc, b * S + half * 512:b * S + (half + 1) * 512],
                                            start=dc == 0, stop=dc == DC - 1)
                        ins.then_inc(projected, 1)
                for kt in range(SB):
                    pe.wait_ge(proj_read, b * 2 * DC + kt // 4 + 1)
                    for dc in range(DC):
                        ins = t_.matmul(banks[kt // 2][:, (kt % 2) * D:(kt % 2 + 1) * D],
                                        xwT[:, dc, b * S + kt * P:b * S + (kt + 1) * P], wqkv[:, 2, dc],
                                        start=dc == 0, stop=dc == DC - 1)
                    ins.then_inc(projected, 1)
                pe.wait_ge(stack_in, 16 * 2 * len(PRODUCTS) * (b + 1))
                pe.wait_ge(masks_set, 3)
                pe.wait_ge(v_cleared, 3)
                pe.wait_ge(proj_read, (b + 1) * 2 * DC)
                pe.wait_ge(v_ready, b + 1)

                def side_bank(m, slot, ahead=1):
                    pe.wait_ge(max_read, m + (b * SIDE_BATCH + ahead))
                    return banks[6 + slot]

                def max_chunk(g, i, m0):
                    h, r = i // 12, i % 12
                    qb, kc = (r, 0) if r < 4 else (4 + (r - 4) // 2, (r - 4) % 2)
                    keys = min((qb + 1) * P - kc * 512, 512)
                    diagonal = qb * P < kc * 512 + keys and qb * P >= kc * 512
                    bank = side_bank(m0 + i, i % 2, 1 if i else 2)
                    ins = t_.matmul(bank[:, 0:keys],
                                    q_stack[0:KROWS, bass.ds(g * HG + h, 1), qb * P:(qb + 1) * P].squeeze(1),
                                    k_stack[0:KROWS, bass.ds(g * HG + h, 1), kc * 512:kc * 512 + keys].squeeze(1),
                                    start=True, stop=not diagonal)
                    if diagonal:
                        at = qb * P - kc * 512
                        ins = t_.matmul(bank[:, at:at + P], ident_b[:], mask_qk[:], start=False, stop=True)
                    ins.then_inc(max_scored, 1)

                def turn_neg(g, m):
                    pe.wait_ge(neg_ready, g + (b * NG + 1))
                    bank = side_bank(m, 0)
                    t_.transpose(bank[0:HG * SB, 0:P], neg_max, ident).then_inc(max_scored, 1)

                def weighted(g, kt):
                    pe.wait_ge(exp_done, g * (SB * HG) + (b * NG * SB * HG + HG * (kt + 1) + 2))
                    if kt == 0:
                        pe.wait_ge(o_read, g + (b * NG + 1))
                        pe.wait_ge(v_group_ready, g + (b * NG + 1))
                    for half in range(kt // 4, 2):
                        q0 = max(kt * P, half * 512)
                        for h in range(HG):
                            ins = t_.matmul(banks[4 + half][32 * h:32 * h + 32, q0 - half * 512:512],
                                            v_group[:, kt, h], probs[kt % 2][h][:, q0:(half + 1) * 512],
                                            start=kt == 0, stop=kt == 4 * half + 3)
                    ins.then_inc(pv_done, 1)

                def group(g, m0, chunks):
                    n0 = g * (SB * HG) + b * NG * SB * HG
                    pe.wait_ge(neg_in, g * 48 + (b * NG * 48 + 48))
                    i = 0
                    for kt in range(SB):
                        for h in range(HG):
                            n = kt * HG + h
                            pe.wait_ge(exp_done, n0 + (n + 1))
                            for half in range(kt // 4, 2):
                                q0 = max(kt * P, half * 512)
                                bank = banks[2 * (n % 2) + half]
                                diagonal = q0 == kt * P
                                ins = t_.matmul(
                                    bank[:, q0 - half * 512:512],
                                    k_stack[0:KROWS + 3, bass.ds(g * HG + h, 1), kt * P:(kt + 1) * P].squeeze(1),
                                    q_stack[0:KROWS + 3, bass.ds(g * HG + h, 1), q0:(half + 1) * 512].squeeze(1),
                                    start=True, stop=not diagonal)
                                if diagonal:
                                    at = kt * P - half * 512
                                    ins = t_.matmul(bank[:, at:at + P], ident_b[:], mask_kq[:],
                                                    start=False, stop=True)
                            ins.then_inc(scored, 1)
                            for _ in range(2 if chunks else 0):
                                if i < 48:
                                    max_chunk(g + 1, i, m0)
                                    i += 1
                        if kt:
                            weighted(g, kt - 1)
                        if chunks and kt == SB - 2:
                            turn_neg(g + 1, m0 + 48)
                    weighted(g, SB - 1)
                    pe.wait_ge(o_read, g + (b * NG + 2))
                    m = m0 + (49 if chunks else 0)
                    for half in range(2):
                        bank = side_bank(m + half, 1 - half)
                        t_.matmul(bank, const("head_sum"), o_group[:, half * 512:(half + 1) * 512],
                                  start=True, stop=True).then_inc(max_scored, 1)

                for i in range(48):
                    max_chunk(0, i, 0)
                turn_neg(0, 48)
                with pe.Fori(0, NG - 1) as g:
                    group(g, g * SIDE_GROUP + SIDE_FIRST, True)
                group(NG - 1, SIDE_GROUP * (NG - 1) + SIDE_FIRST, False)
                pe.wait_ge(exp_done, 2 + (b + 1) * NG * SB * HG)
                pe.wait_ge(max_read, 2 + (b + 1) * SIDE_BATCH)
                pe.wait_ge(o_normed, 1 + (b + 1) * NG)
                for i in range(SB):
                    t_.matmul(banks[i][:, 0:D], o_sum[:, i * P:(i + 1) * P], wo_stack[:],
                              start=True, stop=True).then_inc(attended, 1)
            for b in range(NB):
                pe.wait_ge(x1_ready, NBLK)
                for i in range(SB):
                    bank = banks[4 * b + i // 2][:, (i % 2) * D:(i % 2 + 1) * D]
                    terms = [(("lap_first" if i == 0 else "lap_last" if i == SB - 1 else "lap_mid"), i)]
                    terms += [("lap_prev", i - 1)] if i else []
                    terms += [("lap_next", i + 1)] if i < SB - 1 else []
                    for k, (name, j) in enumerate(terms):
                        ins = t_.matmul(bank, const(name), x1[:, b * SB + j], start=k == 0, stop=k == len(terms) - 1)
                    ins.then_inc(lap_made, 1)
            pe.wait_ge(du_ready, NB)
            t_.transpose(banks[3][:, 0:E * FC], b1_rows[:], const("identity")[0:E * FC, 0:E * FC]).then_inc(b1_turned, 1)
            for i in range(NBLK + 1):
                if i < NBLK:
                    if i >= 2:
                        pe.wait_ge(du_t_ready, i - 1)
                    for c in range(DC):
                        ins = t_.transpose(banks[i % 2][:, c * P:(c + 1) * P], du[:, i, c * P:(c + 1) * P], ident)
                    ins.then_inc(du_turned, 1)
                if i:
                    pe.wait_ge(du_t_ready, i)
                    for c in range(DC):
                        ins = t_.matmul(banks[2][:, (i - 1) * E:i * E], du_t[(i - 1) % 2][:, c], wr_cols[:, c],
                                        start=c == 0, stop=c == DC - 1)
                    ins.then_inc(routed, 1)
            pe.wait_ge(chosen_ready, 1)
            t_.matmul(banks[4][:, 0:NBLK * E], const("before"), chosen, start=True, stop=True).then_inc(ranked, 1)
            t_.matmul(banks[5][:, 0:NBLK * E], const("ones"), chosen, start=True, stop=True).then_inc(ranked, 1)
            def turn_x(t):
                pe.wait_ge(x_in, t * 16 + 16)
                for c in range(DC):
                    ins = t_.transpose(banks[2][:, c * P:(c + 1) * P], x_tile[:, c * P:(c + 1) * P], ident)
                ins.then_inc(x_turned, 1)

            def first_product(t, e):
                pe.wait_ge(x_t_ready, t + 1)
                pe.wait_ge(h_ready, t + 1)
                for half in range(2):
                    for c in range(DC):
                        ins = t_.matmul(banks[half], x_t[:, c],
                                        w1_all[:, bass.ds(e, 1), c, half * 512:(half + 1) * 512].squeeze(1),
                                        start=c == 0, stop=c == DC - 1)
                ins.then_inc(h_made, 1)

            def turn_h(t):
                pe.wait_ge(h_ready, t + 2)
                for f in range(FC):
                    ins = t_.transpose(banks[3 + f // 4][:, (f % 4) * P:(f % 4 + 1) * P], h_tile[:, f * P:(f + 1) * P],
                                       ident)
                ins.then_inc(h_turned, 1)

            def second_product(t, e):
                pe.wait_ge(hidden_ready, t + 1)
                pe.wait_ge(y_ready, t + 1)
                for f in range(FC):
                    ins = t_.matmul(banks[5][:, 0:D], hidden_t[:, f], w2_all[:, bass.ds(e, 1), f].squeeze(1),
                                    start=f == 0, stop=f == FC - 1)
                ins.then_inc(y_made, 1)

            def expert_of(t):
                return pe.value_load(tile_expert[0:1, bass.ds(t, 1)], min_val=0, max_val=E - 1)

            pe.wait_ge(slots_ready, 1)
            pe.wait_ge(experts_in, 16 * (2 * E + 1))
            turn_x(0)
            first_product(0, expert_of(0))
            turn_x(1)
            turn_h(0)
            with pe.Fori(1, SLOT_TILES - 1) as t:
                first_product(t, expert_of(t))
                turn_x(t + 1)
                second_product(t - 1, expert_of(t - 1))
                turn_h(t)
            last = SLOT_TILES - 1
            first_product(last, expert_of(last))
            second_product(last - 1, expert_of(last - 1))
            turn_h(last)
            second_product(last, expert_of(last))

        @block.vector
        def _(dve):
            v = nc.vector
            steps = Steps(dve, dve_steps)
            dve.wait_ge(consts_in, 48)
            dve.wait_ge(zeros_set, 1)

            def ts(o, a, s1, op0, s2=None, op1=None):
                if op1 is None:
                    steps.do(v.tensor_scalar(o, a, s1, None, op0))
                else:
                    steps.do(v.tensor_scalar(o, a, s1, s2, op0, op1))

            def tt(o, a, b_, op):
                steps.do(v.tensor_tensor(o, a, b_, op))

            def stt(o, a, s, b_, op0, op1):
                steps.do(v.scalar_tensor_tensor(out=o, in0=a, scalar=s, in1=b_, op0=op0, op1=op1))

            def floor(o, a, whole, above):
                steps.do(v.tensor_copy(whole, a))
                steps.do(v.tensor_copy(o, whole))
                tt(above, o, a, ALU.is_gt)
                tt(o, o, above, ALU.subtract)

            (KQ, RA, Z2, SN, CS, ODD, K4, T0, T1, SIN, COS, TAN, CA, CB, CP, CQ, CU, CV, STEEP, T2) = range(20)
            pr = [prm[:, i] for i in range(40)]
            wi2 = tmp_i[:, 0:NB]
            ts(pr[T0], ang[:], 2 / np.pi, ALU.mult, 0.5, ALU.add)
            floor(pr[KQ], pr[T0], wi2, pr[T1])
            stt(pr[RA], pr[KQ], -1.5703125, ang[:], ALU.mult, ALU.add)
            stt(pr[RA], pr[KQ], -4.837512969970703125e-4, pr[RA], ALU.mult, ALU.add)
            stt(pr[RA], pr[KQ], -7.549789948768648e-8, pr[RA], ALU.mult, ALU.add)
            tt(pr[Z2], pr[RA], pr[RA], ALU.mult)
            ts(pr[T0], pr[Z2], -1.9515295891e-4, ALU.mult, 8.3321608736e-3, ALU.add)
            tt(pr[T0], pr[T0], pr[Z2], ALU.mult)
            ts(pr[T0], pr[T0], -1.6666654611e-1, ALU.add)
            tt(pr[T0], pr[T0], pr[Z2], ALU.mult)
            stt(pr[SN], pr[T0], 1.0, pr[RA], ALU.add, ALU.mult)
            ts(pr[T0], pr[Z2], 2.443315711809948e-5, ALU.mult, -1.388731625493765e-3, ALU.add)
            tt(pr[T0], pr[T0], pr[Z2], ALU.mult)
            ts(pr[T0], pr[T0], 4.166664568298827e-2, ALU.add)
            tt(pr[T0], pr[T0], pr[Z2], ALU.mult)
            ts(pr[T0], pr[T0], -0.5, ALU.add)
            tt(pr[T0], pr[T0], pr[Z2], ALU.mult)
            ts(pr[CS], pr[T0], 1.0, ALU.add)
            ts(pr[T0], pr[KQ], 0.25, ALU.mult)
            floor(pr[K4], pr[T0], wi2, pr[T1])
            stt(pr[K4], pr[K4], -4.0, pr[KQ], ALU.mult, ALU.add)
            ts(pr[T0], pr[K4], 0.5, ALU.mult)
            floor(pr[ODD], pr[T0], wi2, pr[T1])
            stt(pr[ODD], pr[ODD], -2.0, pr[K4], ALU.mult, ALU.add)
            tt(pr[T0], pr[CS], pr[SN], ALU.subtract)
            tt(pr[T0], pr[T0], pr[ODD], ALU.mult)
            tt(pr[SIN], pr[SN], pr[T0], ALU.add)
            tt(pr[COS], pr[CS], pr[T0], ALU.subtract)
            ts(pr[T0], pr[K4], 2.0, ALU.is_ge, -2.0, ALU.mult)
            stt(pr[SIN], pr[T0], 1.0, pr[SIN], ALU.add, ALU.mult)
            ts(pr[T0], pr[K4], 1.0, ALU.is_ge)
            ts(pr[T1], pr[K4], 3.0, ALU.is_lt)
            tt(pr[T0], pr[T0], pr[T1], ALU.mult)
            ts(pr[T0], pr[T0], -2.0, ALU.mult, 1.0, ALU.add)
            tt(pr[COS], pr[COS], pr[T0], ALU.mult)
            most = SHEAR / (S // 2)
            stt(pr[T0], pr[SIN], -1.0, pr[SIN], ALU.mult, ALU.max)
            stt(pr[T1], pr[COS], -1.0, pr[COS], ALU.mult, ALU.max)
            ts(pr[T1], pr[T1], -most, ALU.mult)
            tt(pr[STEEP], pr[T0], pr[T1], ALU.add)
            ts(pr[STEEP], pr[STEEP], 0.0, ALU.is_gt)
            ts(pr[T2], pr[T1], -1.0 / most, ALU.mult, 0.5, ALU.max)
            steps.do(v.reciprocal(pr[T2], pr[T2]))
            ts(pr[T1], pr[COS], 0.0, ALU.is_ge)
            ts(pr[T1], pr[T1], 2.0, ALU.mult, -1.0, ALU.add)
            tt(pr[T2], pr[T2], pr[T1], ALU.mult)
            tt(pr[TAN], pr[SIN], pr[T2], ALU.mult)
            ts(pr[CA], pr[SIN], KX, ALU.mult)
            ts(pr[CB], pr[COS], KX, ALU.mult)
            ts(pr[CP], pr[COS], KY, ALU.mult)
            ts(pr[CQ], pr[SIN], -KY, ALU.mult)
            for o, t, k, mid in ((CU, 1, KX, (D - 1) / 2), (CV, 0, KY, (S - 1) / 2)):
                ts(pr[o], shf[:, :, t], k, ALU.mult, mid, ALU.add)
                ts(pr[o], pr[o], -1.0e5, ALU.max, 1.0e5, ALU.min)

            def scalar(i, b):
                return prm[:, i, b:b + 1]

            t = [tmp[:, i] for i in range(12)]
            for b in range(NB):
                m, nn, ab, w5 = t[0][:, 0:JB], t[1][:, 0:JB], t[2][:, 0:JB], tmp_i[:, 0:JB]
                uj, vj = t[3][:, 0:JB], t[4][:, 0:JB]
                ts(uj, const("sheared"), scalar(CA, b), ALU.mult)
                floor(m, uj, w5, ab)
                tt(col_f[:, b, :, 0], uj, m, ALU.subtract)
                ts(vj, const("sheared"), scalar(CP, b), ALU.mult, scalar(CV, b), ALU.add)
                floor(nn, vj, w5, ab)
                tt(col_f[:, b, :, 1], vj, nn, ALU.subtract)
                ts(m, m, float(-MSHIFT), ALU.max, float(MSHIFT - 1), ALU.min)
                ts(nn, nn, float(-R_LOW), ALU.add, float(-R), ALU.max)
                ts(nn, nn, float(S), ALU.min, float(PAD_Y), ALU.add)
                stt(nn, nn, float(PADW), m, ALU.mult, ALU.add)
                ts(nn, nn, float(PAD_X - X_LOW + b * PADH * PADW), ALU.add)
                steps.do(v.tensor_copy(band_index[:, b * JB:(b + 1) * JB], nn))
            for b in range(NB):
                row = const("row")
                sh, w0, fw, e0, fe, ab, cu, cv = (t[i][:, 0:SB] for i in range(8))
                w8 = tmp_i[:, 0:SB]
                bs = slice(b * SB, (b + 1) * SB)
                ts(cu, row, scalar(TAN, b), ALU.mult, 0.5, ALU.add)
                floor(sh, cu, w8, ab)
                ts(sh, sh, float(-SHEAR), ALU.max, float(SHEAR), ALU.min)
                ts(cu, row, scalar(CB, b), ALU.mult, scalar(CU, b), ALU.add)
                stt(fw, sh, scalar(CA, b), cu, ALU.mult, ALU.add)
                floor(w0, fw, w8, ab)
                tt(fw, fw, w0, ALU.subtract)
                ts(cv, row, scalar(CQ, b), ALU.mult)
                stt(fe, sh, scalar(CP, b), cv, ALU.mult, ALU.add)
                floor(e0, fe, w8, ab)
                tt(fe, fe, e0, ALU.subtract)
                for i, f in ((0, fw), (2, fe)):
                    ts(row_bias[:, bs, i], f, -1.0, ALU.mult, 1.0, ALU.add)
                    ts(row_bias[:, bs, i + 1], f, -1.0, ALU.add)
                ts(w0, w0, float(-X_LOW), ALU.max, float(XW - X_LOW - 3), ALU.min)
                ts(e0, e0, float(-R_LOW), ALU.max, float(R - R_LOW - 3), ALU.min)
                ts(w0, w0, float(X_LOW), ALU.add)
                stt(e0, w0, float(R), e0, ALU.mult, ALU.add)
                ts(e0, e0, float(R_LOW), ALU.add, float(J), ALU.mult)
                tt(e0, e0, sh, ALU.subtract)
                ts(e0, e0, float(SHEAR), ALU.add)
                steps.do(v.tensor_copy(tap_index[:, bs], e0))
                ts(sh, sh, -2.0, ALU.mult, float(2 * (b * J + SHEAR)), ALU.add)
                steps.do(v.tensor_copy(frac_index[:, bs], sh))
                ts(row_par[:, bs, 0], row, 0.0, ALU.mult, scalar(CA, b), ALU.add)
                ts(row_par[:, bs, 1], row, 0.0, ALU.mult, scalar(CP, b), ALU.add)
                steps.do(v.tensor_copy(row_par[:, bs, 2], cu))
                ts(row_par[:, bs, 3], cv, scalar(CV, b), ALU.add)
                ts(t[8][:, 0:SB], row, 0.0, ALU.mult, scalar(STEEP, b), ALU.add)
                steps.do(v.tensor_copy(steep[:, bs], t[8][:, 0:SB]))
            dve.sem_inc(strips_turned, 12)
            dve.sem_inc(index_ready, 1)
            dve.sem_inc(strip_act, 3)
            dve.sem_inc(strip_dve, 3)
            dve.sem_inc(strip_stored[0], 48)
            dve.sem_inc(strip_stored[1], 48)
            dve.sem_inc(warp_mixed, 2)
            dve.sem_inc(exp_done, 2)
            dve.sem_inc(pv_done, 2)
            dve.sem_inc(max_read, 2)
            dve.sem_inc(o_read, 1)
            dve.sem_inc(x_turned, 1)
            dve.sem_inc(h_ready, 1)
            dve.sem_inc(y_ready, 1)
            dve.sem_inc(y_stored, 16)
            dve.sem_inc(o_normed, 1)
            for o, name in ((ident_b, "identity"), (mask_qk, "mask_qk"), (mask_kq, "mask_kq")):
                v.tensor_copy(o[:], const(name)).then_inc(masks_set, 1)
            dve.sem_inc(xwT_done, 2)
            for b, q, n, u, turn in column_blocks(dve):
                dve.wait_ge(strip_stored[u], turn * 48 + 48)
                for g in range(3, 6):
                    k, half = g // 2, g % 2
                    w = XBLOCKS[k][1]
                    dve.wait_ge(strips_turned, n * 6 + g + 13)
                    v.tensor_copy(strip[u][0:w, k, 4 * half:4 * half + 4],
                                  banks[g][0:w, :].rearrange("p (r q) -> p r q", r=4)).then_inc(strip_dve, 1)
            with dve.Fori(0, NBLK // 2) as it:
                st = Steps(dve, warp_dve, it * 14)
                for u in range(2):
                    blk = it * 2 + u
                    dve.wait_ge(taps_landed[u], it * 160 + 160)
                    dve.wait_ge(hats_ready, blk + 1)
                    for d in range(3):
                        hat = hats[u][:, 0, d].unsqueeze(1).broadcast_to([P, 3, D])
                        st.mark(v.tensor_tensor(taps[u][:, d], taps[u][:, d], hat, ALU.mult))
                    st.wait()
                    for d in (1, 2):
                        st.do(v.tensor_tensor(taps[u][:, 0], taps[u][:, 0], taps[u][:, d], ALU.add))
                    st.do(v.tensor_tensor(taps[u][:, 0], taps[u][:, 0], hats[u][:, 1, 0:3], ALU.mult))
                    st.do(v.tensor_tensor(taps[u][:, 0, 0], taps[u][:, 0, 0], taps[u][:, 0, 1], ALU.add))
                    dve.wait_ge(xwT_done, blk + 1)
                    v.tensor_tensor(warped[u][:], taps[u][:, 0, 0], taps[u][:, 0, 2], ALU.add).then_inc(warp_mixed, 1)
            dve.wait_ge(xwT_done, NBLK + 2)
            steps.do(v.memset(max_parts, -3.0e38))
            for b in range(NB):
                for k in range(2 * DC):
                    n = b * 2 * DC + k
                    dve.wait_ge(proj_read, n + 1)
                    if n >= 2:
                        dve.wait_ge(parts_stored[k % 2], 16 * (n // 2))
                    pt = parts[k % 2]
                    steps.do(v.tensor_copy(pt[:, 0], proj))
                    steps.do(v.tensor_tensor(resid, proj, pt[:, 0], ALU.subtract))
                    steps.do(v.tensor_copy(pt[:, 1], resid))
                    v.tensor_tensor(pt[:, 2], resid, pt[:, 1], ALU.subtract).then_inc(parts_ready, 1)
                dve.wait_ge(v_cleared, 3)
                dve.wait_ge(weights_in, 16 * N_WEIGHTS)
                if b:
                    dve.wait_ge(v_group_ready, b * NG)
                for k in range(4):
                    dve.wait_ge(projected, b * PROJ_BATCH + 8 + 2 * (k + 1))
                    steps.mark(v.tensor_tensor(v_all[:, 2 * k:2 * k + 2, :, 0:DH],
                                               banks[k].rearrange("p (t h d) -> p t h d", t=2, h=H),
                                               bv_rows[:].rearrange("p (h d) -> p h d", h=H).unsqueeze(1)
                                               .broadcast_to([P, 2, H, DH]), ALU.add))
                steps.wait()
                dve.sem_inc(v_ready, 1)
                steps.do(v.memset(o_sum, 0.0))

                def max_pass(g, m0):
                    st = Steps(dve, max_steps, g * 4 + b * NG * 4)
                    mb = m0 + b * SIDE_BATCH
                    for i in range(48):
                        h, r = i // 12, i % 12
                        qb, kc = (r, 0) if r < 4 else (4 + (r - 4) // 2, (r - 4) % 2)
                        keys = min((qb + 1) * P - kc * 512, 512)
                        dve.wait_ge(max_scored, mb + (i + 1))
                        v.reduce_max(max_parts[:, kc, h * SB + qb:h * SB + qb + 1], banks[6 + i % 2][:, 0:keys],
                                     AX_X).then_inc(max_read, 1)
                    dve.wait_ge(max_read, mb + 50)
                    st.do(v.tensor_tensor(neg_max, max_parts[:, 0], max_parts[:, 1], ALU.max))
                    v.tensor_scalar(neg_max, neg_max, -1.0, None, ALU.mult).then_inc(neg_ready, 1)
                    dve.wait_ge(max_scored, mb + 49)
                    v.tensor_copy(neg_rows[0:HG * SB], banks[6][0:HG * SB, 0:P]).then_inc(max_read, 1)
                    dve.wait_ge(max_read, mb + 51)
                    if not (isinstance(g, int) and b * NG + g == 0):
                        dve.wait_ge(neg_in, g * 48 + b * NG * 48)
                    nr, np_ = neg_rows[0:HG * SB], neg_parts[0:HG * SB]
                    st.do(v.tensor_copy(np_[:, 0], nr))
                    st.do(v.tensor_tensor(nr, nr, np_[:, 0], ALU.subtract))
                    st.do(v.tensor_copy(np_[:, 1], nr))
                    v.tensor_tensor(np_[:, 2], nr, np_[:, 1], ALU.subtract).then_inc(neg_parted, 1)

                def normalize(g, m):
                    st = Steps(dve, norm_steps, g + b * NG)
                    mb = m + b * SIDE_BATCH
                    for half in range(2):
                        dve.wait_ge(max_scored, mb + (half + 1))
                        v.reciprocal(recip[:, half * 512:(half + 1) * 512], banks[7 - half]).then_inc(max_read, 1)
                    dve.wait_ge(max_read, mb + 4)
                    st.do(v.tensor_tensor(recip, recip, o_group, ALU.mult))
                    v.tensor_tensor(o_sum, o_sum, recip, ALU.add).then_inc(o_normed, 1)

                max_pass(0, 0)
                with dve.Fori(0, NG - 1) as g:
                    max_pass(g + 1, g * SIDE_GROUP + SIDE_FIRST)
                    normalize(g, g * SIDE_GROUP + (SIDE_FIRST + 49))
                normalize(NG - 1, SIDE_GROUP * (NG - 1) + SIDE_FIRST)
                for i in range(SB):
                    dve.wait_ge(attended, b * SB + i + 1)
                    v.tensor_tensor(x1[:, b * SB + i], x1[:, b * SB + i], banks[i][:, 0:D],
                                    ALU.add).then_inc(x1_ready, 1)
            for b in range(NB):
                y = x1[:, b * SB:(b + 1) * SB]
                d = du[:, b * SB:(b + 1) * SB]
                zb = [z_cols[:, i, b:b + 1] for i in range(4)]
                if b == 0:
                    dve.wait_ge(x1_ready, NBLK)
                steps.do(v.tensor_scalar(z_cols[:, 3, b:b + 1], zb[2], -1.0, None, ALU.mult))
                steps.mark(v.tensor_scalar(d, y, zb[3], zb[2], ALU.mult, ALU.add))
                steps.mark(v.tensor_tensor(lap_x[:, :, 1:D - 1], y[:, :, 0:D - 2], y[:, :, 2:D], ALU.add))
                steps.mark(v.tensor_scalar(lap_x[:, :, 0:1], y[:, :, 1:2], 2.0, None, ALU.mult))
                steps.do(v.tensor_scalar(lap_x[:, :, D - 1:D], y[:, :, D - 2:D - 1], 2.0, None, ALU.mult))
                steps.mark(v.tensor_tensor(d, d, y, ALU.mult))
                steps.do(v.scalar_tensor_tensor(out=lap_x, in0=y, scalar=-2.0, in1=lap_x, op0=ALU.mult, op1=ALU.add))
                steps.do(v.scalar_tensor_tensor(out=d, in0=lap_x, scalar=zb[0], in1=d, op0=ALU.mult, op1=ALU.add))
                dve.wait_ge(lap_made, (b + 1) * SB)
                v.scalar_tensor_tensor(out=d.rearrange("p (k i) d -> p k (i d)", i=2), in0=psum[:, 4 * b:4 * b + 4],
                                       scalar=zb[1], in1=d.rearrange("p (k i) d -> p k (i d)", i=2),
                                       op0=ALU.mult, op1=ALU.add).then_inc(du_ready, 1)
            dve.wait_ge(b1_turned, 1)
            steps.do(v.tensor_copy(b1_cols.rearrange("p e f -> p (e f)"), banks[3][:, 0:E * FC]))
            dve.wait_ge(routed, NBLK)
            lg, first, second, cand, both, pos = (rt[:, i] for i in range(6))
            iota = const("experts").unsqueeze(1).broadcast_to([P, NBLK, E])

            def wide(a):
                return a.unsqueeze(2).broadcast_to([P, NBLK, E])

            gap, _, m1, m2, w_1, w_2, idx, den = (route[:, i] for i in range(8))
            tt(lg, banks[2][:, 0:NBLK * E].rearrange("p (i e) -> p i e", e=E),
               br_row[:].unsqueeze(1).broadcast_to([P, NBLK, E]), ALU.add)
            for m, hot in ((m1, first), (m2, second)):
                steps.do(v.reduce_max(m, lg, AX_X))
                tt(cand, lg, wide(m), ALU.is_equal)
                stt(cand, iota, float(-E), cand, ALU.add, ALU.mult)
                steps.do(v.tensor_reduce(idx, cand, AX_X, ALU.min))
                ts(idx, idx, float(E), ALU.add)
                tt(hot, iota, wide(idx), ALU.is_equal)
                if hot is first:
                    stt(lg, first, -3.0e38, lg, ALU.mult, ALU.add)
            tt(gap, m2, m1, ALU.subtract)
            dve.sem_inc(gap_ready, 1)
            steps.mark(v.tensor_tensor(both, first, second, ALU.add))
            steps.wait()
            dve.sem_inc(chosen_ready, 1)
            dve.wait_ge(gap_exp, 1)
            ts(den, route[:, 1], 1.0, ALU.add)
            steps.do(v.reciprocal(w_1, den))
            tt(w_2, route[:, 1], w_1, ALU.mult)
            dve.wait_ge(ranked, 2)
            total = banks[5][:, 0:NBLK * E].rearrange("p (i e) -> p i e", e=E)
            steps.do(v.memset(cand[:, 0], 0.0))
            for i in range(1, NBLK):
                tt(cand[:, i], cand[:, i - 1], total[:, i - 1], ALU.add)
            tt(ex[:, 0], cand[:, NBLK - 1], total[:, NBLK - 1], ALU.add)
            ts(ex[:, 0], ex[:, 0], float(P - 1), ALU.add, 1.0 / P, ALU.mult)
            floor(ex[:, 1], ex[:, 0], ex_i[:], ex[:, 2])
            steps.do(v.tensor_copy(ex[:, 3], ex[:, 1]))
            for e in range(1, E):
                tt(ex[:, 3, e:e + 1], ex[:, 3, e - 1:e], ex[:, 3, e:e + 1], ALU.add)
            tt(ex[:, 4], ex[:, 3], ex[:, 1], ALU.subtract)
            ts(ex[:, 4], ex[:, 4], float(P), ALU.mult)
            tt(pos, banks[4][:, 0:NBLK * E].rearrange("p (i e) -> p i e", e=E), cand, ALU.add)
            tt(pos, pos, ex[:, 4].unsqueeze(1).broadcast_to([P, NBLK, E]), ALU.add)
            for k, hot in enumerate((first, second)):
                tt(cand, hot, pos, ALU.mult)
                steps.do(v.tensor_reduce(idx, cand, AX_X, ALU.add))
                steps.do(v.tensor_copy(slot_index[:, k], idx))
            te = te_f[:]
            tt(te, const("tiles").unsqueeze(2).broadcast_to([P, SLOT_TILES, E]),
               ex[:, 3].unsqueeze(1).broadcast_to([P, SLOT_TILES, E]), ALU.is_ge)
            steps.do(v.tensor_reduce(te_s[:], te, AX_X, ALU.add))
            ts(te_s[:], te_s[:], float(E - 1), ALU.min)
            steps.do(v.tensor_copy(tile_expert[:], te_s[:]))
            dve.sem_inc(slots_ready, 1)
            dve.wait_ge(experts_in, 16 * (2 * E + 1))

            def x_out(t):
                dve.wait_ge(x_turned, t + 2)
                v.tensor_copy(x_t, banks[2][:, 0:D].rearrange("p (c q) -> p c q", c=DC)).then_inc(x_t_ready, 1)

            def h_out(t):
                dve.wait_ge(h_made, t + 1)
                v.tensor_copy(h_tile.rearrange("p (a q) -> p a q", a=2), psum[:, 0:2]).then_inc(h_ready, 1)

            def y_out(t):
                dve.wait_ge(y_made, t + 1)
                dve.wait_ge(y_stored, t * 16 + 16)
                e = dve.value_load(tile_expert[0:1, bass.ds(t, 1)], min_val=0, max_val=E - 1)
                v.tensor_tensor(y_tile, banks[5][:, 0:D], b2_rows[:, bass.ds(e, 1)].squeeze(1),
                                ALU.add).then_inc(y_ready, 1)

            x_out(0)
            h_out(0)
            x_out(1)
            with dve.Fori(1, SLOT_TILES - 1) as t:
                h_out(t)
                x_out(t + 1)
                y_out(t - 1)
            h_out(SLOT_TILES - 1)
            y_out(SLOT_TILES - 2)
            y_out(SLOT_TILES - 1)
            for i in range(NBLK):
                dve.wait_ge(gathered[i], 32)
                steps.do(v.scalar_tensor_tensor(out=x1[:, i], in0=y_back[:, i, 0], scalar=route[:, 4, i:i + 1],
                                                in1=x1[:, i], op0=ALU.mult, op1=ALU.add))
                v.scalar_tensor_tensor(out=x1[:, i], in0=y_back[:, i, 1], scalar=route[:, 5, i:i + 1],
                                       in1=x1[:, i], op0=ALU.mult, op1=ALU.add).then_inc(summed, 1)



_INS = ['x', 'fside_Bx2_0', 'condB_angle', 'condB_zX', 'condB_zY', 'condB_zR', 'L0_attn_WQ', 'L0_attn_bQ', 'L0_attn_WK',
        'L0_attn_bK', 'L0_attn_WV', 'L0_attn_bV', 'L0_attn_WO', 'L0_attn_bO', 'L0_ffn_W_router', 'L0_ffn_b_router',
        'L0_ffn_W1', 'L0_ffn_b1', 'L0_ffn_W2', 'L0_ffn_b2']


def kernel(**inputs):
    import concourse.bacc as bacc
    from concourse.bass_utils import run_bass_kernel_spmd

    nc = bacc.Bacc("TRN2", target_bir_lowering=False, num_devices=1)
    arrays, args = {}, []
    for name in _INS:
        a = np.ascontiguousarray(inputs[name])
        arrays[name] = a
        args.append(nc.dram_tensor(name, a.shape, mybir.dt.from_np(a.dtype), kind="ExternalInput").ap())
    arrays["constants"] = constants()
    args.append(nc.dram_tensor("constants", arrays["constants"].shape, F32, kind="ExternalInput").ap())
    args.append(nc.dram_tensor("result", (NB, S, D), F32, kind="ExternalOutput").ap())
    build(nc, *args)
    r = run_bass_kernel_spmd(nc, [arrays], core_ids=[0])
    return r.results[0]["result"]
```

```python
from contextlib import ExitStack

import concourse.bass as bass
import numpy as np
from concourse import mybir

ALU = mybir.AluOpType
ACT = mybir.ActivationFunctionType
AX_X = mybir.AxisListType.X
F32 = mybir.dt.float32
BF16 = mybir.dt.bfloat16
I32 = mybir.dt.int32
U32 = mybir.dt.uint32

P = 128
NB, S, D = 2, 1024, 256
H, DH = 16, 16
E, FF = 8, 1024
SB = S // P
NBLK = NB * SB
DC = D // P
FC = FF // P

SHEAR = 192
J = D + 2 * SHEAR
JB = J // P
R = 8
R_LOW = 3
X_LOW = 36
XW = 336
MSHIFT = 32
PAD_Y = R
PAD_X = X_LOW + MSHIFT
PADW = 400
PADH = S + 2 * PAD_Y
BAND = (R - 1) * PADW + XW
XBLOCKS = [(0, P), (P, P), (2 * P, XW - 2 * P)]
KX = (D - 1) / S
KY = (S - 1) / D
NTAP = 9

SLOT_TILES = 2 * NB * S // P + E - 1
NSLOT = SLOT_TILES * P

HG = 4
NG = H // HG
PRODUCTS = [(0, 0), (0, 1), (0, 2), (1, 0), (1, 1), (2, 0)]
KROWS = DH * len(PRODUCTS)
CHUNKS = HG * 12
KEY_BLOCKS = [0, 4, 5, 6, 7, 1, 2, 3]
CHUNKS_AFTER = ([2] * 8 + [2, 2, 2, 1] * SB)[:26] + [0] * (SB * HG - 26)
TURN_UNIT = 26
STACK_IN = 16 * 2 * len(PRODUCTS)
N_WEIGHTS = 3 + 2 + 1 + 2 + 1 + 6
PROJ_BATCH = 8 + SB
PROJECTION_WORDS = NB * S // P * H * (DH + 1) + 2 * S + 3 * S
ARENA = 37632

NEG = -1.0e30

CONST_PARTS = [("sheared", JB), ("row", SB), ("identity", P), ("mask_qk", P), ("mask_kq", P), ("before", P),
               ("lap_mid", P), ("lap_first", P), ("lap_last", P), ("lap_prev", P), ("lap_next", P),
               ("experts", E), ("tiles", SLOT_TILES), ("column", D), ("ones", P)]
CONST_AT, CONST_W = {}, 0
for _name, _width in CONST_PARTS:
    CONST_AT[_name] = (CONST_W, _width)
    CONST_W += _width


def constants():
    p = np.arange(P)
    eye = np.eye(P)
    second = np.eye(P, k=1) + np.eye(P, k=-1) - 2 * eye
    first, last = second.copy(), second.copy()
    first[1, 0] = 2
    last[P - 2, P - 1] = 2
    prev, nxt = np.zeros((P, P)), np.zeros((P, P))
    prev[P - 1, 0] = nxt[0, P - 1] = 1
    part = {
        "sheared": p[:, None] + P * np.arange(JB)[None, :] - D // 2 - SHEAR,
        "row": p[:, None] + P * np.arange(SB)[None, :] - S // 2,
        "identity": eye,
        "mask_qk": np.where(p[None, :] > p[:, None], NEG, 0),
        "mask_kq": np.where(p[None, :] < p[:, None], NEG, 0),
        "before": p[:, None] < p[None, :],
        "lap_mid": second, "lap_first": first, "lap_last": last, "lap_prev": prev, "lap_next": nxt,
        "experts": np.broadcast_to(np.arange(E), (P, E)),
        "tiles": np.broadcast_to(np.arange(SLOT_TILES), (P, SLOT_TILES)),
        "column": np.broadcast_to(np.arange(D) - D // 2, (P, D)),
        "ones": np.ones((P, P)),
    }
    return np.concatenate([np.asarray(part[n], np.float32) for n, _ in CONST_PARTS], axis=1)


class Steps:

    def __init__(self, eng, sem, base=0, hold=None):
        self.eng, self.sem, self.base, self.n = eng, sem, base, 0
        self.hold = hold or eng.wait_ge

    def mark(self, ins):
        ins.then_inc(self.sem, 1)
        self.n += 1

    def wait(self):
        self.hold(self.sem, self.base + self.n)

    def do(self, ins):
        self.mark(ins)
        self.wait()


def build(nc, x, shift, angle, zx, zy, zr, wq, bq, wk, bk, wv, bv, wo, bo, wr, br, w1, b1, w2, b2, consts, out):
    ctx = ExitStack()
    with ctx:
        def sb(name, shape, dt=F32):
            return ctx.enter_context(nc.sbuf_tensor(name, shape, dt))

        def sem(name):
            return ctx.enter_context(nc.semaphore(name))

        def dram(name, shape, dt=F32):
            return nc.dram_tensor(name, shape, dt, kind="Internal").ap()

        padded = dram("padded", [NB * PADH * PADW])
        table = [dram(f"table{b}", [XW * R * J]) for b in range(NB)]
        fracs = dram("fracs", [NB * J * 2])
        qk_parts = dram("qk_parts", [2, 3, NB * D, S], BF16)
        pairs_x = dram("pairs_x", [NSLOT, D])
        pairs_y = dram("pairs_y", [NSLOT, D])
        padded_v = padded.rearrange("(b y x) -> b y x", b=NB, y=PADH)
        table_v = [t.rearrange("(x r j) -> x r j", x=XW, r=R) for t in table]

        cst = sb("cst", [P, CONST_W])

        def const(name):
            at, width = CONST_AT[name]
            return cst[:, at:at + width]

        ident = const("identity")
        zeros = sb("zeros", [P, SB * (PADW - D - PAD_X)])
        ang = sb("ang", [P, NB])
        shf = sb("shf", [P, NB, 2])
        prm = sb("prm", [P, 40, NB])
        col_f = sb("col_f", [P, NB, JB, 2])
        band_index = sb("band_index", [P, NB * JB], I32)
        tap_index = sb("tap_index", [P, NBLK], I32)
        frac_index = sb("frac_index", [P, NBLK], I32)
        row_bias = sb("row_bias", [P, NBLK, 4])
        row_par = sb("row_par", [P, NBLK, 4])
        steep = sb("steep", [P, NBLK], I32)
        tmp = sb("tmp", [P, 12, 16])
        tmp_i = sb("tmp_i", [P, 16], I32)
        band_col = sb("band_col", [P, 2], I32)
        tap_col = sb("tap_col", [P, 2], I32)
        frac_col = sb("frac_col", [P, 2], I32)
        xwT = sb("xwT", [P, DC, NB * S])
        x1 = sb("x1", [P, NBLK, D])
        wqkv = sb("wqkv", [P, 3, DC, D])
        bqk = sb("bqk", [P, 2, DC])
        bv_rows = sb("bv_rows", [P, D])
        wo_rows = sb("wo_rows", [DH + 1, D])
        ident_b = sb("ident_b", [P, P], BF16)
        mask_qk = sb("mask_qk", [P, P], BF16)
        mask_kq = sb("mask_kq", [P, P], BF16)
        z_cols = sb("z_cols", [P, 4, NB])
        wr_cols = sb("wr_cols", [P, DC, E])
        br_row = sb("br_row", [P, E])
        b1_rows = sb("b1_rows", [E * FC, P])
        b1_cols_t = sb("b1_cols", [P, E * FC])
        b1_cols = b1_cols_t[:].rearrange("p (e f) -> p e f", e=E)
        route = sb("route", [P, 8, NBLK])
        rt = sb("rt", [P, 6, NBLK, E])
        chosen = rt[:, 4].rearrange("p i e -> p (i e)")
        ex = sb("ex", [P, 5, E])
        ex_i = sb("ex_i", [P, E], I32)
        slot_index = sb("slot_index", [P, 2, NBLK], I32)
        te_f = sb("te_f", [P, SLOT_TILES, E])
        te_s = sb("te_s", [P, SLOT_TILES])
        tile_expert = sb("tile_expert", [P, SLOT_TILES], I32)
        du_t = [sb(f"du_t{u}", [P, DC, P])[:] for u in range(2)]
        arena = sb("arena", [P, ARENA])

        def region(first=0):
            at = [first]

            def tile(shape, dt=F32):
                n = int(np.prod(shape))
                words = n if dt != BF16 else (n + 1) // 2
                flat = arena[:, at[0]:at[0] + words]
                at[0] += words
                assert at[0] <= ARENA, at[0]
                if dt != F32:
                    flat = flat.bitcast(dt)
                names = [f"a{i}" for i in range(len(shape))]
                if len(shape) == 1:
                    return flat
                return flat.rearrange(f"p ({' '.join(names)}) -> p {' '.join(names)}",
                                      **{n_: k for n_, k in zip(names, shape)})
            return tile

        tile = region()
        band = [tile([BAND]) for u in range(2)]
        strip = [tile([3, R, P]) for u in range(2)]
        taps = [tile([3, 3, D]) for u in range(2)]
        frac = [tile([D, 2]) for u in range(2)]
        hats = [tile([2, 4, D]) for u in range(2)]
        warped = [tile([D]) for u in range(2)]
        slow = tile([5, D])
        slow_taps = tile([3, 3, D])
        slow_frac = tile([D, 2])
        slow_i = tile([D], I32)
        slow_par = tile([8])
        slow_col = tile([1], I32)
        slow_run = tile([PADW + 2])
        tile = region(ARENA - PROJECTION_WORDS)
        v_all = tile([NB, SB, H, DH + 1])
        proj = tile([S])
        resid = tile([S])
        parts = [tile([3, S], BF16) for u in range(2)]
        tile = region()
        stacks = tile([NG, 2, HG, S], BF16)
        probs = [[tile([S]) for h in range(HG)] for u in range(2)]
        v_group = tile([SB, HG, 32])
        max_parts = tile([2, HG * SB])
        neg_max = tile([HG * SB])
        neg_rows = tile([P])
        neg_parts = tile([3, P], BF16)
        o_group = tile([S])
        normed = tile([4 * HG, DH + 1])
        inverse = tile([4 * HG])
        head_sum = tile([4, DH + 1])
        z = tile([NB, SB, DH + 1])
        z_t = tile([S])

        tile = region()
        w1_all = tile([E, DC, FF])
        w2_all = tile([E, FC, D])
        b2_rows = tile([E, D])
        x_tile = tile([D])
        x_t = tile([DC, P])
        h_tile = tile([FF])
        hidden_t = tile([FC, P])
        y_tile = tile([D])
        y_back = region()([NBLK, 2, D])
        lap_x = arena[:, ARENA - SB * D:].rearrange("p (i d) -> p i d", d=D)
        du = xwT[:].rearrange("p c s -> p (c s)").rearrange("p (i d) -> p i d", d=D)

        psum = ctx.enter_context(nc.psum_tensor("psum", [P, 8, 512], F32))
        banks = [psum[:, i] for i in range(8)]

        consts_in = sem("consts_in")
        zeros_set = sem("zeros_set")
        padded_done = sem("padded_done")
        dve_steps = sem("dve_steps")
        fracs_done = sem("fracs_done")
        index_ready = sem("index_ready")
        pool_steps = sem("pool_steps")
        pool_held = sem("pool_held")
        band_landed = [sem(f"band_landed{u}") for u in range(2)]
        strips_turned = sem("strips_turned")
        strip_act = sem("strip_act")
        strip_dve = sem("strip_dve")
        strip_stored = [sem(f"strip_stored{u}") for u in range(2)]
        taps_landed = [sem(f"taps_landed{u}") for u in range(2)]
        hats_ready = sem("hats_ready")
        act_hats = sem("act_hats")
        warp_dve = sem("warp_dve")
        warp_mixed = sem("warp_mixed")
        fast_steps = [sem(f"fast_steps{b}") for b in range(NB)]
        slow_steps = [sem(f"slow_steps{b}") for b in range(NB)]
        slow_landed = [[sem(f"slow_landed{b}{u}") for u in range(2)] for b in range(NB)]
        warp_turned = sem("warp_turned")
        xwT_done = sem("xwT_done")
        weights_in = sem("weights_in")
        masks_set = sem("masks_set")
        projected = sem("projected")
        proj_read = sem("proj_read")
        split_act = sem("split_act")
        split_dve = sem("split_dve")
        parts_ready = sem("parts_ready")
        parts_stored = [sem(f"parts_stored{u}") for u in range(2)]
        stack_in = sem("stack_in")
        v_ready = sem("v_ready")
        v_group_ready = sem("v_group_ready")
        scored = sem("scored")
        exp_done = sem("exp_done")
        pv_done = sem("pv_done")
        max_scored = sem("max_scored")
        max_read = sem("max_read")
        max_steps = sem("max_steps")
        neg_ready = sem("neg_ready")
        neg_parted = sem("neg_parted")
        neg_in = sem("neg_in")
        o_read = sem("o_read")
        z_turned = sem("z_turned")
        o_normed = sem("o_normed")
        attended = sem("attended")
        x1_ready = sem("x1_ready")
        norm_steps = sem("norm_steps")
        v_cleared = sem("v_cleared")
        pairs_cleared = sem("pairs_cleared")
        experts_in = sem("experts_in")
        lap_made = sem("lap_made")
        du_ready = sem("du_ready")
        b1_turned = sem("b1_turned")
        du_turned = sem("du_turned")
        du_t_ready = sem("du_t_ready")
        routed = sem("routed")
        gap_ready = sem("gap_ready")
        gap_exp = sem("gap_exp")
        chosen_ready = sem("chosen_ready")
        ranked = sem("ranked")
        slots_ready = sem("slots_ready")
        scattered = sem("scattered")
        x_in = sem("x_in")
        x_turned = sem("x_turned")
        x_t_ready = sem("x_t_ready")
        h_made = sem("h_made")
        h_ready = sem("h_ready")
        h_turned = sem("h_turned")
        hidden_ready = sem("hidden_ready")
        y_made = sem("y_made")
        y_ready = sem("y_ready")
        y_stored = sem("y_stored")
        gathered = [sem(f"gathered{i}") for i in range(NBLK)]
        summed = sem("summed")
        all_out = sem("all_out")

        block = ctx.enter_context(nc.Block())

        def warp_stages(eng):
            def strip_stage(b, q, n):
                return "strip", b, q, n, n % 2, n // 2

            with eng.Fori(0, JB // 2) as it:
                for i in range(2):
                    yield "strip", 0, it * 2 + i, it * 2 + i, i, it
            for q in range(JB // 2 * 2, JB):
                yield strip_stage(0, q, q)
            with eng.Fori(0, SB // 4) as it:
                for i in range(2):
                    yield "taps", 0, it * 2 + i
                    yield "strip", 1, it * 2 + i, it * 2 + (JB + i), (JB + i) % 2, it + (JB + i) // 2
            for q in range(SB // 2, JB):
                yield strip_stage(1, q, JB + q)
            yield "project", 0
            with eng.Fori(SB // 2, SB) as it:
                yield "taps", 1, it
            yield "project", 1

        def side_plan(last, chunks, project):
            plan = [[] for _ in range(SB * HG)]
            i = 0
            for unit in range(SB * HG):
                for _ in range(CHUNKS_AFTER[unit] if chunks else 0):
                    plan[unit].append(("chunk", i))
                    i += 1
            if last:
                plan[2 * HG - 1] += [("sum", 0), ("sum", 1)]
            if project:
                plan[3 * HG - 1] += [("turn_z", 0), ("turn_z", 1)]
                plan[4 * HG - 1] += [("attend", k) for k in range(4)]
            if chunks:
                plan[TURN_UNIT] += [("turn_max", 0)]
            return plan

        def side_uses(last, chunks, project):
            return sum(map(len, side_plan(last, chunks, project)))

        def chunk_of(i):
            h, r = i // 12, i % 12
            qb, kc = (r, 0) if r < 4 else (4 + (r - 4) // 2, (r - 4) % 2)
            return h, qb, kc, min((qb + 1) * P - kc * 512, 512)

        FIRST_USES = CHUNKS + 1
        USES = side_uses(True, True, False)

        def attention_groups(eng):
            m = FIRST_USES
            yield 0, 0, 1, m, side_plan(False, True, False), True
            m += side_uses(False, True, False)
            with eng.Fori(1, NG - 1) as g:
                yield g, g, g + 1, (g - 1) * USES + m, side_plan(True, True, False), False
            m += USES * (NG - 2)
            yield NG - 1, NG - 1, 0, m, side_plan(True, True, False), False
            m += USES
            yield NG, 0, 1, m, side_plan(True, True, True), False
            m += side_uses(True, True, True)
            with eng.Fori(1, NG - 1) as g:
                yield g + NG, g, g + 1, (g - 1) * USES + m, side_plan(True, True, False), False
            m += USES * (NG - 2)
            yield 2 * NG - 1, NG - 1, None, m, side_plan(True, False, False), False

        LAST_PLAN = ([("sum", 0), ("sum", 1), ("turn_z", 0), ("turn_z", 1)] + [("attend", k) for k in range(4)])

        def z_batch(n):
            return 0 if isinstance(n, int) and n <= NG or not isinstance(n, int) and n.max_val <= NG else 1

        LAST_USES = (FIRST_USES + side_uses(False, True, False) + USES * (2 * NG - 4) + USES
                     + side_uses(True, True, True) + side_uses(True, False, False))

        @block.sync
        def _(sp):
            def load_stack(n, g):
                if not isinstance(n, int) or n:
                    sp.wait_ge(stack_in, n * STACK_IN)
                for i, pair in enumerate(PRODUCTS):
                    for kind in range(2):
                        sp.dma_start(
                            stacks[i * DH:(i + 1) * DH, bass.ds(g, 1), kind].squeeze(1),
                            qk_parts[kind, pair[kind], bass.ds(n * (HG * DH), HG * DH)]
                            .rearrange("(h d) s -> d h s", h=HG)).then_inc(stack_in, 16)

            sp.dma_start(cst[:], consts).then_inc(consts_in, 16)
            sp.dma_start(ang[:], angle.unsqueeze(0).broadcast_to([P, NB])).then_inc(consts_in, 16)
            sp.dma_start(shf[:], shift.rearrange("b t -> (b t)").unsqueeze(0).broadcast_to([P, NB * 2])
                         .rearrange("p (b t) -> p b t", b=NB)).then_inc(consts_in, 16)
            for b in range(NB):
                sp.dma_start(padded_v[b, PAD_Y:PAD_Y + S, PAD_X:PAD_X + D], x[b]).then_inc(padded_done, 16)
            sp.wait_ge(zeros_set, 1)
            for b in range(NB):
                for y in (0, PAD_Y + S):
                    sp.dma_start(padded_v[b, y:y + PAD_Y].rearrange("y x -> (y x)").rearrange("(p n) -> p n", p=16),
                                 zeros[0:16, 0:PAD_Y * PADW // 16]).then_inc(padded_done, 16)
                for x0, w in ((0, PAD_X), (PAD_X + D, PADW - PAD_X - D)):
                    sp.dma_start(padded_v[b, PAD_Y:PAD_Y + S, x0:x0 + w].rearrange("(q p) x -> p q x", p=P),
                                 zeros[:, 0:SB * w].rearrange("p (q x) -> p q x", q=SB)).then_inc(padded_done, 16)
            sp.dma_start(pairs_x.rearrange("(p i) d -> p i d", p=P),
                         zeros[:, 0:D].unsqueeze(1).broadcast_to([P, SLOT_TILES, D])).then_inc(pairs_cleared, 16)
            sp.wait_ge(index_ready, 1)
            for b in range(NB):
                sp.dma_start(fracs[b * J * 2:(b + 1) * J * 2].rearrange("(n p t) -> p n t", p=P, t=2),
                             col_f[:, b]).then_inc(fracs_done, 16)
            for stage, b, *at in warp_stages(sp):
                if stage == "strip":
                    q, n, u, turn = at
                    sp.wait_ge(strip_act, n * 3 + 6)
                    sp.wait_ge(strip_dve, n * 3 + 6)
                    for k, (x0, w) in enumerate(XBLOCKS):
                        sp.dma_start(table_v[b][x0:x0 + w, :, bass.ds(q * P, P)],
                                     strip[u][0:w, k]).then_inc(strip_stored[u], 16)
                elif stage == "project":
                    for k in range(2 * DC):
                        kind, c = k // DC, k % DC
                        sp.wait_ge(parts_ready, b * 2 * DC + k + 1)
                        sp.dma_start(qk_parts[kind, :, b * D + c * P:b * D + (c + 1) * P].rearrange("t p s -> p t s"),
                                     parts[k % 2]).then_inc(parts_stored[k % 2], 16)
                    for u in range(2):
                        sp.wait_ge(parts_stored[u], 16 * DC * (b + 1))
                    if b == 0:
                        for u in range(2):
                            sp.wait_ge(strip_stored[u], 48 * (JB + 1))
                        for g in range(NG - 1):
                            load_stack(g, g)
            sp.wait_ge(xwT_done, NBLK + 2)
            load_stack(NG - 1, NG - 1)

            def store_neg(n, g):
                sp.wait_ge(neg_parted, n + 1)
                for i in range(3):
                    sp.dma_start(stacks[KROWS + i:KROWS + i + 1, bass.ds(g, 1), 0].rearrange("p g h s -> p (g h s)"),
                                 neg_parts[0:HG * SB, i]).then_inc(neg_in, 16)

            store_neg(0, 0)
            with sp.Fori(0, NG - 1) as g:
                store_neg(g + 1, g + 1)
                sp.wait_ge(pv_done, (g + 1) * SB + 2)
                load_stack(g + NG, g)
            store_neg(NG, 0)
            sp.wait_ge(pv_done, NG * SB + 2)
            load_stack(2 * NG - 1, NG - 1)
            with sp.Fori(1, NG) as g:
                store_neg(g + NG, g)

            sp.wait_ge(x1_ready, NBLK)
            for e in range(E):
                sp.dma_start(w1_all[:, e], w1[e].rearrange("(c p) f -> p c f", p=P)).then_inc(experts_in, 16)
                sp.dma_start(w2_all[:, e], w2[e].rearrange("(c p) d -> p c d", p=P)).then_inc(experts_in, 16)
            sp.dma_start(b2_rows, b2.rearrange("e d -> (e d)").unsqueeze(0).broadcast_to([P, E * D])
                         .rearrange("p (e d) -> p e d", e=E)).then_inc(experts_in, 16)

            def load_tile(t):
                sp.wait_ge(x_turned, t + 1)
                sp.dma_start(x_tile, pairs_x[bass.ds(t * P, P), :]).then_inc(x_in, 16)

            def store_tile(t):
                sp.wait_ge(y_ready, t + 2)
                sp.dma_start(pairs_y[bass.ds(t * P, P), :], y_tile).then_inc(y_stored, 16)

            sp.wait_ge(scattered, 16 * 2 * NBLK)
            for t in range(3):
                load_tile(t)
            with sp.Fori(1, SLOT_TILES - 2) as t:
                load_tile(t + 2)
                store_tile(t - 1)
            store_tile(SLOT_TILES - 3)
            store_tile(SLOT_TILES - 2)
            store_tile(SLOT_TILES - 1)
            for i in range(NBLK):
                sp.wait_ge(summed, i + 1)
                b, r = i // SB, i % SB
                sp.dma_start(out[b, r * P:(r + 1) * P], x1[:, i]).then_inc(all_out, 16)
            sp.wait_ge(all_out, 16 * NBLK)

        def pool_hold(semaphore, value):
            nc.gpsimd.wait_ge(semaphore, value)
            nc.gpsimd.sem_inc(pool_held, 1)

        SLOW_HEAD, SLOW_POINT = 32, 3
        SLOW_BLOCK = SLOW_HEAD + SLOW_POINT * D

        def steep_block(pool, b, blk, u, it):
            g = nc.gpsimd
            block_base = it * (2 * SLOW_BLOCK) + u * SLOW_BLOCK
            steps = Steps(pool, slow_steps[b], block_base, pool_hold)
            par = [slow_par[:, i:i + 1] for i in range(8)]
            us, vs, fl, ab, ix = (slow[:, i] for i in range(5))
            pool_hold(warp_mixed, blk + 1)
            steps.do(g.memset(slow_taps[:], 0.0))
            steps.do(g.tensor_copy(slow_par[:, 0:4], row_par[:, bass.ds(blk, 1)].squeeze(1)))
            steps.do(g.tensor_copy(slow_par[:, 4:8], row_bias[:, bass.ds(blk, 1)].squeeze(1)))
            steps.do(g.tensor_scalar(us, const("column"), par[0], par[2], ALU.mult, ALU.add))
            steps.do(g.tensor_scalar(us, us, -2.0, float(D + 2), ALU.max, ALU.min))
            steps.do(g.tensor_scalar(vs, const("column"), par[1], par[3], ALU.mult, ALU.add))
            steps.do(g.tensor_scalar(vs, vs, -2.0, float(S + 2), ALU.max, ALU.min))
            steps.do(g.memset(ix, float(b * PADH * PADW)))
            for ax, w, pad, width in ((0, us, PAD_X, 1), (1, vs, PAD_Y, PADW)):
                steps.do(g.tensor_copy(slow_i[:], w))
                steps.do(g.tensor_copy(fl, slow_i[:]))
                steps.do(g.tensor_tensor(ab, fl, w, ALU.subtract))
                steps.do(g.tensor_scalar(ab, ab, 0.0, None, ALU.is_gt))
                steps.do(g.tensor_tensor(fl, fl, ab, ALU.subtract))
                steps.do(g.tensor_tensor(w, w, fl, ALU.subtract))
                steps.do(g.tensor_scalar(w, w, par[4 + 2 * ax + 1], None, ALU.subtract))
                steps.do(g.tensor_scalar(slow_frac[:, :, ax], w, -1.0, None, ALU.add))
                steps.do(g.tensor_scalar(fl, fl, float(pad), None, ALU.add))
                steps.do(g.tensor_scalar(fl, fl, float(width), None, ALU.mult))
                steps.do(g.tensor_tensor(ix, ix, fl, ALU.add))
            steps.do(g.tensor_copy(slow_i[:], ix))
            steps.do(g.memset(slow_run[:, 0:2], 0.0))
            assert steps.n == SLOW_HEAD, steps.n
            with pool.Fori(0, D) as j:
                inner = Steps(pool, slow_steps[b], block_base + SLOW_HEAD + j * SLOW_POINT, pool_hold)
                inner.do(g.tensor_copy(slow_col[:], slow_i[:, bass.ds(j, 1)]))
                g.indirect_dma_start(slow_run[:], None, padded.unsqueeze(0),
                                     bass.IndirectOffsetOnAxis(ap=slow_col[:], axis=1)).then_inc(slow_landed[b][u], 16)
                pool_hold(slow_landed[b][u], it * (16 * D) + j * 16 + 16)
                for r in range(2):
                    inner.do(g.tensor_copy(slow_taps[:, 0:2, r, bass.ds(j, 1)],
                                           slow_run[:, r * PADW:r * PADW + 2].unsqueeze(2)))
            pool.dma_start(frac[u][:], slow_frac[:]).then_inc(taps_landed[u], 16)
            for d in range(3):
                for r in range(3):
                    pool.dma_start(taps[u][:, d, r], slow_taps[:, d, r]).then_inc(taps_landed[u], 16)
            pool_hold(taps_landed[u], (it + b * SB // 2) * 160 + 160)

        @block.gpsimd
        def _(pool):
            nc.gpsimd.memset(zeros[:], 0.0).then_inc(zeros_set, 1)
            nc.gpsimd.memset(v_all[:, :, :, :, DH:DH + 1], 1.0).then_inc(v_cleared, 1)
            pool.wait_ge(index_ready, 1)
            pool.wait_ge(padded_done, 16 * 5 * NB)
            for stage, b, *at in warp_stages(pool):
                if stage == "strip":
                    q, n, u, turn = at
                    steps = Steps(pool, pool_steps, n, pool_hold)
                    pool_hold(strips_turned, n * 6 + 6)
                    steps.do(nc.gpsimd.tensor_copy(band_col[:, u:u + 1], band_index[:, bass.ds(n, 1)]))
                    nc.gpsimd.indirect_dma_start(
                        band[u], None, padded.unsqueeze(0),
                        bass.IndirectOffsetOnAxis(ap=band_col[:, u:u + 1], axis=1)).then_inc(band_landed[u], 16)
                elif stage == "taps":
                    pair, = at
                    it = pair - b * SB // 2
                    for u in range(2):
                        strips = ((b + 1) * JB + 1 - u) // 2
                        pool.wait_ge(strip_stored[u], 48 * (strips + 1))
                    pool.wait_ge(fracs_done, 16 * NB)
                    beyond = pool.value_load(steep[0:1, b * SB:b * SB + 1], min_val=0, max_val=1)
                    with pool.If(beyond < 1):
                        steps = Steps(pool, fast_steps[b], it * 4, pool_hold)
                        for u in range(2):
                            blk = pair * 2 + u
                            pool_hold(warp_mixed, blk + 1)
                            steps.mark(nc.gpsimd.tensor_copy(tap_col[:, u:u + 1], tap_index[:, bass.ds(blk, 1)]))
                            steps.do(nc.gpsimd.tensor_copy(frac_col[:, u:u + 1], frac_index[:, bass.ds(blk, 1)]))
                            nc.gpsimd.indirect_dma_start(
                                frac[u].rearrange("p d t -> p (d t)"), None, fracs.unsqueeze(0),
                                bass.IndirectOffsetOnAxis(ap=frac_col[:, u:u + 1], axis=1)
                            ).then_inc(taps_landed[u], 16)
                            for d in range(3):
                                for r in range(3):
                                    nc.gpsimd.indirect_dma_start(
                                        taps[u][:, d, r], None, table[b].unsqueeze(0),
                                        bass.IndirectOffsetOnAxis(ap=tap_col[:, u:u + 1], axis=1),
                                        element_offset=(d * R + r) * J).then_inc(taps_landed[u], 16)
                    with pool.If(beyond > 0):
                        for u in range(2):
                            steep_block(pool, b, pair * 2 + u, u, it)

            pool.wait_ge(xwT_done, NBLK + 2)
            g_ = nc.gpsimd
            g_.memset(v_group, 0.0).then_inc(v_cleared, 1)
            pool.wait_ge(v_cleared, 2)
            g_.memset(stacks[KROWS:KROWS + 3, :, 1], 1.0).then_inc(v_cleared, 1)
            pool.wait_ge(v_cleared, 3)
            pool.wait_ge(v_ready, NB)
            for b in range(NB):
                with pool.Fori(0, NG) as g:
                    pool_hold(pv_done, (g + b * NG) * SB + 2)
                    g_.tensor_copy(v_group[:, :, :, 0:DH + 1],
                                   v_all[:, b, :, bass.ds(g * HG, HG)]).then_inc(v_group_ready, 1)

            pool.wait_ge(slots_ready, 1)
            pool.wait_ge(pairs_cleared, 16)
            for i in range(NBLK):
                for k in range(2):
                    g_.indirect_dma_start(pairs_x, bass.IndirectOffsetOnAxis(ap=slot_index[:, k, i:i + 1], axis=0),
                                          du[:, i], None).then_inc(scattered, 16)
            pool.wait_ge(y_stored, 16 * SLOT_TILES + 16)
            for i in range(NBLK):
                for k in range(2):
                    g_.indirect_dma_start(y_back[:, i, k], None, pairs_y,
                                          bass.IndirectOffsetOnAxis(ap=slot_index[:, k, i:i + 1], axis=0)
                                          ).then_inc(gathered[i], 16)

        @block.scalar
        def _(act):
            for i, w in enumerate((wq, wk, wv)):
                act.dma_start(wqkv[:, i], w.rearrange("(c p) n -> p c n", p=P)).then_inc(weights_in, 16)
            for i, w in enumerate((bq, bk)):
                act.dma_start(bqk[:, i], w.rearrange("(c p) -> p c", p=P),
                              allow_slow_non_contiguous=True).then_inc(weights_in, 16)
            act.dma_start(bv_rows[:], bv.unsqueeze(0).broadcast_to([P, D])).then_inc(weights_in, 16)
            for i, z in enumerate((zx, zy, zr)):
                act.dma_start(z_cols[:, i], z.unsqueeze(0).broadcast_to([P, NB])).then_inc(weights_in, 16)
            act.dma_start(wr_cols[:], wr.rearrange("(c p) e -> p c e", p=P)).then_inc(weights_in, 16)
            act.dma_start(br_row[:], br.unsqueeze(0).broadcast_to([P, E])).then_inc(weights_in, 16)
            act.dma_start(b1_rows[:], b1.rearrange("e (f p) -> (e f) p", p=P)).then_inc(weights_in, 16)
            act.dma_start(wo_rows[0:DH], wo).then_inc(weights_in, 16)
            act.dma_start(wo_rows[DH:DH + 1], bo.unsqueeze(0)).then_inc(weights_in, 16)
            act.dma_start(x1[:].rearrange("p (b i) d -> p b i d", b=NB),
                          x.rearrange("b (i p) d -> p b i d", p=P)).then_inc(weights_in, 16)
            for stage, b, *at in warp_stages(act):
                if stage == "strip":
                    q, n, u, turn = at
                    act.wait_ge(strip_stored[u], turn * 48 + 48)
                    for g in range(3):
                        k, half = g // 2, g % 2
                        w = XBLOCKS[k][1]
                        act.wait_ge(strips_turned, n * 6 + g + 13)
                        nc.scalar.activation(strip[u][0:w, k, 4 * half:4 * half + 4],
                                             banks[g][0:w, :].rearrange("p (r q) -> p r q", r=4),
                                             ACT.Copy).then_inc(strip_act, 1)
                elif stage == "taps":
                    pair, = at
                    steps = Steps(act, act_hats, pair * 4)
                    for u in range(2):
                        blk = pair * 2 + u
                        act.wait_ge(taps_landed[u], pair * 160 + 160)
                        act.wait_ge(warp_mixed, blk + 1)
                        for ax in range(2):
                            f = frac[u][:, :, ax]
                            up = row_bias[:, bass.ds(blk, 1), 2 * ax]
                            down = row_bias[:, bass.ds(blk, 1), 2 * ax + 1]
                            h = hats[u][:, ax]
                            nc.scalar.activation(h[:, 0], f, ACT.Relu, bias=up, scale=-1.0)
                            nc.scalar.activation(h[:, 2], f, ACT.Relu, bias=down)
                            steps.mark(nc.scalar.activation(h[:, 3], f, ACT.Abs, bias=down))
                        steps.wait()
                        for ax in range(2):
                            h = hats[u][:, ax]
                            ins = nc.scalar.activation(h[:, 1], h[:, 3], ACT.Relu, bias=const("ones")[:, 0:1],
                                                       scale=-1.0)
                        ins.then_inc(hats_ready, 1)
                    for u in range(2):
                        blk = pair * 2 + u
                        act.wait_ge(warp_turned, blk + 1)
                        nc.scalar.activation(xwT[:, :, bass.ds(blk * P, P)],
                                             banks[6 + u][:, 0:D].rearrange("p (c q) -> p c q", c=DC),
                                             ACT.Copy).then_inc(xwT_done, 1)
                else:
                    for k in range(2 * DC):
                        kind, c = k // DC, k % DC
                        n = b * 2 * DC + k
                        act.wait_ge(projected, b * PROJ_BATCH + 2 * k + 2)
                        if n:
                            act.wait_ge(parts_ready, n)
                        nc.scalar.activation(proj.rearrange("p (a q) -> p a q", a=2), psum[:, 2 * k:2 * k + 2],
                                             ACT.Identity, bias=bqk[:, kind, c:c + 1]).then_inc(proj_read, 1)

            def exponentials(n, j):
                kt = KEY_BLOCKS[j]
                act.wait_ge(pv_done, n * SB + (j + 1))
                for h in range(HG):
                    act.wait_ge(scored, n * (SB * HG) + (j * HG + h + 1))
                    slot = (j * HG + h) % 2
                    nc.scalar.activation(
                        probs[j % 2][h][:, kt * P:S],
                        psum[:, 2 * slot:2 * slot + 2].rearrange("p a q -> p (a q)")[:, kt * P:S],
                        ACT.Exp, scale=DH ** -0.5).then_inc(exp_done, 1)

            def copy_output(n):
                act.wait_ge(pv_done, n * SB + (SB + 2))
                act.wait_ge(o_normed, n + 1)
                nc.scalar.activation(o_group.rearrange("p (a q) -> p a q", a=2), psum[:, 4:6],
                                     ACT.Copy).then_inc(o_read, 1)

            for n, _, _, _, _, first in attention_groups(act):
                exponentials(n, 0)
                if not first:
                    copy_output(n - 1)
                for j in range(1, SB):
                    exponentials(n, j)
            copy_output(2 * NG - 1)

            for i in range(NBLK):
                act.wait_ge(du_turned, i + 1)
                if i >= 2:
                    act.wait_ge(routed, i - 1)
                nc.scalar.activation(du_t[i % 2], banks[i % 2][:, 0:D].rearrange("p (c q) -> p c q", c=DC),
                                     ACT.Copy).then_inc(du_t_ready, 1)
            act.wait_ge(gap_ready, 1)
            nc.scalar.activation(route[:, 1], route[:, 0], ACT.Exp).then_inc(gap_exp, 1)

            def hidden(t):
                act.wait_ge(h_turned, t + 1)
                e = act.value_load(tile_expert[0:1, bass.ds(t, 1)], min_val=0, max_val=E - 1)
                for f in range(FC):
                    ins = nc.scalar.activation(hidden_t[:, f], banks[3 + f // 4][:, (f % 4) * P:(f % 4 + 1) * P],
                                               ACT.Relu, bias=b1_cols[:, bass.ds(e, 1), f])
                ins.then_inc(hidden_ready, 1)

            act.wait_ge(slots_ready, 1)
            with act.Fori(0, SLOT_TILES) as t:
                hidden(t)

        @block.tensor
        def _(pe):
            pe.wait_ge(consts_in, 48)
            t_ = nc.tensor
            for stage, b, *at in warp_stages(pe):
                if stage == "strip":
                    q, n, u, turn = at
                    pe.wait_ge(band_landed[u], turn * 16 + 16)
                    for g in range(6):
                        k, half = g // 2, g % 2
                        x0, w = XBLOCKS[k]
                        if g < 3:
                            pe.wait_ge(strip_act, n * 3 + g + 1)
                        else:
                            pe.wait_ge(strip_dve, n * 3 + g - 2)
                        for r in range(4):
                            at_ = (4 * half + r) * PADW + x0
                            ins = t_.transpose(banks[g][0:w, r * P:(r + 1) * P], band[u][:, at_:at_ + w], ident)
                        ins.then_inc(strips_turned, 1)
                elif stage == "taps":
                    for u in range(2):
                        blk = at[0] * 2 + u
                        pe.wait_ge(warp_mixed, blk + 3)
                        pe.wait_ge(xwT_done, blk + 1)
                        for c in range(DC):
                            ins = t_.transpose(banks[6 + u][:, c * P:(c + 1) * P], warped[u][:, c * P:(c + 1) * P],
                                               ident)
                        ins.then_inc(warp_turned, 1)
                else:
                    pe.wait_ge(weights_in, 16 * N_WEIGHTS)
                    pe.wait_ge(xwT_done, SB * (b + 1) + 2)
                    pe.wait_ge(strip_act, 3 * 2 * JB + 3)
                    pe.wait_ge(strip_dve, 3 * 2 * JB + 3)
                    for k in range(2 * DC):
                        kind, c = k // DC, k % DC
                        for half in range(2):
                            for dc in range(DC):
                                ins = t_.matmul(banks[2 * k + half], wqkv[:, kind, dc, c * P:(c + 1) * P],
                                                xwT[:, dc, b * S + half * 512:b * S + (half + 1) * 512],
                                                start=dc == 0, stop=dc == DC - 1)
                            ins.then_inc(projected, 1)
                    for kt in range(SB):
                        pe.wait_ge(proj_read, b * 2 * DC + kt // 4 + 1)
                        for dc in range(DC):
                            ins = t_.matmul(banks[kt // 2][:, (kt % 2) * D:(kt % 2 + 1) * D],
                                            xwT[:, dc, b * S + kt * P:b * S + (kt + 1) * P], wqkv[:, 2, dc],
                                            start=dc == 0, stop=dc == DC - 1)
                        ins.then_inc(projected, 1)
                    pe.wait_ge(proj_read, (b + 1) * 2 * DC)
                    pe.wait_ge(v_ready, b + 1)

            pe.wait_ge(masks_set, 3)
            pe.wait_ge(v_cleared, 3)

            def side(n, g, first_use, k, what, i):
                bank = banks[6 + k % 2]
                pe.wait_ge(max_read, first_use + k + (1 if k else 2))
                if what == "chunk":
                    h, qb, kc, keys = chunk_of(i)
                    diagonal = qb // 4 == kc
                    ins = t_.matmul(bank[:, 0:keys],
                                    stacks[0:KROWS, bass.ds(g, 1), 0, h, qb * P:(qb + 1) * P].squeeze(1),
                                    stacks[0:KROWS, bass.ds(g, 1), 1, h, kc * 512:kc * 512 + keys].squeeze(1),
                                    start=True, stop=not diagonal)
                    if diagonal:
                        at_ = qb * P - kc * 512
                        ins = t_.matmul(bank[:, at_:at_ + P], ident_b[:], mask_qk[:], start=False, stop=True)
                elif what == "turn_max":
                    pe.wait_ge(neg_ready, n + 1)
                    ins = t_.transpose(bank[0:HG * SB, 0:P], neg_max, ident)
                elif what == "sum":
                    pe.wait_ge(o_read, n + 1)
                    for k in range(4):
                        at_ = (4 * i + k) * P
                        ins = t_.transpose(bank[:, k * P:(k + 1) * P], o_group[:, at_:at_ + P], ident)
                elif what == "turn_z":
                    pe.wait_ge(o_normed, n + 1)
                    for k in range(4):
                        ins = t_.transpose(bank[0:DH + 1, k * P:(k + 1) * P], z[:, z_batch(n), 4 * i + k], ident)
                elif what == "attend":
                    pe.wait_ge(z_turned, z_batch(n) + 1)
                    for k in range(2):
                        at_ = (2 * i + k) * P
                        ins = t_.matmul(bank[:, k * D:(k + 1) * D], z_t[0:DH + 1, at_:at_ + P], wo_rows[:],
                                        start=True, stop=True)
                ins.then_inc(max_scored, 1)

            def weighted(n, j, half):
                kt = KEY_BLOCKS[j]
                if half:
                    pe.wait_ge(exp_done, n * (SB * HG) + (HG * (j + 1) + 2))
                    if j == 0:
                        pe.wait_ge(o_read, n + 1)
                        pe.wait_ge(v_group_ready, n + 1)
                q0 = max(kt * P, half * 512)
                for h in range(HG):
                    ins = t_.matmul(banks[4 + half][32 * h:32 * h + 32, q0 - half * 512:512],
                                    v_group[:, kt, h], probs[j % 2][h][:, q0:(half + 1) * 512],
                                    start=j == 0, stop=j == SB - 1)
                if half == 0 or kt >= SB // 2:
                    ins.then_inc(pv_done, 1)

            def score(n, g, j, h):
                kt = KEY_BLOCKS[j]
                unit = j * HG + h
                pe.wait_ge(exp_done, n * (SB * HG) + (unit + 1))
                for half in range(kt // 4, 2):
                    q0 = max(kt * P, half * 512)
                    bank = banks[2 * (unit % 2) + half]
                    diagonal = q0 == kt * P
                    ins = t_.matmul(bank[:, q0 - half * 512:512],
                                    stacks[0:KROWS + 3, bass.ds(g, 1), 1, h, kt * P:(kt + 1) * P].squeeze(1),
                                    stacks[0:KROWS + 3, bass.ds(g, 1), 0, h, q0:(half + 1) * 512].squeeze(1),
                                    start=True, stop=not diagonal)
                    if diagonal:
                        at_ = kt * P - half * 512
                        ins = t_.matmul(bank[:, at_:at_ + P], ident_b[:], mask_kq[:], start=False, stop=True)
                ins.then_inc(scored, 1)

            pe.wait_ge(stack_in, STACK_IN)
            for i in range(CHUNKS):
                side(-1, 0, 0, i, "chunk", i)
            side(0, 0, 0, CHUNKS, "turn_max", 0)
            for n, g, following, uses, plan, first in attention_groups(pe):
                pe.wait_ge(neg_in, n * 48 + 48)
                if following is not None:
                    pe.wait_ge(stack_in, n * STACK_IN + 2 * STACK_IN)
                use = 0
                for j in range(SB):
                    for h in range(HG):
                        score(n, g, j, h)
                        if h % 2 and (j or not first):
                            half = 1 - h // 2
                            if half or KEY_BLOCKS[j - 1] < SB // 2:
                                weighted(n if j else n - 1, (j - 1) % SB, half)
                        for what, i in plan[j * HG + h]:
                            side(n + 1 if what == "turn_max" else n, following, uses, use, what, i)
                            use += 1
            for half in (1, 0):
                weighted(2 * NG - 1, SB - 1, half)
            for use, (what, i) in enumerate(LAST_PLAN):
                side(2 * NG, None, LAST_USES, use, what, i)

            for b in range(NB):
                pe.wait_ge(x1_ready, NBLK)
                for i in range(SB):
                    bank = banks[4 * b + i // 2][:, (i % 2) * D:(i % 2 + 1) * D]
                    terms = [(("lap_first" if i == 0 else "lap_last" if i == SB - 1 else "lap_mid"), i)]
                    terms += [("lap_prev", i - 1)] if i else []
                    terms += [("lap_next", i + 1)] if i < SB - 1 else []
                    for k, (name, j) in enumerate(terms):
                        ins = t_.matmul(bank, const(name), x1[:, b * SB + j], start=k == 0, stop=k == len(terms) - 1)
                    ins.then_inc(lap_made, 1)
            pe.wait_ge(du_ready, NB)
            t_.transpose(banks[3][:, 0:E * FC], b1_rows[:], const("identity")[0:E * FC, 0:E * FC]).then_inc(b1_turned, 1)
            for i in range(NBLK + 1):
                if i < NBLK:
                    if i >= 2:
                        pe.wait_ge(du_t_ready, i - 1)
                    for c in range(DC):
                        ins = t_.transpose(banks[i % 2][:, c * P:(c + 1) * P], du[:, i, c * P:(c + 1) * P], ident)
                    ins.then_inc(du_turned, 1)
                if i:
                    pe.wait_ge(du_t_ready, i)
                    for c in range(DC):
                        ins = t_.matmul(banks[2][:, (i - 1) * E:i * E], du_t[(i - 1) % 2][:, c], wr_cols[:, c],
                                        start=c == 0, stop=c == DC - 1)
                    ins.then_inc(routed, 1)
            pe.wait_ge(chosen_ready, 1)
            t_.matmul(banks[4][:, 0:NBLK * E], const("before"), chosen, start=True, stop=True).then_inc(ranked, 1)
            t_.matmul(banks[5][:, 0:NBLK * E], const("ones"), chosen, start=True, stop=True).then_inc(ranked, 1)
            def turn_x(t):
                pe.wait_ge(x_in, t * 16 + 16)
                for c in range(DC):
                    ins = t_.transpose(banks[2][:, c * P:(c + 1) * P], x_tile[:, c * P:(c + 1) * P], ident)
                ins.then_inc(x_turned, 1)

            def first_product(t, e):
                pe.wait_ge(x_t_ready, t + 1)
                pe.wait_ge(h_ready, t + 1)
                for half in range(2):
                    for c in range(DC):
                        ins = t_.matmul(banks[half], x_t[:, c],
                                        w1_all[:, bass.ds(e, 1), c, half * 512:(half + 1) * 512].squeeze(1),
                                        start=c == 0, stop=c == DC - 1)
                ins.then_inc(h_made, 1)

            def turn_h(t):
                pe.wait_ge(h_ready, t + 2)
                for f in range(FC):
                    ins = t_.transpose(banks[3 + f // 4][:, (f % 4) * P:(f % 4 + 1) * P], h_tile[:, f * P:(f + 1) * P],
                                       ident)
                ins.then_inc(h_turned, 1)

            def second_product(t, e):
                pe.wait_ge(hidden_ready, t + 1)
                pe.wait_ge(y_ready, t + 1)
                for f in range(FC):
                    ins = t_.matmul(banks[5][:, 0:D], hidden_t[:, f], w2_all[:, bass.ds(e, 1), f].squeeze(1),
                                    start=f == 0, stop=f == FC - 1)
                ins.then_inc(y_made, 1)

            def expert_of(t):
                return pe.value_load(tile_expert[0:1, bass.ds(t, 1)], min_val=0, max_val=E - 1)

            pe.wait_ge(slots_ready, 1)
            pe.wait_ge(experts_in, 16 * (2 * E + 1))
            turn_x(0)
            first_product(0, expert_of(0))
            turn_x(1)
            turn_h(0)
            with pe.Fori(1, SLOT_TILES - 1) as t:
                first_product(t, expert_of(t))
                expert_before = expert_of(t - 1)
                turn_x(t + 1)
                second_product(t - 1, expert_before)
                turn_h(t)
            last = SLOT_TILES - 1
            first_product(last, expert_of(last))
            second_product(last - 1, expert_of(last - 1))
            turn_h(last)
            second_product(last, expert_of(last))

        @block.vector
        def _(dve):
            v = nc.vector
            steps = Steps(dve, dve_steps)
            dve.wait_ge(consts_in, 48)
            dve.wait_ge(zeros_set, 1)

            def ts(o, a, s1, op0, s2=None, op1=None):
                if op1 is None:
                    steps.do(v.tensor_scalar(o, a, s1, None, op0))
                else:
                    steps.do(v.tensor_scalar(o, a, s1, s2, op0, op1))

            def tt(o, a, b_, op):
                steps.do(v.tensor_tensor(o, a, b_, op))

            def stt(o, a, s, b_, op0, op1):
                steps.do(v.scalar_tensor_tensor(out=o, in0=a, scalar=s, in1=b_, op0=op0, op1=op1))

            def floor(o, a, whole, above):
                steps.do(v.tensor_copy(whole, a))
                steps.do(v.tensor_copy(o, whole))
                tt(above, o, a, ALU.is_gt)
                tt(o, o, above, ALU.subtract)

            (KQ, RA, Z2, SN, CS, ODD, K4, T0, T1, SIN, COS, TAN, CA, CB, CP, CQ, CU, CV, STEEP, T2) = range(20)
            pr = [prm[:, i] for i in range(40)]
            wi2 = tmp_i[:, 0:NB]
            ts(pr[T0], ang[:], 2 / np.pi, ALU.mult, 0.5, ALU.add)
            floor(pr[KQ], pr[T0], wi2, pr[T1])
            stt(pr[RA], pr[KQ], -1.5703125, ang[:], ALU.mult, ALU.add)
            stt(pr[RA], pr[KQ], -4.837512969970703125e-4, pr[RA], ALU.mult, ALU.add)
            stt(pr[RA], pr[KQ], -7.549789948768648e-8, pr[RA], ALU.mult, ALU.add)
            tt(pr[Z2], pr[RA], pr[RA], ALU.mult)
            ts(pr[T0], pr[Z2], -1.9515295891e-4, ALU.mult, 8.3321608736e-3, ALU.add)
            tt(pr[T0], pr[T0], pr[Z2], ALU.mult)
            ts(pr[T0], pr[T0], -1.6666654611e-1, ALU.add)
            tt(pr[T0], pr[T0], pr[Z2], ALU.mult)
            stt(pr[SN], pr[T0], 1.0, pr[RA], ALU.add, ALU.mult)
            ts(pr[T0], pr[Z2], 2.443315711809948e-5, ALU.mult, -1.388731625493765e-3, ALU.add)
            tt(pr[T0], pr[T0], pr[Z2], ALU.mult)
            ts(pr[T0], pr[T0], 4.166664568298827e-2, ALU.add)
            tt(pr[T0], pr[T0], pr[Z2], ALU.mult)
            ts(pr[T0], pr[T0], -0.5, ALU.add)
            tt(pr[T0], pr[T0], pr[Z2], ALU.mult)
            ts(pr[CS], pr[T0], 1.0, ALU.add)
            ts(pr[T0], pr[KQ], 0.25, ALU.mult)
            floor(pr[K4], pr[T0], wi2, pr[T1])
            stt(pr[K4], pr[K4], -4.0, pr[KQ], ALU.mult, ALU.add)
            ts(pr[T0], pr[K4], 0.5, ALU.mult)
            floor(pr[ODD], pr[T0], wi2, pr[T1])
            stt(pr[ODD], pr[ODD], -2.0, pr[K4], ALU.mult, ALU.add)
            tt(pr[T0], pr[CS], pr[SN], ALU.subtract)
            tt(pr[T0], pr[T0], pr[ODD], ALU.mult)
            tt(pr[SIN], pr[SN], pr[T0], ALU.add)
            tt(pr[COS], pr[CS], pr[T0], ALU.subtract)
            ts(pr[T0], pr[K4], 2.0, ALU.is_ge, -2.0, ALU.mult)
            stt(pr[SIN], pr[T0], 1.0, pr[SIN], ALU.add, ALU.mult)
            ts(pr[T0], pr[K4], 1.0, ALU.is_ge)
            ts(pr[T1], pr[K4], 3.0, ALU.is_lt)
            tt(pr[T0], pr[T0], pr[T1], ALU.mult)
            ts(pr[T0], pr[T0], -2.0, ALU.mult, 1.0, ALU.add)
            tt(pr[COS], pr[COS], pr[T0], ALU.mult)
            most = SHEAR / (S // 2)
            stt(pr[T0], pr[SIN], -1.0, pr[SIN], ALU.mult, ALU.max)
            stt(pr[T1], pr[COS], -1.0, pr[COS], ALU.mult, ALU.max)
            ts(pr[T1], pr[T1], -most, ALU.mult)
            tt(pr[STEEP], pr[T0], pr[T1], ALU.add)
            ts(pr[STEEP], pr[STEEP], 0.0, ALU.is_gt)
            ts(pr[T2], pr[T1], -1.0 / most, ALU.mult, 0.5, ALU.max)
            steps.do(v.reciprocal(pr[T2], pr[T2]))
            ts(pr[T1], pr[COS], 0.0, ALU.is_ge)
            ts(pr[T1], pr[T1], 2.0, ALU.mult, -1.0, ALU.add)
            tt(pr[T2], pr[T2], pr[T1], ALU.mult)
            tt(pr[TAN], pr[SIN], pr[T2], ALU.mult)
            ts(pr[CA], pr[SIN], KX, ALU.mult)
            ts(pr[CB], pr[COS], KX, ALU.mult)
            ts(pr[CP], pr[COS], KY, ALU.mult)
            ts(pr[CQ], pr[SIN], -KY, ALU.mult)
            for o, t, k, mid in ((CU, 1, KX, (D - 1) / 2), (CV, 0, KY, (S - 1) / 2)):
                ts(pr[o], shf[:, :, t], k, ALU.mult, mid, ALU.add)
                ts(pr[o], pr[o], -1.0e5, ALU.max, 1.0e5, ALU.min)

            def scalar(i, b):
                return prm[:, i, b:b + 1]

            t = [tmp[:, i] for i in range(12)]
            for b in range(NB):
                m, nn, ab, w5 = t[0][:, 0:JB], t[1][:, 0:JB], t[2][:, 0:JB], tmp_i[:, 0:JB]
                uj, vj = t[3][:, 0:JB], t[4][:, 0:JB]
                ts(uj, const("sheared"), scalar(CA, b), ALU.mult)
                floor(m, uj, w5, ab)
                tt(col_f[:, b, :, 0], uj, m, ALU.subtract)
                ts(vj, const("sheared"), scalar(CP, b), ALU.mult, scalar(CV, b), ALU.add)
                floor(nn, vj, w5, ab)
                tt(col_f[:, b, :, 1], vj, nn, ALU.subtract)
                ts(m, m, float(-MSHIFT), ALU.max, float(MSHIFT - 1), ALU.min)
                ts(nn, nn, float(-R_LOW), ALU.add, float(-R), ALU.max)
                ts(nn, nn, float(S), ALU.min, float(PAD_Y), ALU.add)
                stt(nn, nn, float(PADW), m, ALU.mult, ALU.add)
                ts(nn, nn, float(PAD_X - X_LOW + b * PADH * PADW), ALU.add)
                steps.do(v.tensor_copy(band_index[:, b * JB:(b + 1) * JB], nn))
            for b in range(NB):
                row = const("row")
                sh, w0, fw, e0, fe, ab, cu, cv = (t[i][:, 0:SB] for i in range(8))
                w8 = tmp_i[:, 0:SB]
                bs = slice(b * SB, (b + 1) * SB)
                ts(cu, row, scalar(TAN, b), ALU.mult, 0.5, ALU.add)
                floor(sh, cu, w8, ab)
                ts(sh, sh, float(-SHEAR), ALU.max, float(SHEAR), ALU.min)
                ts(cu, row, scalar(CB, b), ALU.mult, scalar(CU, b), ALU.add)
                stt(fw, sh, scalar(CA, b), cu, ALU.mult, ALU.add)
                floor(w0, fw, w8, ab)
                tt(fw, fw, w0, ALU.subtract)
                ts(cv, row, scalar(CQ, b), ALU.mult)
                stt(fe, sh, scalar(CP, b), cv, ALU.mult, ALU.add)
                floor(e0, fe, w8, ab)
                tt(fe, fe, e0, ALU.subtract)
                for i, f in ((0, fw), (2, fe)):
                    ts(row_bias[:, bs, i], f, -1.0, ALU.mult, 1.0, ALU.add)
                    ts(row_bias[:, bs, i + 1], f, -1.0, ALU.add)
                ts(w0, w0, float(-X_LOW), ALU.max, float(XW - X_LOW - 3), ALU.min)
                ts(e0, e0, float(-R_LOW), ALU.max, float(R - R_LOW - 3), ALU.min)
                ts(w0, w0, float(X_LOW), ALU.add)
                stt(e0, w0, float(R), e0, ALU.mult, ALU.add)
                ts(e0, e0, float(R_LOW), ALU.add, float(J), ALU.mult)
                tt(e0, e0, sh, ALU.subtract)
                ts(e0, e0, float(SHEAR), ALU.add)
                steps.do(v.tensor_copy(tap_index[:, bs], e0))
                ts(sh, sh, -2.0, ALU.mult, float(2 * (b * J + SHEAR)), ALU.add)
                steps.do(v.tensor_copy(frac_index[:, bs], sh))
                ts(row_par[:, bs, 0], row, 0.0, ALU.mult, scalar(CA, b), ALU.add)
                ts(row_par[:, bs, 1], row, 0.0, ALU.mult, scalar(CP, b), ALU.add)
                steps.do(v.tensor_copy(row_par[:, bs, 2], cu))
                ts(row_par[:, bs, 3], cv, scalar(CV, b), ALU.add)
                ts(t[8][:, 0:SB], row, 0.0, ALU.mult, scalar(STEEP, b), ALU.add)
                steps.do(v.tensor_copy(steep[:, bs], t[8][:, 0:SB]))
            dve.sem_inc(strips_turned, 12)
            dve.sem_inc(index_ready, 1)
            dve.sem_inc(strip_act, 3)
            dve.sem_inc(strip_dve, 3)
            dve.sem_inc(strip_stored[0], 48)
            dve.sem_inc(strip_stored[1], 48)
            dve.sem_inc(warp_mixed, 2)
            dve.sem_inc(exp_done, 2)
            dve.sem_inc(pv_done, 2)
            dve.sem_inc(max_read, 2)
            dve.sem_inc(o_read, 1)
            dve.sem_inc(x_turned, 1)
            dve.sem_inc(h_ready, 1)
            dve.sem_inc(y_ready, 1)
            dve.sem_inc(y_stored, 16)
            dve.sem_inc(o_normed, 1)
            for o, name in ((ident_b, "identity"), (mask_qk, "mask_qk"), (mask_kq, "mask_kq")):
                v.tensor_copy(o[:], const(name)).then_inc(masks_set, 1)
            dve.sem_inc(xwT_done, 2)
            for stage, b, *at in warp_stages(dve):
                if stage == "strip":
                    q, n, u, turn = at
                    dve.wait_ge(strip_stored[u], turn * 48 + 48)
                    for g in range(3, 6):
                        k, half = g // 2, g % 2
                        w = XBLOCKS[k][1]
                        dve.wait_ge(strips_turned, n * 6 + g + 13)
                        v.tensor_copy(strip[u][0:w, k, 4 * half:4 * half + 4],
                                      banks[g][0:w, :].rearrange("p (r q) -> p r q", r=4)).then_inc(strip_dve, 1)
                elif stage == "taps":
                    pair, = at
                    st = Steps(dve, warp_dve, pair * 14)
                    for u in range(2):
                        blk = pair * 2 + u
                        dve.wait_ge(taps_landed[u], pair * 160 + 160)
                        dve.wait_ge(hats_ready, blk + 1)
                        for d in range(3):
                            hat = hats[u][:, 0, d].unsqueeze(1).broadcast_to([P, 3, D])
                            st.mark(v.tensor_tensor(taps[u][:, d], taps[u][:, d], hat, ALU.mult))
                        st.wait()
                        for d in (1, 2):
                            st.do(v.tensor_tensor(taps[u][:, 0], taps[u][:, 0], taps[u][:, d], ALU.add))
                        st.do(v.tensor_tensor(taps[u][:, 0], taps[u][:, 0], hats[u][:, 1, 0:3], ALU.mult))
                        st.do(v.tensor_tensor(taps[u][:, 0, 0], taps[u][:, 0, 0], taps[u][:, 0, 1], ALU.add))
                        dve.wait_ge(xwT_done, blk + 1)
                        v.tensor_tensor(warped[u], taps[u][:, 0, 0], taps[u][:, 0, 2], ALU.add).then_inc(warp_mixed, 1)
                else:
                    for k in range(2 * DC):
                        n = b * 2 * DC + k
                        dve.wait_ge(proj_read, n + 1)
                        if n >= 2:
                            dve.wait_ge(parts_stored[k % 2], 16 * (n // 2))
                        pt = parts[k % 2]
                        steps.do(v.tensor_copy(pt[:, 0], proj))
                        steps.do(v.tensor_tensor(resid, proj, pt[:, 0], ALU.subtract))
                        steps.do(v.tensor_copy(pt[:, 1], resid))
                        v.tensor_tensor(pt[:, 2], resid, pt[:, 1], ALU.subtract).then_inc(parts_ready, 1)
                    dve.wait_ge(v_cleared, 1)
                    dve.wait_ge(weights_in, 16 * N_WEIGHTS)
                    for k in range(4):
                        dve.wait_ge(projected, b * PROJ_BATCH + 8 + 2 * (k + 1))
                        steps.mark(v.tensor_tensor(v_all[:, b, 2 * k:2 * k + 2, :, 0:DH],
                                                   banks[k].rearrange("p (t h d) -> p t h d", t=2, h=H),
                                                   bv_rows[:].rearrange("p (h d) -> p h d", h=H).unsqueeze(1)
                                                   .broadcast_to([P, 2, H, DH]), ALU.add))
                    steps.wait()
                    dve.sem_inc(v_ready, 1)

            dve.wait_ge(xwT_done, NBLK + 2)
            steps.mark(v.memset(z, 0.0))
            steps.do(v.memset(max_parts, -3.0e38))

            def side(n, use, slot, what, i):
                bank = banks[6 + slot]
                dve.wait_ge(max_scored, use + 1)
                if what == "chunk":
                    h, qb, kc, keys = chunk_of(i)
                    v.reduce_max(max_parts[:, kc, h * SB + qb:h * SB + qb + 1], bank[:, 0:keys],
                                 AX_X).then_inc(max_read, 1)
                    if i == CHUNKS - 1:
                        st = Steps(dve, max_steps, (n + 1) * 4)
                        dve.wait_ge(max_read, use + 3)
                        st.do(v.tensor_tensor(neg_max, max_parts[:, 0], max_parts[:, 1], ALU.max))
                        v.tensor_scalar(neg_max, neg_max, -1.0, None, ALU.mult).then_inc(neg_ready, 1)
                elif what == "turn_max":
                    st = Steps(dve, max_steps, n * 4 + 1)
                    nr, parts_ = neg_rows[0:HG * SB], neg_parts[0:HG * SB]
                    v.tensor_copy(nr, bank[0:HG * SB, 0:P]).then_inc(max_read, 1)
                    dve.wait_ge(max_read, use + 3)
                    if not isinstance(n, int) or n:
                        dve.wait_ge(neg_in, n * 48)
                    st.do(v.tensor_copy(parts_[:, 0], nr))
                    st.do(v.tensor_tensor(nr, nr, parts_[:, 0], ALU.subtract))
                    st.do(v.tensor_copy(parts_[:, 1], nr))
                    v.tensor_tensor(parts_[:, 2], nr, parts_[:, 1], ALU.subtract).then_inc(neg_parted, 1)
                elif what == "sum":
                    st = Steps(dve, norm_steps, (n - 1) * 5 + 3 * i)
                    o = bank.rearrange("p (k c) -> p k c", c=32)
                    st.do(v.reciprocal(inverse, o[:, :, DH]))
                    v.tensor_tensor(normed, o[:, :, 0:DH + 1], inverse.unsqueeze(2).broadcast_to([P, 4 * HG, DH + 1]),
                                    ALU.mult).then_inc(max_read, 1)
                    dve.wait_ge(max_read, use + 3)
                    st.do(v.tensor_reduce(head_sum, normed.rearrange("p (k h) d -> p k d h", h=HG), AX_X, ALU.add))
                    zb = z[:, z_batch(n), 4 * i:4 * i + 4]
                    ins = v.tensor_tensor(zb, zb, head_sum, ALU.add)
                    if i:
                        ins.then_inc(o_normed, 1)
                    else:
                        st.do(ins)
                elif what == "turn_z":
                    v.tensor_copy(z_t[0:DH + 1, i * 512:(i + 1) * 512], bank[0:DH + 1, :]).then_inc(max_read, 1)
                    if i:
                        dve.wait_ge(max_read, use + 3)
                        dve.sem_inc(z_turned, 1)
                elif what == "attend":
                    rows = x1[:, z_batch(n) * SB + 2 * i:z_batch(n) * SB + 2 * i + 2]
                    v.tensor_tensor(rows, rows, bank.rearrange("p (i d) -> p i d", i=2), ALU.add).then_inc(max_read, 1)
                    if i == 3:
                        dve.wait_ge(max_read, use + 3)
                        dve.sem_inc(x1_ready, SB)

            for i in range(CHUNKS):
                side(-1, i, i % 2, "chunk", i)
            side(0, CHUNKS, 0, "turn_max", 0)
            for n, g, following, uses, plan, first in attention_groups(dve):
                use = 0
                for unit in plan:
                    for what, i in unit:
                        side(n + 1 if what == "turn_max" else n, uses + use, use % 2, what, i)
                        use += 1
            for use, (what, i) in enumerate(LAST_PLAN):
                side(2 * NG, LAST_USES + use, use % 2, what, i)

            for b in range(NB):
                y = x1[:, b * SB:(b + 1) * SB]
                d = du[:, b * SB:(b + 1) * SB]
                zb = [z_cols[:, i, b:b + 1] for i in range(4)]
                if b == 0:
                    dve.wait_ge(x1_ready, NBLK)
                steps.do(v.tensor_scalar(z_cols[:, 3, b:b + 1], zb[2], -1.0, None, ALU.mult))
                steps.mark(v.tensor_scalar(d, y, zb[3], zb[2], ALU.mult, ALU.add))
                steps.mark(v.tensor_tensor(lap_x[:, :, 1:D - 1], y[:, :, 0:D - 2], y[:, :, 2:D], ALU.add))
                steps.mark(v.tensor_scalar(lap_x[:, :, 0:1], y[:, :, 1:2], 2.0, None, ALU.mult))
                steps.do(v.tensor_scalar(lap_x[:, :, D - 1:D], y[:, :, D - 2:D - 1], 2.0, None, ALU.mult))
                steps.mark(v.tensor_tensor(d, d, y, ALU.mult))
                steps.do(v.scalar_tensor_tensor(out=lap_x, in0=y, scalar=-2.0, in1=lap_x, op0=ALU.mult, op1=ALU.add))
                steps.do(v.scalar_tensor_tensor(out=d, in0=lap_x, scalar=zb[0], in1=d, op0=ALU.mult, op1=ALU.add))
                dve.wait_ge(lap_made, (b + 1) * SB)
                v.scalar_tensor_tensor(out=d.rearrange("p (k i) d -> p k (i d)", i=2), in0=psum[:, 4 * b:4 * b + 4],
                                       scalar=zb[1], in1=d.rearrange("p (k i) d -> p k (i d)", i=2),
                                       op0=ALU.mult, op1=ALU.add).then_inc(du_ready, 1)
            dve.wait_ge(b1_turned, 1)
            steps.do(v.tensor_copy(b1_cols.rearrange("p e f -> p (e f)"), banks[3][:, 0:E * FC]))
            dve.wait_ge(routed, NBLK)
            lg, first, second, cand, both, pos = (rt[:, i] for i in range(6))
            iota = const("experts").unsqueeze(1).broadcast_to([P, NBLK, E])

            def wide(a):
                return a.unsqueeze(2).broadcast_to([P, NBLK, E])

            gap, _, m1, m2, w_1, w_2, idx, den = (route[:, i] for i in range(8))
            tt(lg, banks[2][:, 0:NBLK * E].rearrange("p (i e) -> p i e", e=E),
               br_row[:].unsqueeze(1).broadcast_to([P, NBLK, E]), ALU.add)
            for m, hot in ((m1, first), (m2, second)):
                steps.do(v.reduce_max(m, lg, AX_X))
                tt(cand, lg, wide(m), ALU.is_equal)
                stt(cand, iota, float(-E), cand, ALU.add, ALU.mult)
                steps.do(v.tensor_reduce(idx, cand, AX_X, ALU.min))
                ts(idx, idx, float(E), ALU.add)
                tt(hot, iota, wide(idx), ALU.is_equal)
                if hot is first:
                    stt(lg, first, -3.0e38, lg, ALU.mult, ALU.add)
            tt(gap, m2, m1, ALU.subtract)
            dve.sem_inc(gap_ready, 1)
            steps.mark(v.tensor_tensor(both, first, second, ALU.add))
            steps.wait()
            dve.sem_inc(chosen_ready, 1)
            dve.wait_ge(gap_exp, 1)
            ts(den, route[:, 1], 1.0, ALU.add)
            steps.do(v.reciprocal(w_1, den))
            tt(w_2, route[:, 1], w_1, ALU.mult)
            dve.wait_ge(ranked, 2)
            total = banks[5][:, 0:NBLK * E].rearrange("p (i e) -> p i e", e=E)
            steps.do(v.memset(cand[:, 0], 0.0))
            for i in range(1, NBLK):
                tt(cand[:, i], cand[:, i - 1], total[:, i - 1], ALU.add)
            tt(ex[:, 0], cand[:, NBLK - 1], total[:, NBLK - 1], ALU.add)
            ts(ex[:, 0], ex[:, 0], float(P - 1), ALU.add, 1.0 / P, ALU.mult)
            floor(ex[:, 1], ex[:, 0], ex_i[:], ex[:, 2])
            steps.do(v.tensor_copy(ex[:, 3], ex[:, 1]))
            for e in range(1, E):
                tt(ex[:, 3, e:e + 1], ex[:, 3, e - 1:e], ex[:, 3, e:e + 1], ALU.add)
            tt(ex[:, 4], ex[:, 3], ex[:, 1], ALU.subtract)
            ts(ex[:, 4], ex[:, 4], float(P), ALU.mult)
            tt(pos, banks[4][:, 0:NBLK * E].rearrange("p (i e) -> p i e", e=E), cand, ALU.add)
            tt(pos, pos, ex[:, 4].unsqueeze(1).broadcast_to([P, NBLK, E]), ALU.add)
            for k, hot in enumerate((first, second)):
                tt(cand, hot, pos, ALU.mult)
                steps.do(v.tensor_reduce(idx, cand, AX_X, ALU.add))
                steps.do(v.tensor_copy(slot_index[:, k], idx))
            te = te_f[:]
            tt(te, const("tiles").unsqueeze(2).broadcast_to([P, SLOT_TILES, E]),
               ex[:, 3].unsqueeze(1).broadcast_to([P, SLOT_TILES, E]), ALU.is_ge)
            steps.do(v.tensor_reduce(te_s[:], te, AX_X, ALU.add))
            ts(te_s[:], te_s[:], float(E - 1), ALU.min)
            steps.do(v.tensor_copy(tile_expert[:], te_s[:]))
            dve.sem_inc(slots_ready, 1)
            dve.wait_ge(experts_in, 16 * (2 * E + 1))

            def x_out(t):
                dve.wait_ge(x_turned, t + 2)
                v.tensor_copy(x_t, banks[2][:, 0:D].rearrange("p (c q) -> p c q", c=DC)).then_inc(x_t_ready, 1)

            def h_out(t):
                dve.wait_ge(h_made, t + 1)
                v.tensor_copy(h_tile.rearrange("p (a q) -> p a q", a=2), psum[:, 0:2]).then_inc(h_ready, 1)

            def y_out(t):
                dve.wait_ge(y_made, t + 1)
                dve.wait_ge(y_stored, t * 16 + 16)
                e = dve.value_load(tile_expert[0:1, bass.ds(t, 1)], min_val=0, max_val=E - 1)
                v.tensor_tensor(y_tile, banks[5][:, 0:D], b2_rows[:, bass.ds(e, 1)].squeeze(1),
                                ALU.add).then_inc(y_ready, 1)

            x_out(0)
            h_out(0)
            x_out(1)
            with dve.Fori(1, SLOT_TILES - 1) as t:
                h_out(t)
                x_out(t + 1)
                y_out(t - 1)
            h_out(SLOT_TILES - 1)
            y_out(SLOT_TILES - 2)
            y_out(SLOT_TILES - 1)
            for i in range(NBLK):
                dve.wait_ge(gathered[i], 32)
                steps.do(v.scalar_tensor_tensor(out=x1[:, i], in0=y_back[:, i, 0], scalar=route[:, 4, i:i + 1],
                                                in1=x1[:, i], op0=ALU.mult, op1=ALU.add))
                v.scalar_tensor_tensor(out=x1[:, i], in0=y_back[:, i, 1], scalar=route[:, 5, i:i + 1],
                                       in1=x1[:, i], op0=ALU.mult, op1=ALU.add).then_inc(summed, 1)



_INS = ['x', 'fside_Bx2_0', 'condB_angle', 'condB_zX', 'condB_zY', 'condB_zR', 'L0_attn_WQ', 'L0_attn_bQ', 'L0_attn_WK',
        'L0_attn_bK', 'L0_attn_WV', 'L0_attn_bV', 'L0_attn_WO', 'L0_attn_bO', 'L0_ffn_W_router', 'L0_ffn_b_router',
        'L0_ffn_W1', 'L0_ffn_b1', 'L0_ffn_W2', 'L0_ffn_b2']


def kernel(**inputs):
    import concourse.bacc as bacc
    from concourse.bass_utils import run_bass_kernel_spmd

    nc = bacc.Bacc("TRN2", target_bir_lowering=False, num_devices=1)
    arrays, args = {}, []
    for name in _INS:
        a = np.ascontiguousarray(inputs[name])
        arrays[name] = a
        args.append(nc.dram_tensor(name, a.shape, mybir.dt.from_np(a.dtype), kind="ExternalInput").ap())
    arrays["constants"] = constants()
    args.append(nc.dram_tensor("constants", arrays["constants"].shape, F32, kind="ExternalInput").ap())
    args.append(nc.dram_tensor("result", (NB, S, D), F32, kind="ExternalOutput").ap())
    build(nc, *args)
    r = run_bass_kernel_spmd(nc, [arrays], core_ids=[0])
    return r.results[0]["result"]
```

```python
from contextlib import ExitStack

import concourse.bass as bass
import numpy as np
from concourse import mybir

ALU = mybir.AluOpType
ACT = mybir.ActivationFunctionType
AX_X = mybir.AxisListType.X
F32 = mybir.dt.float32
BF16 = mybir.dt.bfloat16
I32 = mybir.dt.int32

P = 128
NB, S, D = 2, 1024, 256
H, DH = 16, 16
E, FF = 8, 1024
SB = S // P
NBLK = NB * SB
DC = D // P
FC = FF // P

SHEAR = 192
J = D + 2 * SHEAR
JB = J // P
R = 8
R_LOW = 3
X_LOW = 36
XW = 336
MSHIFT = 32
PAD_Y = R
PAD_X = X_LOW + MSHIFT
PADW = 400
PADH = S + 2 * PAD_Y
BAND = (R - 1) * PADW + XW
XBLOCKS = [(0, P), (P, P), (2 * P, XW - 2 * P)]
KX = (D - 1) / S
KY = (S - 1) / D

SLOT_TILES = 2 * NB * S // P + E - 1
REGION = NB * S

HG = 4
NG = H // HG
PRODUCTS = [(0, 0), (0, 1), (0, 2), (1, 0), (1, 1), (2, 0)]
KROWS = DH * len(PRODUCTS)
CHUNKS = HG * 12
KEY_BLOCKS = [0, 4, 5, 6, 7, 1, 2, 3]
CHUNKS_BEFORE = ([2] * 8 + [2, 2, 2, 1] * SB)[:26] + [0] * (SB * HG - 26)
TURN_UNIT = 26
STACK_IN = 16 * 2 * len(PRODUCTS)
N_WEIGHTS = 3 + 2 + 1 + 2 + 1 + 6
QK_CHUNKS = 2 * DC * S // 512
PART_SLOTS = 4
PROJ_BATCH = QK_CHUNKS + SB // 2
PROJECTION_WORDS = NB * S // P * H * (DH + 1) + 2 * 512 + PART_SLOTS * 3 * 256
ARENA = 37632

NEG = -1.0e30

CONST_PARTS = [("sheared", JB), ("row", SB), ("identity", P), ("mask_qk", P), ("mask_kq", P), ("before", P),
               ("lap_mid", P), ("lap_first", P), ("lap_last", P), ("lap_prev", P), ("lap_next", P),
               ("experts", E), ("tiles", SLOT_TILES), ("column", D), ("ones", P)]
CONST_AT, CONST_W = {}, 0
for _name, _width in CONST_PARTS:
    CONST_AT[_name] = (CONST_W, _width)
    CONST_W += _width


def constants():
    p = np.arange(P)
    eye = np.eye(P)
    second = np.eye(P, k=1) + np.eye(P, k=-1) - 2 * eye
    first, last = second.copy(), second.copy()
    first[1, 0] = 2
    last[P - 2, P - 1] = 2
    prev, nxt = np.zeros((P, P)), np.zeros((P, P))
    prev[P - 1, 0] = nxt[0, P - 1] = 1
    part = {
        "sheared": p[:, None] + P * np.arange(JB)[None, :] - D // 2 - SHEAR,
        "row": p[:, None] + P * np.arange(SB)[None, :] - S // 2,
        "identity": eye,
        "mask_qk": np.where(p[None, :] > p[:, None], NEG, 0),
        "mask_kq": np.where(p[None, :] < p[:, None], NEG, 0),
        "before": p[:, None] < p[None, :],
        "lap_mid": second, "lap_first": first, "lap_last": last, "lap_prev": prev, "lap_next": nxt,
        "experts": np.broadcast_to(np.arange(E), (P, E)),
        "tiles": np.broadcast_to(np.arange(SLOT_TILES), (P, SLOT_TILES)),
        "column": np.broadcast_to(np.arange(D) - D // 2, (P, D)),
        "ones": np.ones((P, P)),
    }
    return np.concatenate([np.asarray(part[n], np.float32) for n, _ in CONST_PARTS], axis=1)


class Steps:

    def __init__(self, eng, sem, base=0, hold=None):
        self.eng, self.sem, self.base, self.n = eng, sem, base, 0
        self.hold = hold or eng.wait_ge

    def mark(self, ins):
        ins.then_inc(self.sem, 1)
        self.n += 1

    def wait(self):
        self.hold(self.sem, self.base + self.n)

    def do(self, ins):
        self.mark(ins)
        self.wait()


def build(nc, x, shift, angle, zx, zy, zr, wq, bq, wk, bk, wv, bv, wo, bo, wr, br, w1, b1, w2, b2, consts, out):
    ctx = ExitStack()
    with ctx:
        def sb(name, shape, dt=F32):
            return ctx.enter_context(nc.sbuf_tensor(name, shape, dt))

        def sem(name):
            return ctx.enter_context(nc.semaphore(name))

        def dram(name, shape, dt=F32):
            return nc.dram_tensor(name, shape, dt, kind="Internal").ap()

        padded = dram("padded", [NB * PADH * PADW])
        table = [dram(f"table{b}", [XW * R * J]) for b in range(NB)]
        fracs = dram("fracs", [NB * J * 2])
        qk_parts = dram("qk_parts", [2, 3, NB * D, S], BF16)
        pairs_x = dram("pairs_x", [E * REGION, D])
        pair_home = dram("pair_home", [E * REGION, 1], I32)
        results = dram("results", [2 * NB * S + P, D])
        padded_v = padded.rearrange("(b y x) -> b y x", b=NB, y=PADH)
        table_v = [t.rearrange("(x r j) -> x r j", x=XW, r=R) for t in table]

        cst = sb("cst", [P, CONST_W])

        def const(name):
            at, width = CONST_AT[name]
            return cst[:, at:at + width]

        ident = const("identity")
        zeros = sb("zeros", [P, SB * (PADW - D - PAD_X)])
        ang = sb("ang", [P, NB])
        shf = sb("shf", [P, NB, 2])
        prm = sb("prm", [P, 40, NB])
        col_f = sb("col_f", [P, NB, JB, 2])
        band_index = sb("band_index", [P, NB * JB], I32)
        tap_index = sb("tap_index", [P, NBLK], I32)
        frac_index = sb("frac_index", [P, NBLK], I32)
        row_bias = sb("row_bias", [P, NBLK, 4])
        row_par = sb("row_par", [P, NBLK, 4])
        steep = sb("steep", [P, NBLK], I32)
        tmp = sb("tmp", [P, 12, 16])
        tmp_i = sb("tmp_i", [P, 16], I32)
        band_col = sb("band_col", [P, 2], I32)
        tap_col = sb("tap_col", [P, 2], I32)
        frac_col = sb("frac_col", [P, 2], I32)
        xwT = sb("xwT", [P, DC, NB * S])
        x1 = sb("x1", [P, NBLK, D])
        wqkv = sb("wqkv", [P, 3, DC, D])
        bqk = sb("bqk", [P, 2, DC])
        bv_rows = sb("bv_rows", [P, D])
        wo_rows = sb("wo_rows", [DH + 1, D])
        ident_b = sb("ident_b", [P, P], BF16)
        mask_qk = sb("mask_qk", [P, P], BF16)
        mask_kq = sb("mask_kq", [P, P], BF16)
        z_cols = sb("z_cols", [P, 5, NB])
        wr_cols = sb("wr_cols", [P, DC, E])
        br_row = sb("br_row", [P, E])
        b1_rows = sb("b1_rows", [E * FC, P])
        b1_cols_t = sb("b1_cols", [P, E * FC])
        b1_cols = b1_cols_t[:].rearrange("p (e f) -> p e f", e=E)
        route = sb("route", [P, 8, NBLK])
        rt = sb("rt", [P, 6, NBLK, E])
        chosen = rt[:, 4].rearrange("p i e -> p (i e)")
        ex = sb("ex", [P, 5, E])
        ex_i = sb("ex_i", [P, E], I32)
        x_index = sb("x_index", [P, 2, NBLK], I32)
        home = sb("home", [P, 2, NBLK], I32)
        home_col = sb("home_col", [P, 1], I32)
        te_row = sb("te_row", [P, SLOT_TILES])
        tile_row = sb("tile_row", [P, SLOT_TILES], I32)
        te_f = sb("te_f", [P, SLOT_TILES, E])
        no_home_f = te_f[:].rearrange("p t e -> p (t e)")[:, 0:P]
        no_home = te_f[:].rearrange("p t e -> p (t e)")[:, P:2 * P].bitcast(I32)
        te_s = sb("te_s", [P, SLOT_TILES])
        tile_expert = sb("tile_expert", [P, SLOT_TILES], I32)
        arena = sb("arena", [P, ARENA])

        def region(first=0):
            at = [first]

            def tile(shape, dt=F32):
                n = int(np.prod(shape))
                words = n if dt != BF16 else (n + 1) // 2
                flat = arena[:, at[0]:at[0] + words]
                at[0] += words
                assert at[0] <= ARENA, at[0]
                if dt != F32:
                    flat = flat.bitcast(dt)
                names = [f"a{i}" for i in range(len(shape))]
                if len(shape) == 1:
                    return flat
                return flat.rearrange(f"p ({' '.join(names)}) -> p {' '.join(names)}",
                                      **{n_: k for n_, k in zip(names, shape)})
            return tile

        tile = region()
        band = [tile([BAND]) for u in range(2)]
        strip = [tile([3, R, P]) for u in range(2)]
        taps = [tile([3, 3, D]) for u in range(2)]
        frac = [tile([D, 2]) for u in range(2)]
        hats = [tile([2, 4, D]) for u in range(2)]
        warped = [tile([D]) for u in range(2)]
        slow = tile([5, D])
        slow_taps = tile([3, 3, D])
        slow_frac = tile([D, 2])
        slow_i = tile([D], I32)
        slow_par = tile([8])
        slow_col = tile([1], I32)
        slow_run = tile([PADW + 2])
        tile = region(ARENA - PROJECTION_WORDS)
        v_all = tile([NB, SB, H, DH + 1])
        resid = [tile([512]) for u in range(2)]
        parts = [tile([3, 512], BF16) for u in range(PART_SLOTS)]
        tile = region()
        stacks = tile([NG, 2, HG, S], BF16)
        probs = [[tile([S]) for h in range(HG)] for u in range(2)]
        v_group = tile([SB, HG, 32])
        neg_max = tile([HG * SB])
        neg_rows = tile([P])
        neg_parts = tile([3, P], BF16)
        o_group = tile([S])
        normed = tile([4 * HG, DH + 1])
        inverse = tile([4 * HG])
        head_sum = tile([4, DH + 1])
        z = tile([NB, SB, DH + 1])
        z_t = tile([S])
        max_parts = region(ARENA - PROJECTION_WORDS - 2 * HG * SB)([2, HG * SB])
        du_t = [z_t[:, u * 512:(u + 1) * 512].rearrange("p (r c q) -> p r c q", r=2, c=DC) for u in range(2)]

        tile = region()
        w1_all = tile([E, DC, FF])
        x_tile = tile([D])
        x_t = tile([DC, P])
        h_tile = tile([FF])
        hidden_t = tile([FC, P])
        y_tile = tile([D])
        w2_all = tile([E, FC, D])
        b2_rows = tile([E, D])
        y_back = region()([NBLK, 2, D])
        lap_x = b2_rows
        du = xwT[:].rearrange("p c s -> p (c s)").rearrange("p (i d) -> p i d", d=D)

        psum = ctx.enter_context(nc.psum_tensor("psum", [P, 8, 512], F32))
        banks = [psum[:, i] for i in range(8)]

        consts_in = sem("consts_in")
        zeros_set = sem("zeros_set")
        padded_done = sem("padded_done")
        dve_steps = sem("dve_steps")
        fracs_done = sem("fracs_done")
        index_ready = sem("index_ready")
        pool_steps = sem("pool_steps")
        pool_held = sem("pool_held")
        band_landed = [sem(f"band_landed{u}") for u in range(2)]
        strips_turned = sem("strips_turned")
        strip_act = sem("strip_act")
        strip_dve = sem("strip_dve")
        strip_stored = [sem(f"strip_stored{u}") for u in range(2)]
        taps_landed = [sem(f"taps_landed{u}") for u in range(2)]
        hats_ready = sem("hats_ready")
        act_hats = sem("act_hats")
        warp_dve = sem("warp_dve")
        warp_mixed = sem("warp_mixed")
        fast_steps = [sem(f"fast_steps{b}") for b in range(NB)]
        slow_steps = [sem(f"slow_steps{b}") for b in range(NB)]
        slow_landed = [[sem(f"slow_landed{b}{u}") for u in range(2)] for b in range(NB)]
        warp_turned = sem("warp_turned")
        xwT_done = sem("xwT_done")
        weights_in = sem("weights_in")
        masks_set = sem("masks_set")
        projected = sem("projected")
        proj_read = sem("proj_read")
        first_parts = sem("first_parts")
        halved = sem("halved")
        parts_ready = sem("parts_ready")
        parts_stored = [sem(f"parts_stored{u}") for u in range(PART_SLOTS)]
        stack_in = sem("stack_in")
        v_ready = sem("v_ready")
        v_group_ready = sem("v_group_ready")
        scored = sem("scored")
        exp_done = sem("exp_done")
        pv_done = sem("pv_done")
        max_scored = sem("max_scored")
        max_read = sem("max_read")
        max_steps = sem("max_steps")
        neg_ready = sem("neg_ready")
        neg_parted = sem("neg_parted")
        neg_in = sem("neg_in")
        o_read = sem("o_read")
        z_turned = sem("z_turned")
        o_normed = sem("o_normed")
        x1_ready = sem("x1_ready")
        norm_steps = sem("norm_steps")
        v_cleared = sem("v_cleared")
        pairs_cleared = sem("pairs_cleared")
        experts_in = sem("experts_in")
        z_ready = sem("z_ready")
        scaled = sem("scaled")
        beside = sem("beside")
        side_steps = sem("side_steps")
        gap_ready = sem("gap_ready")
        gap_exp = sem("gap_exp")
        chosen_ready = sem("chosen_ready")
        slots_ready = sem("slots_ready")
        tiles_ready = sem("tiles_ready")
        homes_set = sem("homes_set")
        homes_out = sem("homes_out")
        home_in = sem("home_in")
        scattered = sem("scattered")
        x_in = sem("x_in")
        x_turned = sem("x_turned")
        x_t_ready = sem("x_t_ready")
        h_made = sem("h_made")
        h_ready = sem("h_ready")
        h_turned = sem("h_turned")
        hidden_ready = sem("hidden_ready")
        y_made = sem("y_made")
        y_ready = sem("y_ready")
        y_stored = sem("y_stored")
        back_in = [sem(f"back_in{i}") for i in range(NBLK // 2)]
        summed = sem("summed")
        all_out = sem("all_out")

        block = ctx.enter_context(nc.Block())

        def warp_stages(eng):
            def strip_stage(b, q, n):
                return "strip", b, q, n, n % 2, n // 2

            with eng.Fori(0, JB // 2) as it:
                for i in range(2):
                    yield "strip", 0, it * 2 + i, it * 2 + i, i, it
            yield "rows", 0
            yield strip_stage(0, JB - 1, JB - 1)
            yield "rows", 1
            yield strip_stage(1, 0, JB)
            with eng.Fori(0, SB // 4) as it:
                for i in range(2):
                    n = JB + 1 + i
                    yield "strip", 1, it * 2 + (i + 1), it * 2 + n, n % 2, it + n // 2
                    yield "taps", 0, it * 2 + i
            yield "project", 0
            with eng.Fori(SB // 2, SB) as it:
                yield "taps", 1, it
                yield "maxima", 0, it - SB // 2
            yield "project", 1

        ROUTE_PLAN = [("lap", 0), ("lap", 1), ("lap", 2), ("lap", 3), ("turn_du", 0), ("turn_du", 1), ("logits", 0),
                      ("turn_du", 2), ("logits", 1), ("turn_du", 3), ("logits", 2), ("logits", 3), ("rank", 0)]

        def side_plan(last, chunks, project):
            plan = [[] for _ in range(SB * HG)]
            i = 0
            for unit in range(SB * HG):
                for _ in range(CHUNKS_BEFORE[unit] if chunks else 0):
                    plan[unit].append(("chunk", i))
                    i += 1
            if last:
                plan[2 * HG - 1] += [("sum", 0), ("sum", 1)]
            if project:
                plan[3 * HG - 1] += [("turn_z", 0), ("turn_z", 1)]
                plan[4 * HG - 1] += [("attend", k) for k in range(4)]
            if chunks:
                plan[TURN_UNIT] += [("turn_max", 0)]
            return plan

        def uses_of(plan):
            return sum(map(len, plan))

        def chunk_of(r):
            qb, kc = (r, 0) if r < 4 else (4 + (r - 4) // 2, (r - 4) % 2)
            return qb, kc, min((qb + 1) * P - kc * 512, 512)

        PLAN = side_plan(True, True, False)
        FIRST_PLAN = side_plan(False, True, False)
        NEXT_PLAN = side_plan(True, True, True)
        END_PLAN = side_plan(True, False, False)
        for step, use in enumerate(ROUTE_PLAN):
            END_PLAN[min(9 + step, SB * HG - 1) if step < len(ROUTE_PLAN) - 1 else SB * HG - 1].append(use)

        def attention_groups(eng):
            m = CHUNKS + 1
            yield 0, 0, 1, m, FIRST_PLAN, True
            m += uses_of(FIRST_PLAN)
            with eng.Fori(1, NG - 1) as g:
                yield g, g, g + 1, (g - 1) * uses_of(PLAN) + m, PLAN, False
            m += uses_of(PLAN) * (NG - 2)
            yield NG - 1, NG - 1, 0, m, PLAN, False
            m += uses_of(PLAN)
            yield NG, 0, 1, m, NEXT_PLAN, False
            m += uses_of(NEXT_PLAN)
            with eng.Fori(1, NG - 1) as g:
                yield g + NG, g, g + 1, (g - 1) * uses_of(PLAN) + m, PLAN, False
            m += uses_of(PLAN) * (NG - 2)
            yield 2 * NG - 1, NG - 1, None, m, END_PLAN, False

        LAST_PLAN = ([("sum", 0), ("sum", 1), ("turn_z", 0), ("turn_z", 1)] + [("attend", k) for k in range(4)]
                     + [("turn_b1", 0)] + ROUTE_PLAN)
        LAST_BANKS = 8

        def side_bank(last, use):
            return (banks[(6 + use) % LAST_BANKS], LAST_BANKS) if last else (banks[6 + use % 2], 2)

        def uses_until(plan, what):
            return [use for unit in plan for use in unit].index(what) + 1

        def z_batch(n):
            return 0 if isinstance(n, int) and n <= NG or not isinstance(n, int) and n.max_val <= NG else 1

        LAST_USES = (CHUNKS + 1 + uses_of(FIRST_PLAN) + uses_of(PLAN) * 2 * (NG - 2) + uses_of(PLAN)
                     + uses_of(NEXT_PLAN) + uses_of(END_PLAN))

        @block.sync
        def _(sp):
            def store_parts(b):
                for j in range(QK_CHUNKS):
                    kind, c, half = j // (2 * DC), j // 2 % DC, j % 2
                    sp.wait_ge(parts_ready, b * QK_CHUNKS + j + 1)
                    u = j % PART_SLOTS
                    sp.dma_start(qk_parts[kind, :, b * D + c * P:b * D + (c + 1) * P, half * 512:(half + 1) * 512]
                                 .rearrange("t p s -> p t s"), parts[u]).then_inc(parts_stored[u], 16)
                for u in range(PART_SLOTS):
                    sp.wait_ge(parts_stored[u], 16 * QK_CHUNKS // PART_SLOTS * (b + 1))

            def load_stack(n, g):
                if not isinstance(n, int) or n:
                    sp.wait_ge(stack_in, n * STACK_IN)
                for i, pair in enumerate(PRODUCTS):
                    for kind in range(2):
                        sp.dma_start(
                            stacks[i * DH:(i + 1) * DH, bass.ds(g, 1), kind].squeeze(1),
                            qk_parts[kind, pair[kind], bass.ds(n * (HG * DH), HG * DH)]
                            .rearrange("(h d) s -> d h s", h=HG)).then_inc(stack_in, 16)

            sp.dma_start(cst[:], consts).then_inc(consts_in, 16)
            sp.dma_start(ang[:], angle.unsqueeze(0).broadcast_to([P, NB])).then_inc(consts_in, 16)
            sp.dma_start(shf[:], shift.rearrange("b t -> (b t)").unsqueeze(0).broadcast_to([P, NB * 2])
                         .rearrange("p (b t) -> p b t", b=NB)).then_inc(consts_in, 16)
            for b in range(NB):
                sp.dma_start(padded_v[b, PAD_Y:PAD_Y + S, PAD_X:PAD_X + D], x[b]).then_inc(padded_done, 16)
            sp.wait_ge(zeros_set, 1)
            for b in range(NB):
                for y in (0, PAD_Y + S):
                    sp.dma_start(padded_v[b, y:y + PAD_Y].rearrange("y x -> (y x)").rearrange("(p n) -> p n", p=16),
                                 zeros[0:16, 0:PAD_Y * PADW // 16]).then_inc(padded_done, 16)
                for x0, w in ((0, PAD_X), (PAD_X + D, PADW - PAD_X - D)):
                    sp.dma_start(padded_v[b, PAD_Y:PAD_Y + S, x0:x0 + w].rearrange("(q p) x -> p q x", p=P),
                                 zeros[:, 0:SB * w].rearrange("p (q x) -> p q x", q=SB)).then_inc(padded_done, 16)
            sp.wait_ge(index_ready, 1)
            for b in range(NB):
                sp.dma_start(fracs[b * J * 2:(b + 1) * J * 2].rearrange("(n p t) -> p n t", p=P, t=2),
                             col_f[:, b]).then_inc(fracs_done, 16)
            for stage, b, *at in warp_stages(sp):
                if stage == "strip":
                    q, n, u, turn = at
                    sp.wait_ge(strip_act, n * 3 + 6)
                    sp.wait_ge(strip_dve, n * 3 + 6)
                    for k, (x0, w) in enumerate(XBLOCKS):
                        sp.dma_start(table_v[b][x0:x0 + w, :, bass.ds(q * P, P)],
                                     strip[u][0:w, k]).then_inc(strip_stored[u], 16)
                elif stage == "project":
                    store_parts(b)
                    if b == 0:
                        for u in range(2):
                            sp.wait_ge(strip_stored[u], 48 * (JB + 1))
                        for g in range(NG - 1):
                            load_stack(g, g)
            sp.wait_ge(xwT_done, NBLK + 2)
            load_stack(NG - 1, NG - 1)

            def store_neg(n, g):
                sp.wait_ge(neg_parted, n + 1)
                for i in range(3):
                    sp.dma_start(stacks[KROWS + i:KROWS + i + 1, bass.ds(g, 1), 0].rearrange("p g h s -> p (g h s)"),
                                 neg_parts[0:HG * SB, i]).then_inc(neg_in, 16)

            def clear_pairs(part):
                rows = E * REGION // NG
                sp.dma_start(pairs_x[bass.ds(part * rows, rows), :].rearrange("(p i two) d -> p i (two d)", p=P, two=2),
                             zeros[:, 0:2 * D].unsqueeze(1).broadcast_to([P, rows // P // 2, 2 * D])
                             ).then_inc(pairs_cleared, 16)

            def load_w1(e):
                sp.dma_start(w1_all[:, bass.ds(e, 1)].squeeze(1),
                             w1[bass.ds(e, 1)].squeeze(0).rearrange("(c p) f -> p c f", p=P)).then_inc(experts_in, 16)

            def load_w2(e):
                sp.dma_start(w2_all[:, e], w2[e].rearrange("(c p) d -> p c d", p=P)).then_inc(experts_in, 16)

            sp.wait_ge(homes_set, 1)
            sp.dma_start(pair_home.rearrange("(q p) one -> q (p one)", p=P), no_home).then_inc(pairs_cleared, 16)
            store_neg(0, 0)
            with sp.Fori(0, NG - 1) as g:
                store_neg(g + 1, g + 1)
                sp.wait_ge(pv_done, (g + 1) * SB + 2)
                load_stack(g + NG, g)
                clear_pairs(g)
            store_neg(NG, 0)
            sp.wait_ge(pv_done, NG * SB + 2)
            load_stack(2 * NG - 1, NG - 1)
            clear_pairs(NG - 1)
            load_w2(E - 1)
            with sp.Fori(1, NG) as g:
                store_neg(g + NG, g)
                sp.wait_ge(pv_done, (g + NG) * SB + 2)
                for i in range(2):
                    load_w1(g * 2 - 2 + i)
            sp.wait_ge(v_group_ready, 2 * NG)
            for e in (E - 3, E - 2):
                load_w2(e)

            sp.wait_ge(pv_done, 2 * NG * SB + 2)
            for e in (E - 2, E - 1):
                load_w1(e)
            sp.wait_ge(x1_ready, NBLK)
            for e in range(E - 4):
                load_w2(e)
            sp.wait_ge(slots_ready, NB)
            load_w2(E - 4)
            sp.dma_start(b2_rows, b2.rearrange("e d -> (e d)").unsqueeze(0).broadcast_to([P, E * D])
                         .rearrange("p (e d) -> p e d", e=E)).then_inc(experts_in, 16)

            def load_tile(t):
                sp.wait_ge(x_turned, t + 1)
                row = sp.value_load(tile_row[0:1, bass.ds(t, 1)], min_val=0, max_val=E * REGION - P)
                sp.dma_start(x_tile, pairs_x[bass.ds(row, P), :]).then_inc(x_in, 16)

            def load_home(t):
                if not isinstance(t, int) or t:
                    sp.wait_ge(y_stored, t * 16)
                row = sp.value_load(tile_row[0:1, bass.ds(t, 1)], min_val=0, max_val=E * REGION - P)
                sp.dma_start(home_col[:], pair_home[bass.ds(row, P), :]).then_inc(home_in, 16)

            sp.wait_ge(scattered, 16 * 2 * NBLK)
            sp.wait_ge(tiles_ready, 1)
            load_tile(0)
            load_tile(1)
            load_tile(2)
            sp.wait_ge(homes_out, 16 * 2 * NBLK)
            load_home(0)
            with sp.Fori(1, SLOT_TILES - 2) as t:
                load_tile(t + 2)
                load_home(t)
            load_home(SLOT_TILES - 2)
            load_home(SLOT_TILES - 1)
            sp.wait_ge(y_stored, 16 * SLOT_TILES)
            for i in range(NBLK // 2):
                sp.dma_start(y_back[:, 2 * i:2 * i + 2].rearrange("p i two d -> p i (two d)"),
                             results[0:2 * NB * S].rearrange("(i p two) d -> p i (two d)", p=P, two=2)
                             [:, 2 * i:2 * i + 2]).then_inc(back_in[i], 16)
            for i in range(NBLK // 2):
                sp.wait_ge(summed, 2 * i + 2)
                b, r = 2 * i // SB, 2 * i % SB
                sp.dma_start(out[b, r * P:(r + 2) * P].rearrange("(i p) d -> p i d", p=P),
                             x1[:, 2 * i:2 * i + 2]).then_inc(all_out, 16)
            sp.wait_ge(all_out, 16 * NBLK // 2)

        def pool_hold(semaphore, value):
            nc.gpsimd.wait_ge(semaphore, value)
            nc.gpsimd.sem_inc(pool_held, 1)

        SLOW_HEAD, SLOW_POINT = 32, 3
        SLOW_BLOCK = SLOW_HEAD + SLOW_POINT * D

        def steep_block(pool, b, blk, u, it):
            g = nc.gpsimd
            block_base = it * (2 * SLOW_BLOCK) + u * SLOW_BLOCK
            steps = Steps(pool, slow_steps[b], block_base, pool_hold)
            par = [slow_par[:, i:i + 1] for i in range(8)]
            us, vs, fl, ab, ix = (slow[:, i] for i in range(5))
            pool_hold(warp_mixed, blk + 1)
            steps.do(g.memset(slow_taps[:], 0.0))
            steps.do(g.tensor_copy(slow_par[:, 0:4], row_par[:, bass.ds(blk, 1)].squeeze(1)))
            steps.do(g.tensor_copy(slow_par[:, 4:8], row_bias[:, bass.ds(blk, 1)].squeeze(1)))
            steps.do(g.tensor_scalar(us, const("column"), par[0], par[2], ALU.mult, ALU.add))
            steps.do(g.tensor_scalar(us, us, -2.0, float(D + 2), ALU.max, ALU.min))
            steps.do(g.tensor_scalar(vs, const("column"), par[1], par[3], ALU.mult, ALU.add))
            steps.do(g.tensor_scalar(vs, vs, -2.0, float(S + 2), ALU.max, ALU.min))
            steps.do(g.memset(ix, float(b * PADH * PADW)))
            for ax, w, pad, width in ((0, us, PAD_X, 1), (1, vs, PAD_Y, PADW)):
                steps.do(g.tensor_copy(slow_i[:], w))
                steps.do(g.tensor_copy(fl, slow_i[:]))
                steps.do(g.tensor_tensor(ab, fl, w, ALU.subtract))
                steps.do(g.tensor_scalar(ab, ab, 0.0, None, ALU.is_gt))
                steps.do(g.tensor_tensor(fl, fl, ab, ALU.subtract))
                steps.do(g.tensor_tensor(w, w, fl, ALU.subtract))
                steps.do(g.tensor_scalar(w, w, par[4 + 2 * ax + 1], None, ALU.subtract))
                steps.do(g.tensor_scalar(slow_frac[:, :, ax], w, -1.0, None, ALU.add))
                steps.do(g.tensor_scalar(fl, fl, float(pad), None, ALU.add))
                steps.do(g.tensor_scalar(fl, fl, float(width), None, ALU.mult))
                steps.do(g.tensor_tensor(ix, ix, fl, ALU.add))
            steps.do(g.tensor_copy(slow_i[:], ix))
            steps.do(g.memset(slow_run[:, 0:2], 0.0))
            assert steps.n == SLOW_HEAD, steps.n
            with pool.Fori(0, D) as j:
                inner = Steps(pool, slow_steps[b], block_base + SLOW_HEAD + j * SLOW_POINT, pool_hold)
                inner.do(g.tensor_copy(slow_col[:], slow_i[:, bass.ds(j, 1)]))
                g.indirect_dma_start(slow_run[:], None, padded.unsqueeze(0),
                                     bass.IndirectOffsetOnAxis(ap=slow_col[:], axis=1)).then_inc(slow_landed[b][u], 16)
                pool_hold(slow_landed[b][u], it * (16 * D) + j * 16 + 16)
                for r in range(2):
                    inner.do(g.tensor_copy(slow_taps[:, 0:2, r, bass.ds(j, 1)],
                                           slow_run[:, r * PADW:r * PADW + 2].unsqueeze(2)))
            pool.dma_start(frac[u][:], slow_frac[:]).then_inc(taps_landed[u], 16)
            for d in range(3):
                for r in range(3):
                    pool.dma_start(taps[u][:, d, r], slow_taps[:, d, r]).then_inc(taps_landed[u], 16)
            pool_hold(taps_landed[u], (it + b * SB // 2) * 160 + 160)

        def neighbours(eng, b, done):
            y = x1[:, b * SB:(b + 1) * SB]
            eng.tensor_tensor(lap_x[:, :, 1:D - 1], y[:, :, 0:D - 2], y[:, :, 2:D], ALU.add).then_inc(done, 1)
            eng.tensor_scalar(lap_x[:, :, 0:1], y[:, :, 1:2], 2.0, None, ALU.mult).then_inc(done, 1)
            eng.tensor_scalar(lap_x[:, :, D - 1:D], y[:, :, D - 2:D - 1], 2.0, None, ALU.mult).then_inc(done, 1)

        @block.gpsimd
        def _(pool):
            nc.gpsimd.memset(zeros[:], 0.0).then_inc(zeros_set, 1)
            nc.gpsimd.memset(v_all[:, :, :, :, DH:DH + 1], 1.0).then_inc(v_cleared, 1)
            pool.wait_ge(index_ready, 1)
            pool.wait_ge(padded_done, 16 * 5 * NB)
            for stage, b, *at in warp_stages(pool):
                if stage == "strip":
                    q, n, u, turn = at
                    steps = Steps(pool, pool_steps, n, pool_hold)
                    pool_hold(strips_turned, n * 6 + 6)
                    steps.do(nc.gpsimd.tensor_copy(band_col[:, u:u + 1], band_index[:, bass.ds(n, 1)]))
                    nc.gpsimd.indirect_dma_start(
                        band[u], None, padded.unsqueeze(0),
                        bass.IndirectOffsetOnAxis(ap=band_col[:, u:u + 1], axis=1)).then_inc(band_landed[u], 16)
                elif stage == "taps":
                    pair, = at
                    it = pair - b * SB // 2
                    for u in range(2):
                        strips = ((b + 1) * JB + 1 - u) // 2
                        pool.wait_ge(strip_stored[u], 48 * (strips + 1))
                    pool.wait_ge(fracs_done, 16 * NB)
                    pool.wait_ge(index_ready, 2 + b)
                    beyond = pool.value_load(steep[0:1, b * SB:b * SB + 1], min_val=0, max_val=1)
                    with pool.If(beyond < 1):
                        steps = Steps(pool, fast_steps[b], it * 4, pool_hold)
                        for u in range(2):
                            blk = pair * 2 + u
                            pool_hold(warp_mixed, blk + 1)
                            steps.mark(nc.gpsimd.tensor_copy(tap_col[:, u:u + 1], tap_index[:, bass.ds(blk, 1)]))
                            steps.do(nc.gpsimd.tensor_copy(frac_col[:, u:u + 1], frac_index[:, bass.ds(blk, 1)]))
                            nc.gpsimd.indirect_dma_start(
                                frac[u].rearrange("p d t -> p (d t)"), None, fracs.unsqueeze(0),
                                bass.IndirectOffsetOnAxis(ap=frac_col[:, u:u + 1], axis=1)
                            ).then_inc(taps_landed[u], 16)
                            for d in range(3):
                                for r in range(3):
                                    nc.gpsimd.indirect_dma_start(
                                        taps[u][:, d, r], None, table[b].unsqueeze(0),
                                        bass.IndirectOffsetOnAxis(ap=tap_col[:, u:u + 1], axis=1),
                                        element_offset=(d * R + r) * J).then_inc(taps_landed[u], 16)
                    with pool.If(beyond > 0):
                        for u in range(2):
                            steep_block(pool, b, pair * 2 + u, u, it)

            pool.wait_ge(xwT_done, NBLK + 2)
            g_ = nc.gpsimd
            g_.memset(v_group, 0.0).then_inc(v_cleared, 1)
            pool.wait_ge(v_cleared, 2)
            g_.memset(stacks[KROWS:KROWS + 3, :, 1], 1.0).then_inc(v_cleared, 1)
            pool.wait_ge(v_cleared, 3)

            def groups_of_v(b):
                pool.wait_ge(v_ready, b + 1)
                with pool.Fori(0, NG) as g:
                    pool_hold(pv_done, (g + b * NG) * SB + 2)
                    g_.tensor_copy(v_group[:, :, :, 0:DH + 1],
                                   v_all[:, b, :, bass.ds(g * HG, HG)]).then_inc(v_group_ready, 1)

            def scatter(b):
                pool.wait_ge(slots_ready, b + 1)
                for i in range(b * SB, (b + 1) * SB):
                    for k in range(2):
                        g_.indirect_dma_start(pairs_x, bass.IndirectOffsetOnAxis(ap=x_index[:, k, i:i + 1], axis=0),
                                              du[:, i], None).then_inc(scattered, 16)
                for i in range(b * SB, (b + 1) * SB):
                    for k in range(2):
                        g_.indirect_dma_start(pair_home, bass.IndirectOffsetOnAxis(ap=x_index[:, k, i:i + 1], axis=0),
                                              home[:, k, i:i + 1], None).then_inc(homes_out, 16)

            groups_of_v(0)
            groups_of_v(1)
            pool.wait_ge(x1_ready, SB)
            neighbours(g_, 0, beside)
            pool.wait_ge(pairs_cleared, 16 * (NG + 1))
            for b in range(NB):
                scatter(b)
            with pool.Fori(0, SLOT_TILES) as t:
                pool_hold(y_ready, t + 2)
                pool_hold(home_in, t * 16 + 16)
                g_.indirect_dma_start(results, bass.IndirectOffsetOnAxis(ap=home_col[:, 0:1], axis=0), y_tile,
                                      None).then_inc(y_stored, 16)

        @block.scalar
        def _(act):
            for i, w in enumerate((wq, wk, wv)):
                act.dma_start(wqkv[:, i], w.rearrange("(c p) n -> p c n", p=P)).then_inc(weights_in, 16)
            for i, w in enumerate((bq, bk)):
                act.dma_start(bqk[:, i], w.rearrange("(c p) -> p c", p=P),
                              allow_slow_non_contiguous=True).then_inc(weights_in, 16)
            act.dma_start(bv_rows[:], bv.unsqueeze(0).broadcast_to([P, D])).then_inc(weights_in, 16)
            for i, z in enumerate((zx, zy, zr)):
                act.dma_start(z_cols[:, i], z.unsqueeze(0).broadcast_to([P, NB])).then_inc(weights_in, 16)
            act.dma_start(wr_cols[:], wr.rearrange("(c p) e -> p c e", p=P)).then_inc(weights_in, 16)
            act.dma_start(br_row[:], br.unsqueeze(0).broadcast_to([P, E])).then_inc(weights_in, 16)
            act.dma_start(b1_rows[:], b1.rearrange("e (f p) -> (e f) p", p=P)).then_inc(weights_in, 16)
            act.dma_start(wo_rows[0:DH], wo).then_inc(weights_in, 16)
            act.dma_start(wo_rows[DH:DH + 1], bo.unsqueeze(0)).then_inc(weights_in, 16)
            act.dma_start(x1[:].rearrange("p (b i) d -> p b i d", b=NB),
                          x.rearrange("b (i p) d -> p b i d", p=P)).then_inc(weights_in, 16)
            for stage, b, *at in warp_stages(act):
                if stage == "strip":
                    q, n, u, turn = at
                    act.wait_ge(strip_stored[u], turn * 48 + 48)
                    for g in range(3):
                        k, half = g // 2, g % 2
                        w = XBLOCKS[k][1]
                        act.wait_ge(strips_turned, n * 6 + g + 13)
                        nc.scalar.activation(strip[u][0:w, k, 4 * half:4 * half + 4],
                                             banks[g][0:w, :].rearrange("p (r q) -> p r q", r=4),
                                             ACT.Copy).then_inc(strip_act, 1)
                elif stage == "taps":
                    pair, = at
                    steps = Steps(act, act_hats, pair * 4)
                    for u in range(2):
                        blk = pair * 2 + u
                        act.wait_ge(taps_landed[u], pair * 160 + 160)
                        act.wait_ge(warp_mixed, blk + 1)
                        for ax in range(2):
                            f = frac[u][:, :, ax]
                            up = row_bias[:, bass.ds(blk, 1), 2 * ax]
                            down = row_bias[:, bass.ds(blk, 1), 2 * ax + 1]
                            h = hats[u][:, ax]
                            nc.scalar.activation(h[:, 0], f, ACT.Relu, bias=up, scale=-1.0)
                            nc.scalar.activation(h[:, 2], f, ACT.Relu, bias=down)
                            steps.mark(nc.scalar.activation(h[:, 3], f, ACT.Abs, bias=down))
                        steps.wait()
                        for ax in range(2):
                            h = hats[u][:, ax]
                            ins = nc.scalar.activation(h[:, 1], h[:, 3], ACT.Relu, bias=const("ones")[:, 0:1],
                                                       scale=-1.0)
                        ins.then_inc(hats_ready, 1)
                    for u in range(2):
                        blk = pair * 2 + u
                        act.wait_ge(warp_turned, blk + 1)
                        nc.scalar.activation(xwT[:, :, bass.ds(blk * P, P)],
                                             banks[6 + u][:, 0:D].rearrange("p (c q) -> p c q", c=DC),
                                             ACT.Copy).then_inc(xwT_done, 1)
                elif stage == "project":
                    act.wait_ge(weights_in, 16 * N_WEIGHTS)
                    for j in range(QK_CHUNKS):
                        kind, c, n = j // (2 * DC), j // 2 % DC, b * QK_CHUNKS + j
                        act.wait_ge(projected, b * PROJ_BATCH + j + 1)
                        if n >= PART_SLOTS:
                            act.wait_ge(parts_stored[j % PART_SLOTS], 16 * (n // PART_SLOTS))
                        nc.scalar.activation(parts[j % PART_SLOTS][:, 0], banks[j], ACT.Identity,
                                             bias=bqk[:, kind, c:c + 1]).then_inc(first_parts, 1)

            def exponentials(n, j):
                kt = KEY_BLOCKS[j]
                act.wait_ge(pv_done, n * SB + (j + 1))
                for h in range(HG):
                    act.wait_ge(scored, n * (SB * HG) + (j * HG + h + 1))
                    slot = (j * HG + h) % 2
                    nc.scalar.activation(
                        probs[j % 2][h][:, kt * P:S],
                        psum[:, 2 * slot:2 * slot + 2].rearrange("p a q -> p (a q)")[:, kt * P:S],
                        ACT.Exp, scale=DH ** -0.5).then_inc(exp_done, 1)

            def copy_output(n):
                act.wait_ge(pv_done, n * SB + (SB + 2))
                act.wait_ge(o_normed, n + 1)
                nc.scalar.activation(o_group.rearrange("p (a q) -> p a q", a=2), psum[:, 4:6],
                                     ACT.Copy).then_inc(o_read, 1)

            def scale(b):
                act.wait_ge(x1_ready, SB * (b + 1))
                nc.scalar.activation(du[:, b * SB:(b + 1) * SB].rearrange("p i d -> p (i d)"),
                                     x1[:, b * SB:(b + 1) * SB].rearrange("p i d -> p (i d)"), ACT.Identity,
                                     bias=z_cols[:, 4, b:b + 1], scale=z_cols[:, 3, b:b + 1]).then_inc(scaled, 1)

            act.wait_ge(z_ready, 2)
            for n, _, _, _, plan, first in attention_groups(act):
                if plan is END_PLAN:
                    scale(0)
                exponentials(n, 0)
                if not first:
                    copy_output(n - 1)
                for j in range(1, SB):
                    exponentials(n, j)
            copy_output(2 * NG - 1)

            scale(1)
            act.wait_ge(gap_ready, 1)
            nc.scalar.activation(route[:, 1], route[:, 0], ACT.Exp).then_inc(gap_exp, 1)

            def hidden(t):
                act.wait_ge(h_turned, t + 1)
                e = act.value_load(tile_expert[0:1, bass.ds(t, 1)], min_val=0, max_val=E - 1)
                for f in range(FC):
                    ins = nc.scalar.activation(hidden_t[:, f], banks[3 + f // 4][:, (f % 4) * P:(f % 4 + 1) * P],
                                               ACT.Relu, bias=b1_cols[:, bass.ds(e, 1), f])
                ins.then_inc(hidden_ready, 1)

            act.wait_ge(tiles_ready, 1)
            with act.Fori(0, SLOT_TILES) as t:
                hidden(t)

        @block.tensor
        def _(pe):
            pe.wait_ge(consts_in, 48)
            t_ = nc.tensor

            def chunk(bank, g, h, r):
                qb, kc, keys = chunk_of(r)
                head = bass.ds(h, 1)
                diagonal = qb // 4 == kc
                ins = t_.matmul(bank[:, 0:keys],
                                stacks[0:KROWS, bass.ds(g, 1), 0, head, qb * P:(qb + 1) * P].squeeze(1).squeeze(1),
                                stacks[0:KROWS, bass.ds(g, 1), 1, head, kc * 512:kc * 512 + keys].squeeze(1).squeeze(1),
                                start=True, stop=not diagonal)
                if diagonal:
                    at_ = qb * P - kc * 512
                    ins = t_.matmul(bank[:, at_:at_ + P], ident_b[:], mask_qk[:], start=False, stop=True)
                return ins

            def project_qk(bank, b, j):
                kind, c, half = j // (2 * DC), j // 2 % DC, j % 2
                for dc in range(DC):
                    ins = t_.matmul(bank, wqkv[:, kind, dc, c * P:(c + 1) * P],
                                    xwT[:, dc, b * S + half * 512:b * S + (half + 1) * 512],
                                    start=dc == 0, stop=dc == DC - 1)
                return ins

            def project_v(bank, b, j):
                for kt in (2 * j, 2 * j + 1):
                    for dc in range(DC):
                        ins = t_.matmul(bank[:, (kt % 2) * D:(kt % 2 + 1) * D],
                                        xwT[:, dc, b * S + kt * P:b * S + (kt + 1) * P], wqkv[:, 2, dc],
                                        start=dc == 0, stop=dc == DC - 1)
                return ins

            for stage, b, *at in warp_stages(pe):
                if stage == "strip":
                    q, n, u, turn = at
                    pe.wait_ge(band_landed[u], turn * 16 + 16)
                    for g in range(6):
                        k, half = g // 2, g % 2
                        x0, w = XBLOCKS[k]
                        if g < 3:
                            pe.wait_ge(strip_act, n * 3 + g + 1)
                        else:
                            pe.wait_ge(strip_dve, n * 3 + g - 2)
                        for r in range(4):
                            at_ = (4 * half + r) * PADW + x0
                            ins = t_.transpose(banks[g][0:w, r * P:(r + 1) * P], band[u][:, at_:at_ + w], ident)
                        ins.then_inc(strips_turned, 1)
                elif stage == "taps":
                    for u in range(2):
                        blk = at[0] * 2 + u
                        pe.wait_ge(warp_mixed, blk + 3)
                        pe.wait_ge(xwT_done, blk + 1)
                        for c in range(DC):
                            ins = t_.transpose(banks[6 + u][:, c * P:(c + 1) * P], warped[u][:, c * P:(c + 1) * P],
                                               ident)
                        ins.then_inc(warp_turned, 1)
                elif stage == "maxima":
                    h, = at
                    pe.wait_ge(stack_in, STACK_IN)
                    pe.wait_ge(masks_set, 3)
                    for r in range(CHUNKS // HG):
                        pe.wait_ge(max_read, h * (CHUNKS // HG) + (2 if r < 6 else r - 3))
                        chunk(banks[r % 6], 0, h, r).then_inc(max_scored, 1)
                elif stage == "project":
                    pe.wait_ge(weights_in, 16 * N_WEIGHTS)
                    pe.wait_ge(xwT_done, SB * (b + 1) + 2)
                    pe.wait_ge(strip_act, 3 * 2 * JB + 3)
                    pe.wait_ge(strip_dve, 3 * 2 * JB + 3)
                    if b:
                        pe.wait_ge(max_read, CHUNKS + 2)
                    for j in range(QK_CHUNKS):
                        project_qk(banks[j], b, j).then_inc(projected, 1)
                    for j in range(SB // 2):
                        pe.wait_ge(proj_read, b * QK_CHUNKS + j + 1)
                        project_v(banks[j], b, j).then_inc(projected, 1)
                    pe.wait_ge(proj_read, (b + 1) * QK_CHUNKS)
                    pe.wait_ge(v_ready, b + 1)

            pe.wait_ge(masks_set, 3)
            pe.wait_ge(xwT_done, NBLK + 2)

            def side(n, g, first_use, use, what, i):
                last = isinstance(n, int) and n == 2 * NG
                b = 1 if last else 0
                plan = [LAST_PLAN] if last else END_PLAN
                bank, again = side_bank(last, use)
                pe.wait_ge(max_read, first_use + max(use - again + 1, 0) + 2)

                def read(what_, i_):
                    pe.wait_ge(max_read, first_use + uses_until(plan, (what_, i_)) + 2)

                if what == "chunk":
                    ins = chunk(bank, g, i // (CHUNKS // HG), i % (CHUNKS // HG))
                elif what == "turn_max":
                    pe.wait_ge(neg_ready, n + 1)
                    ins = t_.transpose(bank[0:HG * SB, 0:P], neg_max, ident)
                elif what == "sum":
                    pe.wait_ge(o_read, n + 1)
                    for k in range(4):
                        at_ = (4 * i + k) * P
                        ins = t_.transpose(bank[:, k * P:(k + 1) * P], o_group[:, at_:at_ + P], ident)
                elif what == "turn_z":
                    pe.wait_ge(o_normed, n + 1)
                    for k in range(4):
                        ins = t_.transpose(bank[0:DH + 1, k * P:(k + 1) * P], z[:, z_batch(n), 4 * i + k], ident)
                elif what == "attend":
                    pe.wait_ge(z_turned, z_batch(n) + 1)
                    for k in range(2):
                        at_ = (2 * i + k) * P
                        ins = t_.matmul(bank[:, k * D:(k + 1) * D], z_t[0:DH + 1, at_:at_ + P], wo_rows[:],
                                        start=True, stop=True)
                elif what == "lap":
                    if last:
                        read("attend", min(i + 1, SB // 2 - 1))
                    else:
                        pe.wait_ge(x1_ready, SB)
                    for k in range(2):
                        r = 2 * i + k
                        terms = [("lap_first" if r == 0 else "lap_last" if r == SB - 1 else "lap_mid", r)]
                        terms += [("lap_prev", r - 1)] if r else []
                        terms += [("lap_next", r + 1)] if r < SB - 1 else []
                        for m, (name, row) in enumerate(terms):
                            ins = t_.matmul(bank[:, k * D:(k + 1) * D], const(name), x1[:, b * SB + row],
                                            start=m == 0, stop=m == len(terms) - 1)
                elif what == "turn_du":
                    read("lap", i)
                    for m in range(2 * DC):
                        r, c = m // DC, m % DC
                        rows = du[:, b * SB + 2 * i + r]
                        ins = t_.transpose(bank[:, m * P:(m + 1) * P], rows[:, c * P:(c + 1) * P], ident)
                elif what == "logits":
                    read("turn_du", i)
                    for r in range(2):
                        for c in range(DC):
                            ins = t_.matmul(bank[:, r * E:(r + 1) * E], du_t[i % 2][:, r, c], wr_cols[:, c],
                                            start=c == 0, stop=c == DC - 1)
                elif what == "rank":
                    pe.wait_ge(chosen_ready, b + 1)
                    own = chosen[:, b * SB * E:(b + 1) * SB * E]
                    t_.matmul(bank[:, 0:SB * E], const("before"), own, start=True, stop=True)
                    ins = t_.matmul(bank[:, SB * E:2 * SB * E], const("ones"), own, start=True, stop=True)
                elif what == "turn_b1":
                    ins = t_.transpose(bank[:, 0:E * FC], b1_rows[:], const("identity")[0:E * FC, 0:E * FC])
                ins.then_inc(max_scored, 1)

            def weighted(n, j, half):
                kt = KEY_BLOCKS[j]
                if half:
                    pe.wait_ge(exp_done, n * (SB * HG) + (HG * (j + 1) + 2))
                    if j == 0:
                        pe.wait_ge(o_read, n + 1)
                        pe.wait_ge(v_group_ready, n + 1)
                q0 = max(kt * P, half * 512)
                for h in range(HG):
                    ins = t_.matmul(banks[4 + half][32 * h:32 * h + 32, q0 - half * 512:512],
                                    v_group[:, kt, h], probs[j % 2][h][:, q0:(half + 1) * 512],
                                    start=j == 0, stop=j == SB - 1)
                if half == 0 or kt >= SB // 2:
                    ins.then_inc(pv_done, 1)

            def score(n, g, j, h):
                kt = KEY_BLOCKS[j]
                unit = j * HG + h
                pe.wait_ge(exp_done, n * (SB * HG) + (unit + 1))
                for half in range(kt // 4, 2):
                    q0 = max(kt * P, half * 512)
                    bank = banks[2 * (unit % 2) + half]
                    diagonal = q0 == kt * P
                    ins = t_.matmul(bank[:, q0 - half * 512:512],
                                    stacks[0:KROWS + 3, bass.ds(g, 1), 1, h, kt * P:(kt + 1) * P].squeeze(1),
                                    stacks[0:KROWS + 3, bass.ds(g, 1), 0, h, q0:(half + 1) * 512].squeeze(1),
                                    start=True, stop=not diagonal)
                    if diagonal:
                        at_ = kt * P - half * 512
                        ins = t_.matmul(bank[:, at_:at_ + P], ident_b[:], mask_kq[:], start=False, stop=True)
                ins.then_inc(scored, 1)

            side(0, 0, CHUNKS, 0, "turn_max", 0)
            pe.wait_ge(v_cleared, 3)
            for n, g, following, uses, plan, first in attention_groups(pe):
                pe.wait_ge(neg_in, n * 48 + 48)
                if following is not None:
                    pe.wait_ge(stack_in, n * STACK_IN + 2 * STACK_IN)
                use = 0
                for j in range(SB):
                    for h in range(HG):
                        for what, i in plan[j * HG + h]:
                            side(n + 1 if what == "turn_max" else n, following, uses, use, what, i)
                            use += 1
                        score(n, g, j, h)
                        if h % 2 and (j or not first):
                            half = 1 - h // 2
                            if half or KEY_BLOCKS[j - 1] < SB // 2:
                                weighted(n if j else n - 1, (j - 1) % SB, half)
            for half in (1, 0):
                weighted(2 * NG - 1, SB - 1, half)
            for use, (what, i) in enumerate(LAST_PLAN):
                side(2 * NG, None, LAST_USES, use, what, i)

            def turn_x(t):
                pe.wait_ge(x_in, t * 16 + 16)
                for c in range(DC):
                    ins = t_.transpose(banks[2][:, c * P:(c + 1) * P], x_tile[:, c * P:(c + 1) * P], ident)
                ins.then_inc(x_turned, 1)

            def first_product(t, e):
                pe.wait_ge(x_t_ready, t + 1)
                pe.wait_ge(h_ready, t + 1)
                for half in range(2):
                    for c in range(DC):
                        ins = t_.matmul(banks[half], x_t[:, c],
                                        w1_all[:, bass.ds(e, 1), c, half * 512:(half + 1) * 512].squeeze(1),
                                        start=c == 0, stop=c == DC - 1)
                ins.then_inc(h_made, 1)

            def turn_h(t):
                pe.wait_ge(h_ready, t + 2)
                for f in range(FC):
                    ins = t_.transpose(banks[3 + f // 4][:, (f % 4) * P:(f % 4 + 1) * P], h_tile[:, f * P:(f + 1) * P],
                                       ident)
                ins.then_inc(h_turned, 1)

            def second_product(t, e):
                pe.wait_ge(hidden_ready, t + 1)
                pe.wait_ge(y_ready, t + 1)
                for f in range(FC):
                    ins = t_.matmul(banks[5][:, 0:D], hidden_t[:, f], w2_all[:, bass.ds(e, 1), f].squeeze(1),
                                    start=f == 0, stop=f == FC - 1)
                ins.then_inc(y_made, 1)

            def expert_of(t):
                return pe.value_load(tile_expert[0:1, bass.ds(t, 1)], min_val=0, max_val=E - 1)

            pe.wait_ge(tiles_ready, 1)
            pe.wait_ge(experts_in, 16 * (2 * E + 1))
            turn_x(0)
            first_product(0, expert_of(0))
            turn_x(1)
            turn_h(0)
            with pe.Fori(1, SLOT_TILES - 1) as t:
                first_product(t, expert_of(t))
                expert_before = expert_of(t - 1)
                turn_x(t + 1)
                second_product(t - 1, expert_before)
                turn_h(t)
            last = SLOT_TILES - 1
            first_product(last, expert_of(last))
            second_product(last - 1, expert_of(last - 1))
            turn_h(last)
            second_product(last, expert_of(last))

        @block.vector
        def _(dve):
            v = nc.vector
            steps = Steps(dve, dve_steps)
            dve.wait_ge(consts_in, 48)
            dve.wait_ge(zeros_set, 1)

            def ts(o, a, s1, op0, s2=None, op1=None):
                if op1 is None:
                    steps.do(v.tensor_scalar(o, a, s1, None, op0))
                else:
                    steps.do(v.tensor_scalar(o, a, s1, s2, op0, op1))

            def tt(o, a, b_, op):
                steps.do(v.tensor_tensor(o, a, b_, op))

            def stt(o, a, s, b_, op0, op1):
                steps.do(v.scalar_tensor_tensor(out=o, in0=a, scalar=s, in1=b_, op0=op0, op1=op1))

            def floor(o, a, whole, above):
                steps.do(v.tensor_copy(whole, a))
                steps.do(v.tensor_copy(o, whole))
                tt(above, o, a, ALU.is_gt)
                tt(o, o, above, ALU.subtract)

            (KQ, RA, Z2, SN, CS, ODD, K4, T0, T1, SIN, COS, TAN, CA, CB, CP, CQ, CU, CV, STEEP, T2) = range(20)
            pr = [prm[:, i] for i in range(40)]
            wi2 = tmp_i[:, 0:NB]
            ts(pr[T0], ang[:], 2 / np.pi, ALU.mult, 0.5, ALU.add)
            floor(pr[KQ], pr[T0], wi2, pr[T1])
            stt(pr[RA], pr[KQ], -1.5703125, ang[:], ALU.mult, ALU.add)
            stt(pr[RA], pr[KQ], -4.837512969970703125e-4, pr[RA], ALU.mult, ALU.add)
            stt(pr[RA], pr[KQ], -7.549789948768648e-8, pr[RA], ALU.mult, ALU.add)
            tt(pr[Z2], pr[RA], pr[RA], ALU.mult)
            ts(pr[T0], pr[Z2], -1.9515295891e-4, ALU.mult, 8.3321608736e-3, ALU.add)
            tt(pr[T0], pr[T0], pr[Z2], ALU.mult)
            ts(pr[T0], pr[T0], -1.6666654611e-1, ALU.add)
            tt(pr[T0], pr[T0], pr[Z2], ALU.mult)
            stt(pr[SN], pr[T0], 1.0, pr[RA], ALU.add, ALU.mult)
            ts(pr[T0], pr[Z2], 2.443315711809948e-5, ALU.mult, -1.388731625493765e-3, ALU.add)
            tt(pr[T0], pr[T0], pr[Z2], ALU.mult)
            ts(pr[T0], pr[T0], 4.166664568298827e-2, ALU.add)
            tt(pr[T0], pr[T0], pr[Z2], ALU.mult)
            ts(pr[T0], pr[T0], -0.5, ALU.add)
            tt(pr[T0], pr[T0], pr[Z2], ALU.mult)
            ts(pr[CS], pr[T0], 1.0, ALU.add)
            ts(pr[T0], pr[KQ], 0.25, ALU.mult)
            floor(pr[K4], pr[T0], wi2, pr[T1])
            stt(pr[K4], pr[K4], -4.0, pr[KQ], ALU.mult, ALU.add)
            ts(pr[T0], pr[K4], 0.5, ALU.mult)
            floor(pr[ODD], pr[T0], wi2, pr[T1])
            stt(pr[ODD], pr[ODD], -2.0, pr[K4], ALU.mult, ALU.add)
            tt(pr[T0], pr[CS], pr[SN], ALU.subtract)
            tt(pr[T0], pr[T0], pr[ODD], ALU.mult)
            tt(pr[SIN], pr[SN], pr[T0], ALU.add)
            tt(pr[COS], pr[CS], pr[T0], ALU.subtract)
            ts(pr[T0], pr[K4], 2.0, ALU.is_ge, -2.0, ALU.mult)
            stt(pr[SIN], pr[T0], 1.0, pr[SIN], ALU.add, ALU.mult)
            ts(pr[T0], pr[K4], 1.0, ALU.is_ge)
            ts(pr[T1], pr[K4], 3.0, ALU.is_lt)
            tt(pr[T0], pr[T0], pr[T1], ALU.mult)
            ts(pr[T0], pr[T0], -2.0, ALU.mult, 1.0, ALU.add)
            tt(pr[COS], pr[COS], pr[T0], ALU.mult)
            most = SHEAR / (S // 2)
            stt(pr[T0], pr[SIN], -1.0, pr[SIN], ALU.mult, ALU.max)
            stt(pr[T1], pr[COS], -1.0, pr[COS], ALU.mult, ALU.max)
            ts(pr[T1], pr[T1], -most, ALU.mult)
            tt(pr[STEEP], pr[T0], pr[T1], ALU.add)
            ts(pr[STEEP], pr[STEEP], 0.0, ALU.is_gt)
            ts(pr[T2], pr[T1], -1.0 / most, ALU.mult, 0.5, ALU.max)
            steps.do(v.reciprocal(pr[T2], pr[T2]))
            ts(pr[T1], pr[COS], 0.0, ALU.is_ge)
            ts(pr[T1], pr[T1], 2.0, ALU.mult, -1.0, ALU.add)
            tt(pr[T2], pr[T2], pr[T1], ALU.mult)
            tt(pr[TAN], pr[SIN], pr[T2], ALU.mult)
            ts(pr[CA], pr[SIN], KX, ALU.mult)
            ts(pr[CB], pr[COS], KX, ALU.mult)
            ts(pr[CP], pr[COS], KY, ALU.mult)
            ts(pr[CQ], pr[SIN], -KY, ALU.mult)
            for o, t, k, mid in ((CU, 1, KX, (D - 1) / 2), (CV, 0, KY, (S - 1) / 2)):
                ts(pr[o], shf[:, :, t], k, ALU.mult, mid, ALU.add)
                ts(pr[o], pr[o], -1.0e5, ALU.max, 1.0e5, ALU.min)

            def scalar(i, b):
                return prm[:, i, b:b + 1]

            t = [tmp[:, i] for i in range(12)]
            def rows_of(b):
                row = const("row")
                sh, w0, fw, e0, fe, ab, cu, cv = (t[i][:, 0:SB] for i in range(8))
                w8 = tmp_i[:, 0:SB]
                bs = slice(b * SB, (b + 1) * SB)
                ts(cu, row, scalar(TAN, b), ALU.mult, 0.5, ALU.add)
                floor(sh, cu, w8, ab)
                ts(sh, sh, float(-SHEAR), ALU.max, float(SHEAR), ALU.min)
                ts(cu, row, scalar(CB, b), ALU.mult, scalar(CU, b), ALU.add)
                stt(fw, sh, scalar(CA, b), cu, ALU.mult, ALU.add)
                floor(w0, fw, w8, ab)
                tt(fw, fw, w0, ALU.subtract)
                ts(cv, row, scalar(CQ, b), ALU.mult)
                stt(fe, sh, scalar(CP, b), cv, ALU.mult, ALU.add)
                floor(e0, fe, w8, ab)
                tt(fe, fe, e0, ALU.subtract)
                for i, f in ((0, fw), (2, fe)):
                    ts(row_bias[:, bs, i], f, -1.0, ALU.mult, 1.0, ALU.add)
                    ts(row_bias[:, bs, i + 1], f, -1.0, ALU.add)
                ts(w0, w0, float(-X_LOW), ALU.max, float(XW - X_LOW - 3), ALU.min)
                ts(e0, e0, float(-R_LOW), ALU.max, float(R - R_LOW - 3), ALU.min)
                ts(w0, w0, float(X_LOW), ALU.add)
                stt(e0, w0, float(R), e0, ALU.mult, ALU.add)
                ts(e0, e0, float(R_LOW), ALU.add, float(J), ALU.mult)
                tt(e0, e0, sh, ALU.subtract)
                ts(e0, e0, float(SHEAR), ALU.add)
                steps.do(v.tensor_copy(tap_index[:, bs], e0))
                ts(sh, sh, -2.0, ALU.mult, float(2 * (b * J + SHEAR)), ALU.add)
                steps.do(v.tensor_copy(frac_index[:, bs], sh))
                ts(row_par[:, bs, 0], row, 0.0, ALU.mult, scalar(CA, b), ALU.add)
                ts(row_par[:, bs, 1], row, 0.0, ALU.mult, scalar(CP, b), ALU.add)
                steps.do(v.tensor_copy(row_par[:, bs, 2], cu))
                ts(row_par[:, bs, 3], cv, scalar(CV, b), ALU.add)
                ts(t[8][:, 0:SB], row, 0.0, ALU.mult, scalar(STEEP, b), ALU.add)
                steps.do(v.tensor_copy(steep[:, bs], t[8][:, 0:SB]))
                dve.sem_inc(index_ready, 1)

            for b in range(NB):
                m, nn, ab, w5 = t[0][:, 0:JB], t[1][:, 0:JB], t[2][:, 0:JB], tmp_i[:, 0:JB]
                uj, vj = t[3][:, 0:JB], t[4][:, 0:JB]
                ts(uj, const("sheared"), scalar(CA, b), ALU.mult)
                floor(m, uj, w5, ab)
                tt(col_f[:, b, :, 0], uj, m, ALU.subtract)
                ts(vj, const("sheared"), scalar(CP, b), ALU.mult, scalar(CV, b), ALU.add)
                floor(nn, vj, w5, ab)
                tt(col_f[:, b, :, 1], vj, nn, ALU.subtract)
                ts(m, m, float(-MSHIFT), ALU.max, float(MSHIFT - 1), ALU.min)
                ts(nn, nn, float(-R_LOW), ALU.add, float(-R), ALU.max)
                ts(nn, nn, float(S), ALU.min, float(PAD_Y), ALU.add)
                stt(nn, nn, float(PADW), m, ALU.mult, ALU.add)
                ts(nn, nn, float(PAD_X - X_LOW + b * PADH * PADW), ALU.add)
                steps.do(v.tensor_copy(band_index[:, b * JB:(b + 1) * JB], nn))
            dve.sem_inc(strips_turned, 12)
            dve.sem_inc(index_ready, 1)
            dve.sem_inc(strip_act, 3)
            dve.sem_inc(strip_dve, 3)
            dve.sem_inc(strip_stored[0], 48)
            dve.sem_inc(strip_stored[1], 48)
            dve.sem_inc(warp_mixed, 2)
            dve.sem_inc(exp_done, 2)
            dve.sem_inc(pv_done, 2)
            dve.sem_inc(max_read, 2)
            dve.sem_inc(o_read, 1)
            dve.sem_inc(x_turned, 1)
            dve.sem_inc(h_ready, 1)
            dve.sem_inc(y_ready, 1)
            dve.sem_inc(o_normed, 1)
            for o, name in ((ident_b, "identity"), (mask_qk, "mask_qk"), (mask_kq, "mask_kq")):
                v.tensor_copy(o[:], const(name)).then_inc(masks_set, 1)
            dve.sem_inc(xwT_done, 2)
            def what_it_leaves(b, j):
                kind, c, n = j // (2 * DC), j // 2 % DC, b * QK_CHUNKS + j
                dve.wait_ge(first_parts, n + 1)
                if j >= 2:
                    dve.wait_ge(parts_ready, n - 1)
                v.scalar_tensor_tensor(out=resid[j % 2], in0=banks[j], scalar=bqk[:, kind, c:c + 1],
                                       in1=parts[j % PART_SLOTS][:, 0], op0=ALU.add,
                                       op1=ALU.subtract).then_inc(proj_read, 1)

            def second_part(b, j):
                dve.wait_ge(proj_read, b * QK_CHUNKS + j + 1)
                v.tensor_copy(parts[j % PART_SLOTS][:, 1], resid[j % 2]).then_inc(halved, 1)

            def third_part(b, j):
                dve.wait_ge(halved, b * QK_CHUNKS + j + 1)
                v.tensor_tensor(parts[j % PART_SLOTS][:, 2], resid[j % 2], parts[j % PART_SLOTS][:, 1],
                                ALU.subtract).then_inc(parts_ready, 1)

            def largest(bank, h, r):
                qb, kc, keys = chunk_of(r)
                return v.reduce_max(max_parts[:, kc, bass.ds(h * SB + qb, 1)], bank[:, 0:keys], AX_X)

            steps.do(v.memset(max_parts, -3.0e38))
            for stage, b, *at in warp_stages(dve):
                if stage == "strip":
                    q, n, u, turn = at
                    dve.wait_ge(strip_stored[u], turn * 48 + 48)
                    for g in range(3, 6):
                        k, half = g // 2, g % 2
                        w = XBLOCKS[k][1]
                        dve.wait_ge(strips_turned, n * 6 + g + 13)
                        v.tensor_copy(strip[u][0:w, k, 4 * half:4 * half + 4],
                                      banks[g][0:w, :].rearrange("p (r q) -> p r q", r=4)).then_inc(strip_dve, 1)
                elif stage == "rows":
                    rows_of(b)
                    if b:
                        for bb in range(NB):
                            for k in range(2):
                                first_row = float(2 * (S // 2 + bb * S) + k)
                                ts(t[0][:, 0:SB], const("row"), 2.0, ALU.mult, first_row, ALU.add)
                                steps.do(v.tensor_copy(home[:, k, bb * SB:(bb + 1) * SB], t[0][:, 0:SB]))
                        ts(no_home_f, const("column")[:, 0:P], float(D // 2 + 2 * NB * S), ALU.add)
                        steps.do(v.tensor_copy(no_home, no_home_f))
                        dve.sem_inc(homes_set, 1)
                elif stage == "taps":
                    pair, = at
                    st = Steps(dve, warp_dve, pair * 10)
                    for u in range(2):
                        blk = pair * 2 + u
                        dve.wait_ge(taps_landed[u], pair * 160 + 160)
                        dve.wait_ge(hats_ready, blk + 1)
                        hat = hats[u][:, 0, 0:3].unsqueeze(2).broadcast_to([P, 3, 3, D])
                        st.do(v.tensor_tensor(taps[u], taps[u], hat, ALU.mult))
                        for d in (1, 2):
                            st.do(v.tensor_tensor(taps[u][:, 0], taps[u][:, 0], taps[u][:, d], ALU.add))
                        st.do(v.tensor_tensor(taps[u][:, 0], taps[u][:, 0], hats[u][:, 1, 0:3], ALU.mult))
                        st.do(v.tensor_tensor(taps[u][:, 0, 0], taps[u][:, 0, 0], taps[u][:, 0, 1], ALU.add))
                        dve.wait_ge(xwT_done, blk + 1)
                        v.tensor_tensor(warped[u], taps[u][:, 0, 0], taps[u][:, 0, 2], ALU.add).then_inc(warp_mixed, 1)
                elif stage == "maxima":
                    h, = at
                    for r in range(CHUNKS // HG):
                        dve.wait_ge(max_scored, h * (CHUNKS // HG) + r + 1)
                        largest(banks[r % 6], h, r).then_inc(max_read, 1)
                elif stage == "project":
                    for j in range(QK_CHUNKS + 1):
                        if j:
                            second_part(b, j - 1)
                        if j < QK_CHUNKS:
                            what_it_leaves(b, j)
                        if j:
                            third_part(b, j - 1)
                    dve.wait_ge(v_cleared, 1)
                    dve.wait_ge(weights_in, 16 * N_WEIGHTS)
                    if b == 0:
                        v.tensor_scalar(z_cols[:, 3], z_cols[:, 2], -1.0, None, ALU.mult).then_inc(z_ready, 1)
                        v.scalar_tensor_tensor(out=z_cols[:, 4], in0=z_cols[:, 0], scalar=-2.0, in1=z_cols[:, 2],
                                               op0=ALU.mult, op1=ALU.add).then_inc(z_ready, 1)
                    for j in range(SB // 2):
                        dve.wait_ge(projected, b * PROJ_BATCH + QK_CHUNKS + j + 1)
                        steps.mark(v.tensor_tensor(v_all[:, b, 2 * j:2 * j + 2, :, 0:DH],
                                                   banks[j].rearrange("p (t h d) -> p t h d", t=2, h=H),
                                                   bv_rows[:].rearrange("p (h d) -> p h d", h=H).unsqueeze(1)
                                                   .broadcast_to([P, 2, H, DH]), ALU.add))
                    steps.wait()
                    dve.sem_inc(v_ready, 1)

            dve.wait_ge(xwT_done, NBLK + 2)
            steps.do(v.memset(z, 0.0))
            dve.wait_ge(max_read, CHUNKS + 2)

            lg, hot_1, hot_2, cand, both, pos = (rt[:, i] for i in range(6))

            def negate(n):
                Steps(dve, max_steps, n * 4).do(v.tensor_tensor(neg_max, max_parts[:, 0], max_parts[:, 1], ALU.max))
                v.tensor_scalar(neg_max, neg_max, -1.0, None, ALU.mult).then_inc(neg_ready, 1)

            def side(n, first_use, k, what, i):
                use = first_use + k
                last = isinstance(n, int) and n == 2 * NG
                b = 1 if last else 0
                bank, _ = side_bank(last, k)
                if what == "lap" and i == 0:
                    react(b)
                dve.wait_ge(max_scored, use + 1)
                if what == "chunk":
                    largest(bank, i // (CHUNKS // HG), i % (CHUNKS // HG)).then_inc(max_read, 1)
                    if i == CHUNKS - 1:
                        dve.wait_ge(max_read, use + 3)
                        negate(n + 1)
                elif what == "turn_max":
                    st = Steps(dve, max_steps, n * 4 + 1)
                    nr, parts_ = neg_rows[0:HG * SB], neg_parts[0:HG * SB]
                    v.tensor_copy(nr, bank[0:HG * SB, 0:P]).then_inc(max_read, 1)
                    dve.wait_ge(max_read, use + 3)
                    if not isinstance(n, int) or n:
                        dve.wait_ge(neg_in, n * 48)
                    st.do(v.tensor_copy(parts_[:, 0], nr))
                    st.do(v.tensor_tensor(nr, nr, parts_[:, 0], ALU.subtract))
                    st.do(v.tensor_copy(parts_[:, 1], nr))
                    v.tensor_tensor(parts_[:, 2], nr, parts_[:, 1], ALU.subtract).then_inc(neg_parted, 1)
                elif what == "sum":
                    st = Steps(dve, norm_steps, (n - 1) * 5 + 3 * i)
                    o = bank.rearrange("p (k c) -> p k c", c=32)
                    st.do(v.reciprocal(inverse, o[:, :, DH]))
                    v.tensor_tensor(normed, o[:, :, 0:DH + 1], inverse.unsqueeze(2).broadcast_to([P, 4 * HG, DH + 1]),
                                    ALU.mult).then_inc(max_read, 1)
                    dve.wait_ge(max_read, use + 3)
                    st.do(v.tensor_reduce(head_sum, normed.rearrange("p (k h) d -> p k d h", h=HG), AX_X, ALU.add))
                    zb = z[:, z_batch(n), 4 * i:4 * i + 4]
                    ins = v.tensor_tensor(zb, zb, head_sum, ALU.add)
                    if i:
                        ins.then_inc(o_normed, 1)
                    else:
                        st.do(ins)
                elif what == "turn_z":
                    v.tensor_copy(z_t[0:DH + 1, i * 512:(i + 1) * 512], bank[0:DH + 1, :]).then_inc(max_read, 1)
                    if i:
                        dve.wait_ge(max_read, use + 3)
                        dve.sem_inc(z_turned, 1)
                elif what == "attend":
                    rows = x1[:, z_batch(n) * SB + 2 * i:z_batch(n) * SB + 2 * i + 2]
                    v.tensor_tensor(rows, rows, bank.rearrange("p (i d) -> p i d", i=2), ALU.add).then_inc(max_read, 1)
                    if i == 3:
                        dve.wait_ge(max_read, use + 3)
                        dve.sem_inc(x1_ready, SB)
                elif what == "lap":
                    rows = du[:, b * SB + 2 * i:b * SB + 2 * i + 2]
                    v.scalar_tensor_tensor(out=rows, in0=bank.rearrange("p (i d) -> p i d", i=2),
                                           scalar=z_cols[:, 1, b:b + 1], in1=rows, op0=ALU.mult,
                                           op1=ALU.add).then_inc(max_read, 1)
                elif what == "turn_du":
                    v.tensor_copy(du_t[i % 2].rearrange("p r c q -> p (r c q)"), bank).then_inc(max_read, 1)
                elif what == "logits":
                    v.tensor_tensor(lg[:, b * SB + 2 * i:b * SB + 2 * i + 2],
                                    bank[:, 0:2 * E].rearrange("p (i e) -> p i e", e=E),
                                    br_row[:].unsqueeze(1).broadcast_to([P, 2, E]), ALU.add).then_inc(max_read, 1)
                    if i == SB // 2 - 1:
                        dve.wait_ge(max_read, use + 3)
                        choose(b)
                elif what == "rank":
                    place(b, bank)
                    dve.sem_inc(max_read, 1)
                    dve.sem_inc(slots_ready, 1)
                elif what == "turn_b1":
                    v.tensor_copy(b1_cols.rearrange("p e f -> p (e f)"), bank[:, 0:E * FC]).then_inc(max_read, 1)

            def react(b):
                d, y = du[:, b * SB:(b + 1) * SB], x1[:, b * SB:(b + 1) * SB]
                if b:
                    neighbours(v, 1, side_steps)
                dve.wait_ge(scaled, b + 1)
                steps.do(v.tensor_tensor(d, d, y, ALU.mult))
                dve.wait_ge(side_steps if b else beside, 3)
                steps.do(v.scalar_tensor_tensor(out=d, in0=lap_x, scalar=z_cols[:, 0, b:b + 1], in1=d,
                                                op0=ALU.mult, op1=ALU.add))

            def choose(b):
                own = slice(b * SB, (b + 1) * SB)
                iota = const("experts").unsqueeze(1).broadcast_to([P, SB, E])
                lg_, cand_, idx_ = lg[:, own], cand[:, own], route[:, 6, own]

                def wide(a):
                    return a.unsqueeze(2).broadcast_to([P, SB, E])

                for turn, hot in enumerate((hot_1[:, own], hot_2[:, own])):
                    m = route[:, 2 + turn, own]
                    steps.do(v.reduce_max(m, lg_, AX_X))
                    tt(cand_, lg_, wide(m), ALU.is_equal)
                    stt(cand_, iota, float(-E), cand_, ALU.add, ALU.mult)
                    steps.do(v.tensor_reduce(idx_, cand_, AX_X, ALU.min))
                    ts(idx_, idx_, float(E), ALU.add)
                    tt(hot, iota, wide(idx_), ALU.is_equal)
                    if turn == 0:
                        stt(lg_, hot, -3.0e38, lg_, ALU.mult, ALU.add)
                tt(both[:, own], hot_1[:, own], hot_2[:, own], ALU.add)
                dve.sem_inc(chosen_ready, 1)

            def place(b, bank):
                own = slice(b * SB, (b + 1) * SB)
                rank = bank[:, 0:SB * E].rearrange("p (i e) -> p i e", e=E)
                total = bank[:, SB * E:2 * SB * E].rearrange("p (i e) -> p i e", e=E)
                before, cand_, idx_ = cand[:, own], cand[:, own], route[:, 6, own]
                steps.do(v.tensor_copy(before[:, 0], ex[:, 0]) if b else v.memset(before[:, 0], 0.0))
                for i in range(1, SB):
                    tt(before[:, i], before[:, i - 1], total[:, i - 1], ALU.add)
                tt(ex[:, 0], before[:, SB - 1], total[:, SB - 1], ALU.add)
                steps.do(v.tensor_tensor(pos[:, own], rank, before, ALU.add))
                stt(both[:, own], const("experts").unsqueeze(1).broadcast_to([P, SB, E]), float(REGION), pos[:, own],
                    ALU.mult, ALU.add)
                for k, hot in enumerate((hot_1, hot_2)):
                    tt(cand_, hot[:, own], both[:, own], ALU.mult)
                    steps.do(v.tensor_reduce(idx_, cand_, AX_X, ALU.add))
                    steps.do(v.tensor_copy(x_index[:, k, own], idx_))

            negate(0)
            side(0, CHUNKS, 0, "turn_max", 0)
            for n, g, following, uses, plan, first in attention_groups(dve):
                use = 0
                for unit in plan:
                    for what, i in unit:
                        side(n + 1 if what == "turn_max" else n, uses, use, what, i)
                        use += 1
            for use, (what, i) in enumerate(LAST_PLAN):
                side(2 * NG, LAST_USES, use, what, i)

            gap, e_gap, m1, m2, w_1, w_2, _, den = (route[:, i] for i in range(8))
            tt(gap, m2, m1, ALU.subtract)
            dve.sem_inc(gap_ready, 1)
            ts(ex[:, 0], ex[:, 0], float(P - 1), ALU.add, 1.0 / P, ALU.mult)
            floor(ex[:, 1], ex[:, 0], ex_i[:], ex[:, 2])
            steps.do(v.tensor_copy(ex[:, 3], ex[:, 1]))
            for e in range(1, E):
                tt(ex[:, 3, e:e + 1], ex[:, 3, e - 1:e], ex[:, 3, e:e + 1], ALU.add)
            dve.wait_ge(pairs_cleared, 16 * (NG + 1))
            te = te_f[:]
            ends = ex[:, 3].unsqueeze(1).broadcast_to([P, SLOT_TILES, E])
            tt(te, const("tiles").unsqueeze(2).broadcast_to([P, SLOT_TILES, E]), ends, ALU.is_ge)
            steps.do(v.tensor_reduce(te_s[:], te, AX_X, ALU.add))
            ts(te_s[:], te_s[:], float(E - 1), ALU.min)
            steps.do(v.tensor_copy(tile_expert[:], te_s[:]))
            tt(te, te, ends, ALU.mult)
            steps.do(v.reduce_max(te_row[:], te, AX_X))
            tt(te_row[:], const("tiles"), te_row[:], ALU.subtract)
            ts(te_row[:], te_row[:], float(REGION // P - 1), ALU.min, float(P), ALU.mult)
            stt(te_row[:], te_s[:], float(REGION), te_row[:], ALU.mult, ALU.add)
            steps.do(v.tensor_copy(tile_row[:], te_row[:]))
            dve.sem_inc(tiles_ready, 1)
            dve.wait_ge(gap_exp, 1)
            ts(den, e_gap, 1.0, ALU.add)
            steps.do(v.reciprocal(w_1, den))
            tt(w_2, e_gap, w_1, ALU.mult)
            dve.wait_ge(experts_in, 16 * (2 * E + 1))

            def x_out(t):
                dve.wait_ge(x_turned, t + 2)
                v.tensor_copy(x_t, banks[2][:, 0:D].rearrange("p (c q) -> p c q", c=DC)).then_inc(x_t_ready, 1)

            def h_out(t):
                dve.wait_ge(h_made, t + 1)
                v.tensor_copy(h_tile.rearrange("p (a q) -> p a q", a=2), psum[:, 0:2]).then_inc(h_ready, 1)

            def y_out(t):
                dve.wait_ge(y_made, t + 1)
                if not isinstance(t, int) or t:
                    dve.wait_ge(y_stored, t * 16)
                e = dve.value_load(tile_expert[0:1, bass.ds(t, 1)], min_val=0, max_val=E - 1)
                v.tensor_tensor(y_tile, banks[5][:, 0:D], b2_rows[:, bass.ds(e, 1)].squeeze(1),
                                ALU.add).then_inc(y_ready, 1)

            x_out(0)
            h_out(0)
            x_out(1)
            h_out(1)
            x_out(2)
            y_out(0)
            with dve.Fori(2, SLOT_TILES - 1) as t:
                h_out(t)
                x_out(t + 1)
                y_out(t - 1)
            h_out(SLOT_TILES - 1)
            y_out(SLOT_TILES - 2)
            y_out(SLOT_TILES - 1)
            for i in range(NBLK):
                dve.wait_ge(back_in[i // 2], 16)
                steps.do(v.scalar_tensor_tensor(out=x1[:, i], in0=y_back[:, i, 0], scalar=route[:, 4, i:i + 1],
                                                in1=x1[:, i], op0=ALU.mult, op1=ALU.add))
                v.scalar_tensor_tensor(out=x1[:, i], in0=y_back[:, i, 1], scalar=route[:, 5, i:i + 1],
                                       in1=x1[:, i], op0=ALU.mult, op1=ALU.add).then_inc(summed, 1)



_INS = ['x', 'fside_Bx2_0', 'condB_angle', 'condB_zX', 'condB_zY', 'condB_zR', 'L0_attn_WQ', 'L0_attn_bQ', 'L0_attn_WK',
        'L0_attn_bK', 'L0_attn_WV', 'L0_attn_bV', 'L0_attn_WO', 'L0_attn_bO', 'L0_ffn_W_router', 'L0_ffn_b_router',
        'L0_ffn_W1', 'L0_ffn_b1', 'L0_ffn_W2', 'L0_ffn_b2']


def kernel(**inputs):
    import concourse.bacc as bacc
    from concourse.bass_utils import run_bass_kernel_spmd

    nc = bacc.Bacc("TRN2", target_bir_lowering=False, num_devices=1)
    arrays, args = {}, []
    for name in _INS:
        a = np.ascontiguousarray(inputs[name])
        arrays[name] = a
        args.append(nc.dram_tensor(name, a.shape, mybir.dt.from_np(a.dtype), kind="ExternalInput").ap())
    arrays["constants"] = constants()
    args.append(nc.dram_tensor("constants", arrays["constants"].shape, F32, kind="ExternalInput").ap())
    args.append(nc.dram_tensor("result", (NB, S, D), F32, kind="ExternalOutput").ap())
    build(nc, *args)
    r = run_bass_kernel_spmd(nc, [arrays], core_ids=[0])
    return r.results[0]["result"]
```
